# Optimizing a Trainium2 kernel written in Bass

```python
import numpy as np
import jax
import jax.numpy as jnp

def _softmax(x, axis=-1):
    return jax.nn.softmax(x, axis=axis)

def _gelu(x):
    return jax.nn.gelu(x, approximate=True)

def _silu(x):
    return jax.nn.silu(x)

def _sigmoid(x):
    return jax.nn.sigmoid(x)

def _layernorm(x, axis=-1, eps=1e-05):
    m = jnp.mean(x, axis=axis, keepdims=True)
    v = jnp.var(x, axis=axis, keepdims=True)
    return (x - m) / jnp.sqrt(v + eps)

def _scatter_add(tgt, idx, src, axis=0):
    return tgt.at[idx].add(src)

def _segment_sum(src, seg, n):
    return jax.ops.segment_sum(src, seg, n)
kernel_name = 'mk_flamingo_gated_d4_seqx_r8_c030b7'

def setup_inputs(seed: int=0):
    np.random.seed(seed)
    _w = jnp.asarray

    def _rec_inputs():
        import jax
        import jax.numpy as jnp
        _rk = jax.random.key(seed)
        x = -7.109e-05 + 0.9999 * jax.random.normal(jax.random.fold_in(_rk, 1), (4, 256, 256), jnp.float32)
        _lenS = 256 - jax.random.randint(jax.random.fold_in(_rk, 7), (4,), 0, max(1, 256 // 4) + 1, jnp.int32)
        _lenS2 = 256 - jax.random.randint(jax.random.fold_in(_rk, 8), (4,), 0, max(1, 256 // 4) + 1, jnp.int32)
        _ctx_512P = jax.random.normal(jax.random.fold_in(_rk, 11), (4, 16, 64), jnp.float32)
        _ctx_512c = jax.random.dirichlet(jax.random.fold_in(_rk, 511), 0.3 * jnp.ones((16,), jnp.float32), (4, 256))
        _ctx_512t = jnp.einsum('bsk,bkd->bsd', _ctx_512c, _ctx_512P)
        _ctx_512t = _ctx_512t * jax.lax.rsqrt(jnp.mean(jnp.square(_ctx_512t)) + 1e-12) * 0.953939
        ctx_512 = 2.81802e-05 + 1.00001 * (_ctx_512t + 0.3 * jax.random.normal(jax.random.fold_in(_rk, 611), (4, 256, 64), jnp.float32))
        _g = jax.random.normal(jax.random.fold_in(_rk, 9001), (2, 4), jnp.float32)
        _g = jnp.sign(_g) * jnp.maximum(jnp.abs(_g), 1.0) + (_g == 0) * 1.0
        g_xattn = _g[0]
        g_ffn = _g[1]
        return (x, ctx_512, g_xattn, g_ffn)
    x, ctx_512, g_xattn, g_ffn = _rec_inputs()

    def _L0_xattn_setup():
        import jax, jax.numpy as jnp
        import numpy as np
        EPS = 1e-06
        IMAGE_DIMS = 256
        key = jax.random.key(seed)
        k1, k2, k3 = jax.random.split(key, 3)
        B, I, J, D = (16, 256, 256, 64)
        p = jax.random.normal(k1, (B, I, J), dtype=jnp.float32)
        k_v = jax.random.normal(k2, (B, J, D), dtype=jnp.float32)
        W_k = jax.random.normal(k3, (D, D), dtype=jnp.float32) * (1.0 / np.sqrt(D))
        b_k = jnp.zeros((D,), dtype=jnp.float32)
        ln_gamma = jnp.ones((J,), dtype=jnp.float32)
        ln_beta = jnp.zeros((J,), dtype=jnp.float32)
        return {'p': p, 'k_v': k_v, 'W_k': W_k, 'b_k': b_k, 'ln_gamma': ln_gamma, 'ln_beta': ln_beta}
    _L0_xattn_all = _L0_xattn_setup()
    _L0_xattn_in = {k: v for k, v in _L0_xattn_all.items() if k in ('W_k', 'b_k', 'ln_gamma', 'ln_beta')}
    del _L0_xattn_all

    def _L0_ffn_setup():
        import jax, jax.numpy as jnp
        import numpy as np
        N, S, D = (8, 256, 256)
        O = 256
        E = 8
        K = 2
        key = jax.random.key(seed)
        ks = jax.random.split(key, 5)
        scale_in = 1.0 / np.sqrt(D)
        x = jax.random.normal(ks[0], (N, S, D), dtype=jnp.float32)
        gate_w = jax.random.uniform(ks[1], (D, E), dtype=jnp.float32, minval=-scale_in, maxval=scale_in)
        gate_b = jax.random.uniform(ks[2], (E,), dtype=jnp.float32, minval=-scale_in, maxval=scale_in)
        expert_w = jax.random.uniform(ks[3], (E, D, O), dtype=jnp.float32, minval=-scale_in, maxval=scale_in)
        expert_b = jax.random.uniform(ks[4], (E, O), dtype=jnp.float32, minval=-scale_in, maxval=scale_in)
        return {'x': x, 'gate_w': gate_w, 'gate_b': gate_b, 'expert_w': expert_w, 'expert_b': expert_b}
    _L0_ffn_all = _L0_ffn_setup()
    _L0_ffn_in = {k: v for k, v in _L0_ffn_all.items() if k in ('gate_w', 'gate_b', 'expert_w', 'expert_b')}
    del _L0_ffn_all

    def _L1_xattn_setup():
        import jax, jax.numpy as jnp
        import numpy as np
        B, S, H, NH, L = (2, 256, 256, 16, 64)
        HD = H // NH
        key = jax.random.key(seed)
        k1, k2, k3, k4, k5 = jax.random.split(key, 5)
        scale = 0.02
        return {'q': jax.random.normal(k1, (B, S, H), dtype=jnp.float32), 'latent_kv': jax.random.normal(k2, (B, S, L), dtype=jnp.float32), 'Wq': jax.random.normal(k3, (H, H), dtype=jnp.float32) * scale, 'Wkv_expand': jax.random.normal(k4, (2 * H, L), dtype=jnp.float32) * scale, 'Wout': jax.random.normal(k5, (H, H), dtype=jnp.float32) * scale}
    _L1_xattn_all = _L1_xattn_setup()
    _L1_xattn_in = {k: v for k, v in _L1_xattn_all.items() if k in ('Wq', 'Wkv_expand', 'Wout')}
    del _L1_xattn_all

    def _L1_ffn_setup():
        import jax, jax.numpy as jnp
        import numpy as np
        ACT_BITS = 8
        EPS = 1e-05

        def act_quant(x, bits=ACT_BITS):
            qb = float(2 ** (bits - 1))
            scale = qb / jnp.clip(jnp.max(jnp.abs(x), axis=-1, keepdims=True), EPS)
            xq = jnp.clip(jnp.round(x * scale), -qb, qb - 1) / scale
            return x + jax.lax.stop_gradient(xq - x)

        def weight_quant(w):
            scale = 1.0 / jnp.clip(jnp.mean(jnp.abs(w)), EPS)
            wq = jnp.clip(jnp.round(w * scale), -1.0, 1.0) / scale
            return w + jax.lax.stop_gradient(wq - w)

        def fwht(x):
            shape = x.shape
            n = shape[-1]
            x = x.reshape(-1, n)
            h = 1
            while h < n:
                x = x.reshape(-1, n // (2 * h), 2, h)
                a, b = (x[..., 0, :], x[..., 1, :])
                x = jnp.stack([a + b, a - b], axis=-2).reshape(-1, n)
                h *= 2
            return (x * (1.0 / np.sqrt(n)).astype(np.float32)).reshape(shape)

        def bitlinear(x, w):
            return jnp.einsum('bsh,oh->bso', act_quant(x), weight_quant(w))

        def h_bitlinear(x, w):
            return jnp.einsum('bsh,oh->bso', act_quant(fwht(x)), weight_quant(w))
        key = jax.random.key(seed)
        k1, k2, k3, k4 = jax.random.split(key, 4)
        H, I = (256, 1024)
        B, S = (4, 256)
        std_in = 1.0 / np.sqrt(H)
        std_mid = 1.0 / np.sqrt(I)
        return {'x': jax.random.normal(k1, (B, S, H), dtype=jnp.float32), 'w_gate': jax.random.normal(k2, (I, H), dtype=jnp.float32) * std_in, 'w_up': jax.random.normal(k3, (I, H), dtype=jnp.float32) * std_in, 'w_down': jax.random.normal(k4, (H, I), dtype=jnp.float32) * std_mid}
    _L1_ffn_all = _L1_ffn_setup()
    _L1_ffn_in = {k: v for k, v in _L1_ffn_all.items() if k in ('w_gate', 'w_up', 'w_down')}
    del _L1_ffn_all

    def _L2_xattn_setup():
        import jax, jax.numpy as jnp
        import numpy as np
        B, N, D = (16, 256, 64)
        H = 4
        TOP_K_RATIO = 0.3
        key = jax.random.key(seed)
        k1, k2, k3, k4 = jax.random.split(key, 4)
        h = jax.random.normal(k1, (B, N, D), dtype=jnp.float32)
        adj_raw = jax.random.uniform(k2, (B, N, N), dtype=jnp.float32)
        lim = 1.0 / np.sqrt(D)
        Wq = jax.random.uniform(k3, (D, D), minval=-lim, maxval=lim, dtype=jnp.float32)
        Wk = jax.random.uniform(k4, (D, D), minval=-lim, maxval=lim, dtype=jnp.float32)
        gamma_raw = jnp.float32(-0.85)
        return {'h': h, 'adj_raw': adj_raw, 'Wq': Wq, 'Wk': Wk, 'gamma_raw': gamma_raw}
    _L2_xattn_all = _L2_xattn_setup()
    _L2_xattn_in = {k: v for k, v in _L2_xattn_all.items() if k in ('Wq', 'Wk', 'gamma_raw')}
    del _L2_xattn_all

    def _L2_ffn_setup():
        import jax, jax.numpy as jnp
        import numpy as np
        B, S, D = (2, 256, 256)
        E = 8
        TOPK = 2
        H_SHARED = 1024
        H_ROUTED = 128
        STD = 0.02
        key = jax.random.key(seed)
        ks = jax.random.split(key, 7)
        return {'x': jax.random.normal(ks[0], (B, S, D), jnp.float32), 'w12': jax.random.normal(ks[1], (E, 2 * H_ROUTED, D), jnp.float32) * STD, 'w3': jax.random.normal(ks[2], (E, D, H_ROUTED), jnp.float32) * STD, 'router_w': jax.random.normal(ks[3], (E, D), jnp.float32) * STD, 'expert_bias': jnp.zeros((E,), jnp.float32), 'sw1': jax.random.normal(ks[4], (H_SHARED, D), jnp.float32) * STD, 'sw2': jax.random.normal(ks[5], (H_SHARED, D), jnp.float32) * STD, 'sw3': jax.random.normal(ks[6], (D, H_SHARED), jnp.float32) * STD}
    _L2_ffn_all = _L2_ffn_setup()
    _L2_ffn_in = {k: v for k, v in _L2_ffn_all.items() if k in ('w12', 'w3', 'router_w', 'expert_bias', 'sw1', 'sw2', 'sw3')}
    del _L2_ffn_all

    def _L3_xattn_setup():
        import jax, jax.numpy as jnp
        import numpy as np
        B, S, E = (2, 256, 256)
        QH, KVH = (32, 8)
        D = E // QH
        G = QH // KVH
        DROPOUT = 1.0
        key = jax.random.key(seed)
        k1, k2, k3 = jax.random.split(key, 3)
        q = jax.random.normal(k1, (B, S, E), dtype=jnp.float32)
        k = jax.random.normal(k2, (B, S, E // G), dtype=jnp.float32)
        v = jax.random.normal(k3, (B, S, E // G), dtype=jnp.float32)
        return {'q': q, 'k': k, 'v': v}
    _L3_xattn_all = _L3_xattn_setup()
    _L3_xattn_in = {k: v for k, v in _L3_xattn_all.items() if k in ()}
    del _L3_xattn_all

    def _L3_ffn_setup():
        import jax, jax.numpy as jnp
        import numpy as np
        H = 256
        I_MOE = 176
        I_SH = 704
        E = 8
        TOP_K = 2
        B, S = (1, 256)

        def _silu_and_mul(gu, inter):
            return jax.nn.silu(gu[..., :inter]) * gu[..., inter:]
        key = jax.random.key(seed)
        ks = jax.random.split(key, 7)
        sc = 0.02
        return {'hidden_states': jax.random.normal(ks[0], (B, S, H), jnp.float32), 'W_router': jax.random.normal(ks[1], (E, H), jnp.float32) * sc, 'W_sgate': jax.random.normal(ks[2], (1, H), jnp.float32) * sc, 'Ws_gate_up': jax.random.normal(ks[3], (H, 2 * I_SH), jnp.float32) * sc, 'Ws_down': jax.random.normal(ks[4], (I_SH, H), jnp.float32) * sc, 'We_gate_up': jax.random.normal(ks[5], (E, H, 2 * I_MOE), jnp.float32) * sc, 'We_down': jax.random.normal(ks[6], (E, I_MOE, H), jnp.float32) * sc}
    _L3_ffn_all = _L3_ffn_setup()
    _L3_ffn_in = {k: v for k, v in _L3_ffn_all.items() if k in ('W_router', 'W_sgate', 'Ws_gate_up', 'Ws_down', 'We_gate_up', 'We_down')}
    del _L3_ffn_all
    return {'x': x, 'ctx_512': ctx_512, 'g_xattn': g_xattn, 'g_ffn': g_ffn, 'L0_xattn_W_k': _L0_xattn_in['W_k'], 'L0_xattn_b_k': _L0_xattn_in['b_k'], 'L0_xattn_ln_gamma': _L0_xattn_in['ln_gamma'], 'L0_xattn_ln_beta': _L0_xattn_in['ln_beta'], 'L0_ffn_gate_w': _L0_ffn_in['gate_w'], 'L0_ffn_gate_b': _L0_ffn_in['gate_b'], 'L0_ffn_expert_w': _L0_ffn_in['expert_w'], 'L0_ffn_expert_b': _L0_ffn_in['expert_b'], 'L1_xattn_Wq': _L1_xattn_in['Wq'], 'L1_xattn_Wkv_expand': _L1_xattn_in['Wkv_expand'], 'L1_xattn_Wout': _L1_xattn_in['Wout'], 'L1_ffn_w_gate': _L1_ffn_in['w_gate'], 'L1_ffn_w_up': _L1_ffn_in['w_up'], 'L1_ffn_w_down': _L1_ffn_in['w_down'], 'L2_xattn_Wq': _L2_xattn_in['Wq'], 'L2_xattn_Wk': _L2_xattn_in['Wk'], 'L2_xattn_gamma_raw': _L2_xattn_in['gamma_raw'], 'L2_ffn_w12': _L2_ffn_in['w12'], 'L2_ffn_w3': _L2_ffn_in['w3'], 'L2_ffn_router_w': _L2_ffn_in['router_w'], 'L2_ffn_expert_bias': _L2_ffn_in['expert_bias'], 'L2_ffn_sw1': _L2_ffn_in['sw1'], 'L2_ffn_sw2': _L2_ffn_in['sw2'], 'L2_ffn_sw3': _L2_ffn_in['sw3'], 'L3_ffn_W_router': _L3_ffn_in['W_router'], 'L3_ffn_W_sgate': _L3_ffn_in['W_sgate'], 'L3_ffn_Ws_gate_up': _L3_ffn_in['Ws_gate_up'], 'L3_ffn_Ws_down': _L3_ffn_in['Ws_down'], 'L3_ffn_We_gate_up': _L3_ffn_in['We_gate_up'], 'L3_ffn_We_down': _L3_ffn_in['We_down']}

def reference(x, ctx_512, g_xattn, g_ffn, L0_xattn_W_k, L0_xattn_b_k, L0_xattn_ln_gamma, L0_xattn_ln_beta, L0_ffn_gate_w, L0_ffn_gate_b, L0_ffn_expert_w, L0_ffn_expert_b, L1_xattn_Wq, L1_xattn_Wkv_expand, L1_xattn_Wout, L1_ffn_w_gate, L1_ffn_w_up, L1_ffn_w_down, L2_xattn_Wq, L2_xattn_Wk, L2_xattn_gamma_raw, L2_ffn_w12, L2_ffn_w3, L2_ffn_router_w, L2_ffn_expert_bias, L2_ffn_sw1, L2_ffn_sw2, L2_ffn_sw3, L3_ffn_W_router, L3_ffn_W_sgate, L3_ffn_Ws_gate_up, L3_ffn_Ws_down, L3_ffn_We_gate_up, L3_ffn_We_down):
    import jax
    import jax.numpy as jnp

    def _L0_xattn_ref(p, k_v, W_k, b_k, ln_gamma, ln_beta):
        import jax, jax.numpy as jnp
        import numpy as np
        EPS = 1e-06
        IMAGE_DIMS = 256
        kv = k_v @ W_k.T + b_k
        out = jnp.einsum('bij,bjd->bid', p, kv)
        scale = IMAGE_DIMS ** (-0.5)
        sim = jnp.einsum('bid,bjd->bij', out, kv) * scale
        mu = jnp.mean(sim, axis=-1, keepdims=True)
        var = jnp.var(sim, axis=-1, keepdims=True)
        sim = (sim - mu) * jax.lax.rsqrt(var + EPS) * ln_gamma + ln_beta
        attn = jax.nn.softmax(sim, axis=-1)
        return attn

    def _L0_ffn_ref(x, gate_w, gate_b, expert_w, expert_b):
        import jax, jax.numpy as jnp
        import numpy as np
        N, S, D = (8, 256, 256)
        O = 256
        E = 8
        K = 2
        gate_logits = jnp.einsum('nsd,de->nse', x, gate_w) + gate_b
        _, top_idx = jax.lax.top_k(gate_logits, K)
        all_out = jax.nn.relu(jnp.einsum('nsd,edo->nseo', x, expert_w) + expert_b)
        sel = jnp.take_along_axis(all_out, top_idx[..., None], axis=2)
        return sel.mean(axis=2)

    def _L1_xattn_ref(q, latent_kv, Wq, Wkv_expand, Wout):
        import jax, jax.numpy as jnp
        import numpy as np
        B, S, H, NH, L = (2, 256, 256, 16, 64)
        HD = H // NH
        b, sq, _ = q.shape
        sk = latent_kv.shape[1]
        qp = q @ Wq.T
        kv = latent_kv @ Wkv_expand.T
        k, v = jnp.split(kv, 2, axis=-1)
        qh = qp.reshape(b, sq, NH, HD).transpose(0, 2, 1, 3)
        kh = k.reshape(b, sk, NH, HD).transpose(0, 2, 1, 3)
        vh = v.reshape(b, sk, NH, HD).transpose(0, 2, 1, 3)
        inv_sqrt_d = 1.0 / jnp.sqrt(jnp.float32(HD))
        scores = jnp.einsum('bhqd,bhkd->bhqk', qh, kh) * inv_sqrt_d
        causal = jnp.tril(jnp.ones((sq, sk), dtype=bool))
        scores = jnp.where(causal, scores, jnp.finfo(scores.dtype).min)
        attn = jax.nn.softmax(scores, axis=-1)
        out = jnp.einsum('bhqk,bhkd->bhqd', attn, vh)
        out = out.transpose(0, 2, 1, 3).reshape(b, sq, H)
        return out @ Wout.T

    def _L1_ffn_ref(x, w_gate, w_up, w_down):
        import jax, jax.numpy as jnp
        import numpy as np
        ACT_BITS = 8
        EPS = 1e-05

        def act_quant(x, bits=ACT_BITS):
            qb = float(2 ** (bits - 1))
            scale = qb / jnp.clip(jnp.max(jnp.abs(x), axis=-1, keepdims=True), EPS)
            xq = jnp.clip(jnp.round(x * scale), -qb, qb - 1) / scale
            return x + jax.lax.stop_gradient(xq - x)

        def weight_quant(w):
            scale = 1.0 / jnp.clip(jnp.mean(jnp.abs(w)), EPS)
            wq = jnp.clip(jnp.round(w * scale), -1.0, 1.0) / scale
            return w + jax.lax.stop_gradient(wq - w)

        def fwht(x):
            shape = x.shape
            n = shape[-1]
            x = x.reshape(-1, n)
            h = 1
            while h < n:
                x = x.reshape(-1, n // (2 * h), 2, h)
                a, b = (x[..., 0, :], x[..., 1, :])
                x = jnp.stack([a + b, a - b], axis=-2).reshape(-1, n)
                h *= 2
            return (x * (1.0 / np.sqrt(n)).astype(np.float32)).reshape(shape)

        def bitlinear(x, w):
            return jnp.einsum('bsh,oh->bso', act_quant(x), weight_quant(w))

        def h_bitlinear(x, w):
            return jnp.einsum('bsh,oh->bso', act_quant(fwht(x)), weight_quant(w))
        gate = bitlinear(x, w_gate)
        up = bitlinear(x, w_up)
        intermediate = jax.nn.silu(gate) * up
        return h_bitlinear(intermediate, w_down)

    def _L2_xattn_ref(h, adj_raw, Wq, Wk, gamma_raw):
        import jax, jax.numpy as jnp
        import numpy as np
        B, N, D = (16, 256, 64)
        H = 4
        TOP_K_RATIO = 0.3
        b, n, dm = h.shape
        d = dm // H
        Q = (h @ Wq.T).reshape(b, n, H, d).transpose(0, 2, 1, 3)
        K = (h @ Wk.T).reshape(b, n, H, d).transpose(0, 2, 1, 3)
        sim = jnp.einsum('bhnd,bhmd->bnm', Q, K) / (jnp.sqrt(jnp.float32(d)) * H)
        k = max(1, int(n * TOP_K_RATIO))
        topk_vals = jax.lax.top_k(sim, k)[0]
        threshold = topk_vals[:, :, -1:]
        sparse_mask = (sim >= threshold).astype(sim.dtype)
        A_learned = jax.nn.sigmoid(sim) * sparse_mask
        A_learned = (A_learned + jnp.swapaxes(A_learned, -1, -2)) * 0.5
        gamma = jax.nn.sigmoid(gamma_raw)
        return (1.0 - gamma) * adj_raw + gamma * A_learned

    def _L2_ffn_ref(x, w12, w3, router_w, expert_bias, sw1, sw2, sw3):
        import jax, jax.numpy as jnp
        import numpy as np
        B, S, D = (2, 256, 256)
        E = 8
        TOPK = 2
        H_SHARED = 1024
        H_ROUTED = 128
        STD = 0.02
        b, s, d = x.shape
        g = x @ sw1.T
        u = x @ sw2.T
        shared_out = jax.nn.silu(g) * u @ sw3.T
        scores = jax.nn.sigmoid(x @ router_w.T)
        selection_scores = scores + expert_bias
        _, top_idx = jax.lax.top_k(selection_scores, TOPK)
        top_scores = jnp.take_along_axis(scores, top_idx, axis=-1)
        top_scores = top_scores / (top_scores.sum(-1, keepdims=True) + 1e-09)
        flat_x = x.reshape(-1, d)
        T = flat_x.shape[0]
        flat_idx = top_idx.reshape(T, TOPK)
        flat_sc = top_scores.reshape(T, TOPK)
        combine = jnp.zeros((T, E), x.dtype).at[jnp.arange(T)[:, None], flat_idx].add(flat_sc)
        h12 = jnp.einsum('td,ehd->teh', flat_x, w12)
        h1, h2 = jnp.split(h12, 2, axis=-1)
        h = jax.nn.silu(h1) * h2
        out_e = jnp.einsum('teh,edh->ted', h, w3)
        routed_out = jnp.einsum('ted,te->td', out_e, combine).reshape(b, s, d)
        return shared_out + routed_out

    def _L3_xattn_ref(q, k, v):
        import jax, jax.numpy as jnp
        import numpy as np
        B, S, E = (2, 256, 256)
        QH, KVH = (32, 8)
        D = E // QH
        G = QH // KVH
        DROPOUT = 1.0
        b, s, _ = q.shape
        qh = q.reshape(b, s, KVH, G, D).transpose(0, 2, 3, 1, 4)
        kh = k.reshape(b, s, KVH, D).transpose(0, 2, 1, 3)
        vh = v.reshape(b, s, KVH, D).transpose(0, 2, 1, 3)
        scale = 1.0 / jnp.sqrt(jnp.float32(D))
        scores = jnp.einsum('bkgsd,bktd->bkgst', qh, kh) * scale
        attn = jax.nn.softmax(scores, axis=-1) / DROPOUT
        out = jnp.einsum('bkgst,bktd->bkgsd', attn, vh)
        return out.transpose(0, 3, 1, 2, 4).reshape(b, s, E)

    def _L3_ffn_ref(hidden_states, W_router, W_sgate, Ws_gate_up, Ws_down, We_gate_up, We_down):
        import jax, jax.numpy as jnp
        import numpy as np
        H = 256
        I_MOE = 176
        I_SH = 704
        E = 8
        TOP_K = 2
        B, S = (1, 256)

        def _silu_and_mul(gu, inter):
            return jax.nn.silu(gu[..., :inter]) * gu[..., inter:]
        orig_shape = hidden_states.shape
        x = hidden_states.reshape(-1, H)
        T = x.shape[0]
        logits = x @ W_router.T
        probs = jax.nn.softmax(logits.astype(jnp.float32), axis=-1)
        rw, sel = jax.lax.top_k(probs, TOP_K)
        rw = rw.astype(x.dtype)
        combine = jnp.zeros((T, E), x.dtype).at[jnp.arange(T)[:, None], sel].add(rw)
        sh = _silu_and_mul(x @ Ws_gate_up, I_SH) @ Ws_down
        shared_out = sh * jax.nn.sigmoid(x @ W_sgate.T)
        gu = jnp.einsum('th,ehi->eti', x, We_gate_up)
        h = _silu_and_mul(gu, I_MOE)
        eo = jnp.einsum('eti,eih->eth', h, We_down)
        sparse_out = jnp.einsum('eth,te->th', eo, combine)
        return (shared_out + sparse_out).reshape(orig_shape)
    x = x + jnp.tanh(g_xattn[0]) * _L0_xattn_ref(_layernorm(x, axis=-1), ctx_512, L0_xattn_W_k, L0_xattn_b_k, L0_xattn_ln_gamma, L0_xattn_ln_beta)
    x = x + jnp.tanh(g_ffn[0]) * _L0_ffn_ref(_layernorm(x, axis=-1), L0_ffn_gate_w, L0_ffn_gate_b, L0_ffn_expert_w, L0_ffn_expert_b)
    x = x + jnp.tanh(g_xattn[1]) * _L1_xattn_ref(_layernorm(x, axis=-1), ctx_512, L1_xattn_Wq, L1_xattn_Wkv_expand, L1_xattn_Wout)
    x = x + jnp.tanh(g_ffn[1]) * _L1_ffn_ref(_layernorm(x, axis=-1), L1_ffn_w_gate, L1_ffn_w_up, L1_ffn_w_down)
    x = x + jnp.tanh(g_xattn[2]) * _L2_xattn_ref(ctx_512, _layernorm(x, axis=-1), L2_xattn_Wq, L2_xattn_Wk, L2_xattn_gamma_raw)
    x = x + jnp.tanh(g_ffn[2]) * _L2_ffn_ref(_layernorm(x, axis=-1), L2_ffn_w12, L2_ffn_w3, L2_ffn_router_w, L2_ffn_expert_bias, L2_ffn_sw1, L2_ffn_sw2, L2_ffn_sw3)
    x = x + jnp.tanh(g_xattn[3]) * _L3_xattn_ref(_layernorm(x, axis=-1), ctx_512, ctx_512)
    x = x + jnp.tanh(g_ffn[3]) * _L3_ffn_ref(_layernorm(x, axis=-1), L3_ffn_W_router, L3_ffn_W_sgate, L3_ffn_Ws_gate_up, L3_ffn_Ws_down, L3_ffn_We_gate_up, L3_ffn_We_down)
    return x

_drawn_inputs = setup_inputs


def setup_inputs(seed=0):
    import zlib

    import numpy as np

    out = dict(_drawn_inputs(seed))
    spreads = {'L0_xattn_b_k': (0.0, 2.0),
     'L0_xattn_ln_gamma': (1.0, 0.6),
     'L0_xattn_ln_beta': (0.0, 0.8),
     'L2_ffn_expert_bias': (0.0, 0.8)}
    factors = {'g_ffn': 8.0,
     'L0_xattn_W_k': 8.0,
     'L0_ffn_expert_b': 6.543,
     'L1_xattn_Wq': 8.0,
     'L1_xattn_Wkv_expand': 3.446,
     'L1_xattn_Wout': 3.55,
     'L2_ffn_w12': 6.487,
     'L2_ffn_w3': 5.946,
     'L2_ffn_router_w': 7.878,
     'L3_ffn_W_router': 8.0,
     'L3_ffn_W_sgate': 64.0,
     'L3_ffn_We_gate_up': 8.0,
     'L3_ffn_We_down': 8.0,
     'L3_ffn_Ws_gate_up': 8.0,
     'L3_ffn_Ws_down': 8.0}
    for name, (base, spread) in spreads.items():
        noise = np.random.default_rng([zlib.crc32(name.encode()), seed]).standard_normal(out[name].shape)
        drawn = base * np.exp(spread * noise) if base else spread * noise
        out[name] = jnp.asarray(drawn.astype(out[name].dtype))
    for name, factor in factors.items():
        out[name] = (out[name] * factor).astype(out[name].dtype)
    return out
```

```python
from contextlib import ExitStack

import concourse.bass as bass
from concourse import mybir

F32 = mybir.dt.float32
BF16 = mybir.dt.bfloat16
U32 = mybir.dt.uint32
ALU = mybir.AluOpType
ACT = mybir.ActivationFunctionType
X = mybir.AxisListType.X

P = 128
B, S, D, C = 4, 256, 256, 64
T = S // P
DC = D // P
W = T * D
E = 8
H_FFN = 1024
HC = H_FFN // P
H_R2 = 128
H_S3, H_R3 = 704, 176
SC3, RC3 = -(-H_S3 // P), E * H_R3 // P
NH1, HD1 = 16, 16
NH3, KV3, HD3 = 32, 8, 8
K1 = 6 * HD1
K3 = 6 * HD3
TOPK_ROW = max(1, int(S * 0.3))
TURNS = B // 2
BANK = 512
ROUND = 1.5 * 2.0 ** 23
QB = 128.0
NEG = -1e30
EPS, EPS0 = 1e-5, 1e-6


class Signal:

    def __init__(self, sem, per=1, credit=0):
        self.sem, self.per, self.credit = sem, per, credit

    def count(self, n, k=None):
        return n * self.per + (self.per if k is None else k) + self.credit

    def free(self, n, k=0):
        return n * self.per + k + 1


class Fills:

    def __init__(self, filled, filled_before, slots, drained, drained_before, keys, turns):
        self.filled, self.filled_before, self.slots = filled, filled_before, slots
        self.banks_drained, self.drained_before = drained, drained_before
        self.index = {key: j for j, key in enumerate(keys)}
        self.per = len(keys)
        assert len(self.index) == self.per and (turns == 1 or self.per % len(slots) == 0)

    def slot(self, key):
        return self.slots[self.index[key] % len(self.slots)]

    def drained(self, key):
        return self.banks_drained[self.index[key] % len(self.slots)]

    def empty(self, i, key):
        j, m = self.index[key], len(self.slots)
        return self.drained_before[j % m] + i * (self.per // m) + j // m

    def full(self, i, key):
        return self.filled_before + i * self.per + self.index[key] + 1

    def read(self, i, key):
        return self.empty(i, key) + 1


class Space:

    def __init__(self, tensor, at=0):
        self.tensor, self.at = tensor, at

    def take(self, n, dt=F32, parts=P):
        words = n if dt is F32 else (n + 1) // 2
        view = self.tensor[0:parts, self.at:self.at + words]
        self.at += words
        assert self.at <= self.tensor.shape[1], (self.at, self.tensor.shape)
        return view if dt is F32 else view.bitcast(dt)


def flamingo_gated(nc, x, ctx_512, g_xattn, g_ffn, W_k0, b_k0, ln_gamma, ln_beta, gate_w, gate_b, expert_w, expert_b,
                   Wq1, Wkv1, Wout1, w_gate, w_up, w_down, Wq2, Wk2, gamma_raw, w12, w3, router_w, expert_bias,
                   sw1, sw2, sw3, W_router, W_sgate, Ws_gate_up, Ws_down, We_gate_up, We_down, consts, out):
    with ExitStack() as ctx:
        def sb(name, shape, dt=F32):
            return ctx.enter_context(nc.sbuf_tensor(name, shape, dt))

        def sem(name):
            return ctx.enter_context(nc.semaphore(name))

        psum = ctx.enter_context(nc.psum_tensor("psum", [P, 8 * BANK], F32))

        xs = sb("xs", [P, B, W])
        adj = sb("adj", [P, B, T * S])
        ctx_all = sb("ctx_all", [P, B, T * C])
        con = sb("con", [P, 4 * P + E])
        ident, hadamard, iota8 = con[:, 0:P], con[:, P:2 * P], con[:, 4 * P:4 * P + E]
        conb = sb("conb", [P, 4 * P], BF16)
        identb, mask_q, mask_k, onesb = (conb[:, k * P:(k + 1) * P] for k in range(4))
        bias3 = sb("bias3", [3, E * D], BF16)
        small = Space(sb("small", [P, 1600]))
        eps5, eps6, onecol = small.take(1), small.take(1), small.take(1)
        graw, gt, gt0_half = small.take(8), small.take(8), small.take(1)
        gam, gam_s, keep_x, keep_a = (small.take(1) for _ in range(4))
        lng, lnb = small.take(S), small.take(S)
        bk_row, bk_col = small.take(C), small.take(1, parts=C)
        gate0, gate0_b = small.take(DC * E), small.take(E)
        bias_f, bias_r = small.take(E * D // P), small.take(E * D // P)
        bias_p = [small.take(E * D // P, BF16) for _ in range(3)]
        raw64 = small.take(3 * C, parts=C)
        wT64 = small.take(3 * C, parts=C)
        wk0T, wq2T, wk2T = (wT64[:, k * C:(k + 1) * C] for k in range(3))
        wsum, wmean, wscale = small.take(3), small.take(3), small.take(3)
        ebias = small.take(E)
        rT = small.take(DC * (2 * E + 1))
        r2T, r3T = rT[:, 0:DC * E], rT[:, DC * E:]

        early = sb("early", [P, 12800])
        sp0 = Space(early)
        ex_w = sp0.take(DC * E * D)
        wgT, wuT = sp0.take(DC * H_FFN, BF16), sp0.take(DC * H_FFN, BF16)
        wdT = sp0.take(HC * D, BF16)
        wq1T, wout1T, wkv1T = sp0.take(DC * D), sp0.take(DC * D), sp0.take(2 * D, parts=C)
        sp0 = Space(early, 8704)
        raw_sw = [sp0.take(2048), sp0.take(2048), early[:, 0:2048]]
        raw_w12, raw_w3 = early[:, 8704:12800], early[:, 0:2048]
        raw_r2, raw_r3 = early[0:E, 2048:2048 + D], early[0:E + 1, 2048 + D:2048 + 2 * D]
        sp3 = Space(early)
        we_gu, ws_gu = sp3.take(DC * E * 2 * H_R3), sp3.take(DC * 2 * H_S3)
        we_dn, ws_dn = sp3.take(RC3 * D), sp3.take(SC3 * D)

        late = sb("late", [P, 12288])
        sp2 = Space(late)
        raw_wq1, raw_wkv1, raw_wout1 = sp2.take(W), sp2.take(4 * C), sp2.take(W)
        raw_f1 = [sp2.take(2048) for _ in range(3)]
        tern = [sp2.take(2048, BF16) for _ in range(3)]
        sp2 = Space(late)
        w12T, w3T = sp2.take(DC * E * 2 * H_R2), sp2.take(E * D)
        sw1T, sw2T, sw3T = sp2.take(DC * H_FFN), sp2.take(DC * H_FFN), sp2.take(HC * D)

        shared = sb("shared", [P, 6912])
        arena = [sb(f"arena{s}", [P, 6400]) for s in range(2)]

        def cols(n, k):
            return [small.take(n * k).rearrange("p (n k) -> p n k", n=n) for _ in range(2)]

        st, mv, m8, idf = cols(T, 6), cols(T, 2), cols(T, 8), cols(T, 2)
        idx = [v.bitcast(U32) for v in cols(T, 8)]
        lg, oh, pick, cw = cols(T, E), cols(T, E), cols(T, E), cols(T, E)
        lnv, y0, ya, yb, rstd, c1, c2, c3, c4 = ([small.take(T) for _ in range(2)] for _ in range(9))

        def carve(*parts):
            made = []
            for s in range(2):
                sp = Space(arena[s])
                made.append([sp.take(*p) for p in parts])
            return [list(v) for v in zip(*made)]

        xn, xnT, cx, ctxT = carve((W,), (W,), (T * C,), (S, F32, C))
        base = (W + W + T * C + S,)
        _, kv0, kvT0, oT0, z0, e0 = carve(base, (T * C,), (S, F32, C), (S, F32, C), (T * S,), (T * S,))
        _, acc0, qkT, sim, work, th, aa = carve(base, (W,), (2 * S, F32, C), (T * S,), (T * S,), (T * S,), (T * S,))
        rexp = [shared[:, t * 2048:(t + 1) * 2048] for t in range(T)]
        _, qT1, kT1, vt1, nmax1, sh1, shT1, rec1 = carve(base, (NH1 * S, BF16), (NH1 * S, BF16), (T * NH1 * (HD1 + 1),),
                                                         (T * NH1,), (T * 2 * NH1, BF16), (S, BF16, 2 * NH1), (T * NH1,))
        sph = Space(shared)
        q1a, q2a, qra, k1a, k2a, kra = (sph.take(W, BF16), sph.take(W, BF16), sph.take(W),
                                        sph.take(W, BF16), sph.take(W, BF16), sph.take(W))
        qs1, ks1 = sph.take(T * NH1 * K1, BF16), sph.take(T * NH1 * (K1 + 2), BF16)
        pexp1 = [sph.take(768) for _ in range(2)]
        _, qT3, kT3, vt3, nmax3, sh3, shT3, rec3 = carve(base, (NH3 // 2 * S, BF16), (KV3 * S, BF16),
                                                         (T * KV3 * (HD3 + 1),), (T * NH3,), (T * 2 * NH3, BF16),
                                                         (S, BF16, 2 * NH3), (T * NH3,))
        sph = Space(shared)
        q1b, q2b, qrb, k1b, k2b, krb = (sph.take(W, BF16), sph.take(W, BF16), sph.take(W),
                                        sph.take(T * C, BF16), sph.take(T * C, BF16), sph.take(T * C))
        qs3, ks3 = sph.take(T * NH3 * 64, BF16), sph.take(T * KV3 * P, BF16)
        pexp3 = [sph.take(1024) for _ in range(2)]
        _, xq, xqT, ha, hb, yqT = carve((W,), (W, BF16), (W, BF16), (T * H_FFN,), (T * H_FFN,), (T * H_FFN, BF16))
        sph = Space(shared)
        sg1 = [sph.take(BANK) for _ in range(4)]
        bfly, yqb = sph.take(H_FFN), [sph.take(T * H_FFN, BF16) for _ in range(2)]
        _, hsT2, hrT2 = carve(base, (HC * S,), (T * E * P,))
        sph = Space(shared)
        sg2 = [sph.take(S) for _ in range(4)]
        hr2 = [sph.take(E * H_R2) for _ in range(T)]
        _, hsT3, hrT3 = carve(base, (SC3 * S,), (T * RC3 * P,))
        sph = Space(shared)
        sg3 = [sph.take(S) for _ in range(4)]
        hr3 = [sph.take(E * H_R3) for _ in range(T)]

        ld = {n: sem("ld_" + n) for n in ("x", "ctx", "con", "cols", "ex", "bias", "l1a", "l1f", "sw12", "sw3",
                                          "w12", "w3", "l3")}
        stored = sem("stored")
        const_ready, gates_ready, bias_ready = sem("const_ready"), sem("gates_ready"), sem("bias_ready")
        tanh_ready, egam_ready, wsum_ready, tern_ready = (sem("tanh_ready"), sem("egam_ready"), sem("wsum_ready"),
                                                          sem("tern_ready"))
        bank_drained = [sem(f"bank{k}_drained") for k in range(8)]
        filled = {g: sem("filled_" + g) for g in "ABC"}

        def sig(name, per=1, credit=0):
            return Signal(sem(name), per, credit)

        ln_names = ("l0x", "l0s", "l0f", "l1x", "l1f", "l2x", "l2f", "l3x", "l3f")
        stats_ready = {l: sig(f"{l}_stats_ready") for l in ln_names}
        rstd_ready = {l: sig(f"{l}_rstd_ready") for l in ln_names}
        xn_ready = {l: sig(f"{l}_xn_ready") for l in ln_names}
        cx_ready = {l: sig(f"{l}_cx_ready") for l in ("l0x", "l0f", "l1x", "l3x")}
        l0_z_ready, l0_e_ready = sig("l0_z_ready"), sig("l0_e_ready")
        l0_pick_ready, rexp_free = sig("l0_pick_ready"), sig("rexp_free", T, 2)
        aa_ready = sig("aa_ready")
        split_q1, split_q2, split_k1, split_k2 = ({l: sig(f"{l}_{n}") for l in ("l1x", "l3x")}
                                                  for n in ("split_q1", "split_q2", "split_k1", "split_k2"))
        qstack_ready, kstack_ready = ({l: sig(f"{l}_{n}") for l in ("l1x", "l3x")}
                                      for n in ("qstack_ready", "kstack_ready"))
        third_ready = {l: sig(f"{l}_third_ready", 2) for l in ("l1x", "l3x")}
        shift_ready = {l: sig(f"{l}_shift_ready") for l in ("l1x", "l3x")}
        shift_in = {"l1x": sig("l1x_shift_in", 32), "l3x": sig("l3x_shift_in", 64)}
        v_ready = sig("l3x_v_ready")
        pv_done = {"l1x": sig("l1x_pv_done", NH1 // 2, 2), "l3x": sig("l3x_pv_done", NH3 // 2, 2)}
        xq_ready, yq_ready = sig("xq_ready"), sig("yq_ready", T)
        sg2_ready, sg3_ready = sig("sg2_ready", HC + T * E // 2), sig("sg3_ready", SC3 + T * E)
        lg3_ready, sc3_ready = sig("lg3_ready"), sig("sc3_ready")
        x_done = sig("x_done")
        with_credit = (rexp_free, pv_done["l1x"], pv_done["l3x"])

        counts, drains, loop_start = {g: 0 for g in "ABCV"}, [1] * 8, {}

        def plan(loop, turns, **groups):
            loop_start[loop] = list(drains)
            made = {}
            for g, (firsts, wide, keys) in groups.items():
                made[g] = Fills(filled.get(g), counts[g], [psum[:, k * BANK:(k + wide) * BANK] for k in firsts],
                                [bank_drained[k] for k in firsts], [drains[k] for k in firsts], keys, turns)
                counts[g] += turns * len(keys)
                for j in range(len(keys)):
                    drains[firsts[j % len(firsts)]] += turns
            return made

        def streams(*stages):
            return [(k[0], s, *k[1:]) for stage in stages for s in range(2) for k in stage]

        pl = {}
        pl["prep0"] = plan("prep0", 1, A=([0], 1, [("w64",)]))
        pl["l0x"] = plan("l0x", TURNS, A=([0, 1, 2, 3, 4], 1, streams([("xT",)], [("cT",)], [("kv",)], [("oT",)], [("sim",)])))
        pl["l0f"] = plan("l0f", TURNS,
                         A=([6, 7], 1, streams([("xT",)], [("gate",)])),
                         B=([0, 1, 2, 3], 1, streams([("ex", t, k) for t in range(T) for k in range(E // 2)])),
                         C=([4, 5], 1, streams([("cT",)], [("qk",)], [("sim",)], [("AT",)])))
        pl["prep1"] = plan("prep1", 1, A=([0, 1, 2, 3], 1, [("wq",), ("wkv",), ("wout",)]))
        pl["l1x"] = plan("l1x", TURNS,
                         A=([4, 5], 1, streams([("xT",)], [("cT",)],
                                               [("qsT", k) for k in range(4)] + [("ksT", k) for k in range(4)],
                                               [("max", k) for k in range(12)] + [("shT",)], [("oT",)], [("out",)])),
                         B=([0, 2], 2, streams([("q",), ("kv",)], [("sc", k) for k in range(NH1 // 2)])),
                         V=([6], 2, streams([("pv",)])))
        pl["prep1b"] = plan("prep1b", 1, A=([0, 1, 2, 3], 1, [("tern", w, k) for w in range(3) for k in range(2)]))
        pl["prep2a"] = plan("prep2a", 1, A=([0, 1, 2, 3], 1, [("sw", w, k) for w in range(3) for k in range(4)]))
        pl["l1f"] = plan("l1f", TURNS,
                         A=([6, 7], 1, streams([("xT",)], [("yT", 0), ("yT", 1)], [("dn",)])),
                         B=([0, 1, 2, 3], 1, streams([(w, t, h) for t in range(T) for h in range(2) for w in "gu"])),
                         C=([4, 5], 1, streams([("hT", t, h) for t in range(T) for h in range(2)],
                                               [("had", t, h) for t in range(T) for h in range(2)])))
        pl["prep2b"] = plan("prep2b", 1, A=([0, 1, 2, 3], 1, [("w12", k) for k in range(8)] + [("w3", k) for k in range(4)]
                                           + [("r",)]))
        pl["l2f"] = plan("l2f", TURNS,
                         A=([6, 7], 1, streams([("xT",)], [("gate",)], [("hrT", t, k) for t in range(T) for k in range(2)]
                                               + [("dn",)])),
                         B=([0, 1, 2, 3], 1, streams([("sh", j) for j in range(HC)]
                                                     + [("ro", t, k) for t in range(T) for k in range(E // 2)])))
        pl["l3x"] = plan("l3x", TURNS,
                         A=([4, 5], 1, streams([("qsT", k) for k in range(4)] + [("ksT", k) for k in range(2)],
                                               [("max", k) for k in range(32)] + [("shT",)])),
                         B=([0, 2], 2, streams([("sc", k) for k in range(NH3 // 2)])),
                         V=([6], 2, streams([("pv",)])))
        pl["l3f"] = plan("l3f", TURNS,
                         A=([6, 7], 1, streams([("xT",)], [("gate",)], [("hrT", t, k) for t in range(T) for k in range(3)]
                                               + [("dnS",), ("dnR",)])),
                         B=([0, 1, 2, 3], 1, streams([("sh", j) for j in range(SC3)]
                                                     + [("ro", t, k) for t in range(T) for k in range(E)])))

        def q3d(v, *dims):
            names = "abcd"[:len(dims)]
            return v.rearrange(f"p ({' '.join(names)}) -> p {' '.join(names)}", **dict(zip(names, dims)))

        waits_passed = sem("waits_passed")

        def own_instruction(eng):
            eng.sem_inc(waits_passed, 1)

        block = ctx.enter_context(nc.Block())

        @block.sync
        def _(sp):
            def load(dst, src, name):
                sp.dma_start(dst, src).then_inc(ld[name], 16)

            load(con[:], consts, "con")
            load(ctx_all[:].rearrange("p b (t c) -> p (b t) c", t=T), ctx_512.rearrange("b (t p) c -> p (b t) c", p=P), "ctx")
            load(xs[:].rearrange("p b (t d) -> p (b t) d", t=T), x.rearrange("b (t p) d -> p (b t) d", p=P), "x")
            for k, w in enumerate((W_k0, Wq2, Wk2)):
                load(raw64[:, k * C:(k + 1) * C], w, "cols")
            load(graw[:, 0:4], g_xattn.partition_broadcast(P), "cols")
            load(graw[:, 4:8], g_ffn.partition_broadcast(P), "cols")
            load(gam, gamma_raw.partition_broadcast(P), "cols")
            load(lng, ln_gamma.partition_broadcast(P), "cols")
            load(lnb, ln_beta.partition_broadcast(P), "cols")
            load(bk_row, b_k0.partition_broadcast(P), "cols")
            load(bk_col, b_k0.rearrange("(c a) -> c a", a=1), "cols")
            load(gate0_b, gate_b.partition_broadcast(P), "cols")
            load(ebias, expert_bias.partition_broadcast(P), "cols")
            load(q3d(gate0, DC, E), gate_w.rearrange("(c p) e -> p c e", p=P), "cols")
            load(bias_f, expert_b.rearrange("e (q k) -> (e q) k", k=E * D // P), "cols")
            for c in range(DC):
                load(q3d(ex_w, DC, E, D)[:, c], expert_w.rearrange("e (c p) o -> c p e o", p=P)[c], "ex")
            load(q3d(raw_wq1, T, D), Wq1.rearrange("(o p) i -> p o i", p=P), "l1a")
            load(q3d(raw_wkv1, 4, C), Wkv1.rearrange("(o p) i -> p o i", p=P), "l1a")
            load(q3d(raw_wout1, T, D), Wout1.rearrange("(o p) i -> p o i", p=P), "l1a")
            load(q3d(raw_f1[0], HC, D), w_gate.rearrange("(o p) i -> p o i", p=P), "l1f")
            load(q3d(raw_f1[1], HC, D), w_up.rearrange("(o p) i -> p o i", p=P), "l1f")
            load(q3d(raw_f1[2], T, H_FFN), w_down.rearrange("(o p) i -> p o i", p=P), "l1f")
            load(q3d(raw_sw[0], HC, D), sw1.rearrange("(o p) i -> p o i", p=P), "sw12")
            load(q3d(raw_sw[1], HC, D), sw2.rearrange("(o p) i -> p o i", p=P), "sw12")
            sp.wait_ge(bias_ready, 1)
            for k in range(3):
                load(bias3[k:k + 1, :], bias_p[k], "bias")
            sp.wait_ge(pl["l0f"]["B"].filled, pl["l0f"]["B"].full(TURNS - 1, ("ex", 1, T - 1, E // 2 - 1)))
            load(q3d(raw_sw[2], T, H_FFN), sw3.rearrange("(o p) i -> p o i", p=P), "sw3")

            f = pl["l1x"]["A"]
            with sp.Fori(0, TURNS) as i:
                for s in range(2):
                    sp.wait_ge(f.drained(("shT", s)), f.read(i, ("shT", s)))
                    for r in range(2):
                        sp.dma_start(qT1[s][K1 + r:K1 + r + 1, :], shT1[s][r * NH1:(r + 1) * NH1, :])\
                          .then_inc(shift_in["l1x"].sem, 16)

            sp.wait_ge(pl["prep2a"]["A"].filled, pl["prep2a"]["A"].full(0, ("sw", 1, 3)))
            load(q3d(raw_w12, E * 2, D), w12.rearrange("e (h p) d -> p (e h) d", p=P), "w12")
            sp.wait_ge(pl["prep2a"]["A"].filled, pl["prep2a"]["A"].full(0, ("sw", 2, 3)))
            load(q3d(raw_w3, E * 2, H_R2), w3.rearrange("e (d p) h -> p (e d) h", p=P), "w3")
            load(raw_r2, router_w, "w3")
            load(raw_r3[0:E, :], W_router, "w3")
            load(raw_r3[E:E + 1, :], W_sgate, "w3")
            sp.wait_ge(pl["l1f"]["A"].filled, pl["l1f"]["A"].full(TURNS - 1, ("dn", 1)))
            sp.wait_ge(pl["prep2b"]["A"].filled, pl["prep2b"]["A"].full(0, ("r",)))
            load(q3d(ws_gu, DC, 2 * H_S3), Ws_gate_up.rearrange("(c p) h -> p c h", p=P), "l3")
            load(q3d(ws_dn, SC3, D)[:, 0:SC3 - 1], Ws_down[0:(SC3 - 1) * P, :].rearrange("(j p) o -> p j o", p=P), "l3")
            load(q3d(ws_dn, SC3, D)[0:H_S3 - (SC3 - 1) * P, SC3 - 1], Ws_down[(SC3 - 1) * P:H_S3, :], "l3")
            for c in range(DC):
                load(q3d(we_gu, DC, E, 2 * H_R3)[:, c], We_gate_up.rearrange("e (c p) h -> c p e h", p=P)[c], "l3")
            load(q3d(we_dn, RC3, D), We_down.rearrange("e i o -> (e i) o").rearrange("(j p) o -> p j o", p=P), "l3")

            f = pl["l3x"]["A"]
            with sp.Fori(0, TURNS) as i:
                for s in range(2):
                    sp.wait_ge(f.drained(("shT", s)), f.read(i, ("shT", s)))
                    for r in range(2):
                        for par in range(2):
                            row, src = 64 * par + K3 + r, (2 * r + par) * (NH3 // 2)
                            sp.dma_start(qT3[s][row:row + 1, :], shT3[s][src:src + NH3 // 2, :])\
                              .then_inc(shift_in["l3x"].sem, 16)

            out_v = out.rearrange("b (t p) d -> b p t d", p=P)
            with sp.Fori(0, TURNS) as i:
                for s in range(2):
                    n = 2 * i + s
                    sp.wait_ge(x_done.sem, x_done.count(n))
                    sp.dma_start(out_v[n], q3d(xs[:, n, :], T, D)).then_inc(stored, 16)
            sp.wait_ge(stored, 16 * B)

        @block.gpsimd
        def _(pool):
            for signal in with_credit:
                pool.sem_inc(signal.sem, signal.credit)
            for k in range(8):
                pool.sem_inc(bank_drained[k], 1)
            pool.memset(eps5, EPS)
            pool.memset(eps6, EPS0)
            pool.memset(onecol, 1.0)
            pool.memset(onesb, 1.0)
            pool.wait_ge(ld["con"], 16)
            pool.tensor_copy(identb, ident)
            pool.tensor_copy(conb[:, P:3 * P], con[:, 2 * P:4 * P])
            pool.drain().then_inc(const_ready, 1)
            pool.wait_ge(wsum_ready, 1)
            pool.partition_all_reduce(wmean, wsum, P, bass.bass_isa.ReduceOp.add).then_inc(wsum_ready, 1)
            pool.wait_ge(wsum_ready, 3)
            for w in range(3):
                pool.tensor_scalar(raw_f1[w], raw_f1[w], wscale[:, w:w + 1], ROUND, ALU.mult, ALU.add)
            pool.drain()
            for w in range(3):
                pool.tensor_scalar(raw_f1[w], raw_f1[w], -ROUND, 1.0, ALU.add, ALU.mult)
            pool.drain()
            for w in range(3):
                last = pool.tensor_scalar(tern[w], raw_f1[w], 1.0, -1.0, ALU.min, ALU.max)
            last.then_inc(tern_ready, 1)

            def stack(layer, i, s, nh, hd, qs, ks, pitch_q, pitch_k, dup, q1, q2, k1, k2):
                n, f = 2 * i + s, pl[layer]["A"]
                if s == 1:
                    pool.wait_ge(f.filled, f.full(i, ("qsT", 0, 3)))
                qv = qs.rearrange("p (h k) -> p h k", k=pitch_q)
                kv = ks.rearrange("p (h u k) -> p h u k", u=dup, k=pitch_k)
                pool.wait_ge(split_q1[layer].sem, split_q1[layer].count(n))
                own_instruction(pool)
                if pitch_q > 6 * hd:
                    pool.memset(qv[:, :, 6 * hd:], 0.0)
                for a in range(3):
                    pool.tensor_copy(qv[:, :, a * hd:(a + 1) * hd], q1.rearrange("p (h k) -> p h k", k=hd))
                pool.wait_ge(split_q2[layer].sem, split_q2[layer].count(n))
                own_instruction(pool)
                for a in range(3, 5):
                    pool.tensor_copy(qv[:, :, a * hd:(a + 1) * hd], q2.rearrange("p (h k) -> p h k", k=hd))
                pool.drain().then_inc(qstack_ready[layer].sem, 1)
                if s == 1:
                    pool.wait_ge(f.filled, f.full(i, ("ksT", 0, 3 if layer == "l1x" else 1)))
                pool.wait_ge(split_k1[layer].sem, split_k1[layer].count(n))
                own_instruction(pool)
                for u in range(dup):
                    pool.memset(kv[:, :, u, 6 * hd:6 * hd + 2], 1.0)
                    if pitch_k > 6 * hd + 2:
                        pool.memset(kv[:, :, u, 6 * hd + 2:], 0.0)
                for u in range(dup):
                    for a in (0, 3, 5):
                        pool.tensor_copy(kv[:, :, u, a * hd:(a + 1) * hd], k1.rearrange("p (h k) -> p h k", k=hd))
                pool.wait_ge(split_k2[layer].sem, split_k2[layer].count(n))
                own_instruction(pool)
                for u in range(dup):
                    for a in (1, 4):
                        pool.tensor_copy(kv[:, :, u, a * hd:(a + 1) * hd], k2.rearrange("p (h k) -> p h k", k=hd))
                pool.drain().then_inc(kstack_ready[layer].sem, 1)

            with pool.Fori(0, TURNS) as i:
                for s in range(2):
                    vt = vt1[s].rearrange("p (t h k) -> p (t h) k", t=T, k=HD1 + 1)
                    pool.wait_ge(cx_ready["l1x"].sem, cx_ready["l1x"].count(2 * i + s))
                    own_instruction(pool)
                    pool.memset(vt[:, :, HD1:], 1.0)
                    stack("l1x", i, s, NH1, HD1, qs1, ks1, K1, K1 + 2, 1, q1a, q2a, k1a, k2a)
            with pool.Fori(0, TURNS) as i:
                for s in range(2):
                    n = 2 * i + s
                    vt = vt3[s].rearrange("p (t h k) -> p (t h) k", t=T, k=HD3 + 1)
                    pool.wait_ge(cx_ready["l3x"].sem, cx_ready["l3x"].count(n))
                    own_instruction(pool)
                    pool.memset(vt[:, :, HD3:], 1.0)
                    pool.tensor_copy(vt[:, :, 0:HD3], cx[s].rearrange("p (h k) -> p h k", k=HD3))
                    pool.drain().then_inc(v_ready.sem, 1)
                    stack("l3x", i, s, NH3, HD3, qs3, ks3, 64, 64, 2, q1b, q2b, k1b, k2b)

        @block.tensor
        def _(pe):
            def banks_free(loop):
                for k in range(8):
                    pe.wait_ge(bank_drained[k], loop_start[loop][k])

            def turn(f, i, key, blocks, idn, dt=F32):
                pe.wait_ge(f.drained(key), f.empty(i, key))
                v = f.slot(key)
                v = v if dt is F32 else v.bitcast(dt)
                if blocks[0][2].shape[1] < P:
                    own_instruction(pe)
                for parts, at, src in blocks:
                    k = src.shape[0]
                    last = pe.transpose(v[0:parts, at:at + k], src, idn[0:k, 0:k])
                last.then_inc(f.filled, 1)

            def turn_x(f, i, s, key, src, idn=ident, dt=F32):
                turn(f, i, key, [(P, c * S + t * P, src[:, t * D + c * P:t * D + (c + 1) * P])
                                 for c in range(DC) for t in range(T)], idn, dt)

            def turn_cx(f, i, s):
                turn(f, i, ("cT", s), [(C, t * P, cx[s][:, t * C:(t + 1) * C]) for t in range(T)], ident)

            pe.wait_ge(ld["con"], 16)
            pe.wait_ge(ld["cols"], 16 * 14)
            pe.wait_ge(const_ready, 1)
            turn(pl["prep0"]["A"], 0, ("w64",), [(C, k * C, raw64[:, k * C:(k + 1) * C]) for k in range(3)], ident)

            banks_free("l0x")
            f = pl["l0x"]["A"]
            with pe.Fori(0, TURNS) as i:
                for s in range(2):
                    pe.wait_ge(xn_ready["l0x"].sem, xn_ready["l0x"].count(2 * i + s))
                    turn_x(f, i, s, ("xT", s), xn[s])
                for s in range(2):
                    pe.wait_ge(cx_ready["l0x"].sem, cx_ready["l0x"].count(2 * i + s))
                    turn_cx(f, i, s)
                for s in range(2):
                    pe.wait_ge(f.drained(("cT", s)), f.read(i, ("cT", s)))
                    pe.wait_ge(f.drained(("kv", s)), f.empty(i, ("kv", s)))
                    v = f.slot(("kv", s))
                    for t in range(T):
                        pe.matmul(v[:, t * C:(t + 1) * C], ctxT[s][:, t * P:(t + 1) * P], wk0T, start=True, stop=True)
                    pe.matmul(v[0:C, S:2 * S], wk0T, ctxT[s], start=True, stop=True).then_inc(f.filled, 1)
                for s in range(2):
                    pe.wait_ge(f.drained(("kv", s)), f.read(i, ("kv", s)))
                    pe.wait_ge(f.drained(("xT", s)), f.read(i, ("xT", s)))
                    pe.wait_ge(f.drained(("oT", s)), f.empty(i, ("oT", s)))
                    v = f.slot(("oT", s))
                    for t in range(T):
                        mm = pe.matmul(v[0:C, 0:S], kv0[s][:, t * C:(t + 1) * C], xnT[s][:, t * S:(t + 1) * S],
                                       start=(t == 0), stop=(t == T - 1))
                    mm.then_inc(f.filled, 1)
                for s in range(2):
                    pe.wait_ge(f.drained(("oT", s)), f.read(i, ("oT", s)))
                    pe.wait_ge(f.drained(("sim", s)), f.empty(i, ("sim", s)))
                    v = f.slot(("sim", s))
                    for t in range(T):
                        mm = pe.matmul(v[:, t * S:(t + 1) * S], oT0[s][:, t * P:(t + 1) * P], kvT0[s], start=True, stop=True)
                    mm.then_inc(f.filled, 1)

            banks_free("l0f")
            fa, fb, fc = (pl["l0f"][g] for g in "ABC")
            pe.wait_ge(ld["ex"], 16 * DC)
            pe.wait_ge(ld["bias"], 16 * 3)
            with pe.Fori(0, TURNS) as i:
                for s in range(2):
                    pe.wait_ge(xn_ready["l0f"].sem, xn_ready["l0f"].count(2 * i + s))
                    turn_x(fa, i, s, ("xT", s), xn[s])
                for s in range(2):
                    pe.wait_ge(cx_ready["l0f"].sem, cx_ready["l0f"].count(2 * i + s))
                    turn_cx(fc, i, s)
                for s in range(2):
                    pe.wait_ge(fa.drained(("xT", s)), fa.read(i, ("xT", s)))
                    pe.wait_ge(fa.drained(("gate", s)), fa.empty(i, ("gate", s)))
                    v = fa.slot(("gate", s))
                    for t in range(T):
                        for c in range(DC):
                            mm = pe.matmul(v[:, t * E:(t + 1) * E], xnT[s][:, c * S + t * P:c * S + (t + 1) * P],
                                           gate0[:, c * E:(c + 1) * E], start=(c == 0), stop=(c == DC - 1))
                    mm.then_inc(fa.filled, 1)
                for s in range(2):
                    pe.wait_ge(fc.drained(("cT", s)), fc.read(i, ("cT", s)))
                    pe.wait_ge(fc.drained(("qk", s)), fc.empty(i, ("qk", s)))
                    v = fc.slot(("qk", s))
                    own_instruction(pe)
                    pe.matmul(v[0:C, 0:S], wq2T, ctxT[s], start=True, stop=True)
                    pe.matmul(v[0:C, S:2 * S], wk2T, ctxT[s], start=True, stop=True).then_inc(fc.filled, 1)
                for s in range(2):
                    pe.wait_ge(fc.drained(("qk", s)), fc.read(i, ("qk", s)))
                    pe.wait_ge(fc.drained(("sim", s)), fc.empty(i, ("sim", s)))
                    v = fc.slot(("sim", s))
                    for t in range(T):
                        mm = pe.matmul(v[:, t * S:(t + 1) * S], qkT[s][:, t * P:(t + 1) * P], qkT[s][:, S:2 * S],
                                       start=True, stop=True)
                    mm.then_inc(fc.filled, 1)
                for s in range(2):
                    for t in range(T):
                        for k in range(E // 2):
                            pe.wait_ge(fb.drained(("ex", s, t, k)), fb.empty(i, ("ex", s, t, k)))
                            v = fb.slot(("ex", s, t, k))
                            for c in range(DC):
                                at = c * E * D + k * 2 * D
                                pe.matmul(v, xnT[s][:, c * S + t * P:c * S + (t + 1) * P], ex_w[:, at:at + 2 * D],
                                          start=(c == 0), stop=False)
                            pe.matmul(v, onesb[0:3, :], bias3[:, k * 2 * D:(k + 1) * 2 * D],
                                      start=False, stop=True).then_inc(fb.filled, 1)
                    pe.wait_ge(aa_ready.sem, aa_ready.count(2 * i + s))
                    turn(fc, i, ("AT", s), [(P, t * S + u * P, aa[s][:, u * S + t * P:u * S + (t + 1) * P])
                                            for t in range(T) for u in range(T)], ident)

            banks_free("prep1")
            f = pl["prep1"]["A"]
            pe.wait_ge(ld["l1a"], 16 * 3)
            for key, raw in ((("wq",), raw_wq1), (("wout",), raw_wout1)):
                if key == ("wout",):
                    turn(f, 0, ("wkv",), [(C, o * P, raw_wkv1[:, o * C:(o + 1) * C]) for o in range(4)], ident)
                turn_x(f, 0, 0, key, raw)
            def attention(layer, i, score_max, n_max, nshift, sh, score_exp, values, n_exp):
                fm, fe = pl[layer]["A"], pl[layer]["B"]

                def shift(s):
                    pe.wait_ge(shift_ready[layer].sem, shift_ready[layer].count(2 * i + s))
                    turn(fm, i, ("shT", s), [(nshift, t * P, sh[s][:, t * nshift:(t + 1) * nshift]) for t in range(T)],
                         identb, BF16)

                def exponentials(s, between):
                    pe.wait_ge(shift_in[layer].sem, shift_in[layer].count(2 * i + s))
                    for m in range(n_exp + 1):
                        if m < n_exp:
                            score_exp(i, s, m)
                        for k in between[m]:
                            score_max(i, 1, k)
                        if m == 0:
                            pe.wait_ge(pl[layer]["V"].drained(("pv", s)), pl[layer]["V"].empty(i, ("pv", s)))
                            if layer == "l3x":
                                pe.wait_ge(v_ready.sem, v_ready.count(2 * i + s))
                        else:
                            pe.wait_ge(fe.drained(("sc", s, m - 1)), fe.read(i, ("sc", s, m - 1)))
                            values(s, m - 1).then_inc(pv_done[layer].sem, 1)

                for k in range(n_max):
                    score_max(i, 0, k)
                shift(0)
                head = min(4, n_max)
                for k in range(head):
                    score_max(i, 1, k)
                rest = list(range(head, n_max))
                cut = [len(rest) * m // (n_exp + 1) for m in range(n_exp + 2)]
                exponentials(0, [rest[cut[m]:cut[m + 1]] for m in range(n_exp + 1)])
                shift(1)
                exponentials(1, [[]] * (n_exp + 1))

            banks_free("l1x")
            fa, fb = pl["l1x"]["A"], pl["l1x"]["B"]

            def max1(i, s, k):
                pe.wait_ge(fa.drained(("max", s, k)), fa.empty(i, ("max", s, k)))
                v = fa.slot(("max", s, k))
                t, heads, nk = (0, range(4 * k, 4 * k + 4), P) if k < 4 else (1, range(2 * k - 8, 2 * k - 6), S)
                for j, h in enumerate(heads):
                    pe.matmul(v[:, j * nk:(j + 1) * nk], qT1[s][0:K1, h * S + t * P:h * S + (t + 1) * P],
                              kT1[s][0:K1, h * S:h * S + nk], start=True, stop=True)
                    mm = pe.matmul(v[:, (j + 1) * nk - P:(j + 1) * nk], identb, mask_q, start=False, stop=True,
                                   skip_group_check=True)
                mm.then_inc(fa.filled, 1)

            def exp1(i, s, m):
                pe.wait_ge(fb.drained(("sc", s, m)), fb.empty(i, ("sc", s, m)))
                v = fb.slot(("sc", s, m))
                for j in range(2):
                    h, o = 2 * m + j, j * BANK
                    for t, at, nq in ((0, o, S), (1, o + S, P)):
                        pe.matmul(v[:, at:at + nq], kT1[s][0:K1 + 2, h * S + t * P:h * S + (t + 1) * P],
                                  qT1[s][0:K1 + 2, h * S + t * P:(h + 1) * S], start=True, stop=True)
                        mm = pe.matmul(v[:, at:at + P], identb, mask_k, start=False, stop=True, skip_group_check=True)
                mm.then_inc(fb.filled, 1)

            def values1(s, m):
                pv, p = pl["l1x"]["V"].slot(("pv", s)), pexp1[m % 2]
                for j in range(2):
                    h, o = 2 * m + j, j * (S + P)
                    for t in range(T):
                        for u in range(t + 1):
                            at = o + (t * P if u == 0 else S)
                            vt = vt1[s][:, (u * NH1 + h) * (HD1 + 1):(u * NH1 + h + 1) * (HD1 + 1)]
                            mm = pe.matmul(pv[:, t * BANK + h * (HD1 + 1):t * BANK + (h + 1) * (HD1 + 1)],
                                           p[:, at:at + P], vt, start=(u == 0), stop=(u == t))
                return mm

            with pe.Fori(0, TURNS) as i:
                for s in range(2):
                    pe.wait_ge(xn_ready["l1x"].sem, xn_ready["l1x"].count(2 * i + s))
                    turn_x(fa, i, s, ("xT", s), xn[s])
                for s in range(2):
                    pe.wait_ge(cx_ready["l1x"].sem, cx_ready["l1x"].count(2 * i + s))
                    turn_cx(fa, i, s)
                for s in range(2):
                    pe.wait_ge(fa.drained(("xT", s)), fa.read(i, ("xT", s)))
                    pe.wait_ge(fb.drained(("q", s)), fb.empty(i, ("q", s)))
                    v = fb.slot(("q", s))
                    for t in range(T):
                        for c in range(DC):
                            mm = pe.matmul(v[:, t * D:(t + 1) * D], xnT[s][:, c * S + t * P:c * S + (t + 1) * P],
                                           wq1T[:, c * D:(c + 1) * D], start=(c == 0), stop=(c == DC - 1))
                    mm.then_inc(fb.filled, 1)
                    pe.wait_ge(fa.drained(("cT", s)), fa.read(i, ("cT", s)))
                    pe.wait_ge(fb.drained(("kv", s)), fb.empty(i, ("kv", s)))
                    v = fb.slot(("kv", s))
                    for t in range(T):
                        mm = pe.matmul(v[:, t * BANK:(t + 1) * BANK], ctxT[s][:, t * P:(t + 1) * P], wkv1T,
                                       start=True, stop=True)
                    mm.then_inc(fb.filled, 1)
                for s in range(2):
                    for name, ready, stack, pitch in (("qsT", qstack_ready, qs1, K1), ("ksT", kstack_ready, ks1, K1 + 2)):
                        pe.wait_ge(ready["l1x"].sem, ready["l1x"].count(2 * i + s))
                        pe.wait_ge(third_ready["l1x"].sem, third_ready["l1x"].count(2 * i + s, 1 if name == "qsT" else 2))
                        for k in range(4):
                            turn(fa, i, (name, s, k), [(pitch, j * S + t * P, stack[:, (t * NH1 + 4 * k + j) * pitch:
                                                                                    (t * NH1 + 4 * k + j + 1) * pitch])
                                                       for j in range(4) for t in range(T)], identb, BF16)
                for s in range(2):
                    pe.wait_ge(fa.drained(("ksT", s, 3)), fa.read(i, ("ksT", s, 3)))
                    pe.wait_ge(fa.drained(("ksT", s, 2)), fa.read(i, ("ksT", s, 2)))
                attention("l1x", i, max1, 12, 2 * NH1, sh1, exp1, values1, NH1 // 2)
                for s in range(2):
                    pe.wait_ge(pl["l1x"]["V"].drained(("pv", s)), pl["l1x"]["V"].read(i, ("pv", s)))
                    turn_x(fa, i, s, ("oT", s), xn[s])
                for s in range(2):
                    pe.wait_ge(fa.drained(("oT", s)), fa.read(i, ("oT", s)))
                    pe.wait_ge(fa.drained(("out", s)), fa.empty(i, ("out", s)))
                    v = fa.slot(("out", s))
                    for t in range(T):
                        for c in range(DC):
                            mm = pe.matmul(v[:, t * D:(t + 1) * D], xnT[s][:, c * S + t * P:c * S + (t + 1) * P],
                                           wout1T[:, c * D:(c + 1) * D], start=(c == 0), stop=(c == DC - 1))
                    mm.then_inc(fa.filled, 1)

            banks_free("prep1b")
            f = pl["prep1b"]["A"]
            pe.wait_ge(tern_ready, 1)
            for w in range(2):
                for c in range(DC):
                    turn(f, 0, ("tern", w, c), [(P, o * P, tern[w][:, o * D + c * P:o * D + (c + 1) * P])
                                                for o in range(HC)], identb, BF16)
            for k in range(2):
                turn(f, 0, ("tern", 2, k), [(P, (c % 4) * D + o * P, tern[2][:, o * H_FFN + c * P:o * H_FFN + (c + 1) * P])
                                            for c in range(4 * k, 4 * k + 4) for o in range(T)], identb, BF16)
            f = pl["prep2a"]["A"]
            pe.wait_ge(ld["sw12"], 16 * 2)
            for w in range(2):
                for k in range(4):
                    c, half = k // 2, k % 2
                    turn(f, 0, ("sw", w, k), [(P, j * P, raw_sw[w][:, (4 * half + j) * D + c * P:(4 * half + j) * D + (c + 1) * P])
                                              for j in range(4)], ident)
            pe.wait_ge(ld["sw3"], 16)
            for k in range(4):
                turn(f, 0, ("sw", 2, k), [(P, j * D + o * P, raw_sw[2][:, o * H_FFN + (2 * k + j) * P:o * H_FFN + (2 * k + j + 1) * P])
                                          for j in range(2) for o in range(T)], ident)

            banks_free("l1f")
            fa, fb, fc = (pl["l1f"][g] for g in "ABC")
            with pe.Fori(0, TURNS) as i:
                for s in range(2):
                    pe.wait_ge(xq_ready.sem, xq_ready.count(2 * i + s))
                    turn_x(fa, i, s, ("xT", s), xq[s], identb, BF16)
                for s in range(2):
                    pe.wait_ge(fa.drained(("xT", s)), fa.read(i, ("xT", s)))
                    for t in range(T):
                        for h in range(2):
                            for w, wT in (("g", wgT), ("u", wuT)):
                                pe.wait_ge(fb.drained((w, s, t, h)), fb.empty(i, (w, s, t, h)))
                                v = fb.slot((w, s, t, h))
                                for c in range(DC):
                                    at = c * H_FFN + h * BANK
                                    mm = pe.matmul(v, xqT[s][:, c * S + t * P:c * S + (t + 1) * P], wT[:, at:at + BANK],
                                                   start=(c == 0), stop=(c == DC - 1))
                                mm.then_inc(fb.filled, 1)
                for s in range(2):
                    for t in range(T):
                        for h in range(2):
                            pe.wait_ge(fb.drained(("u", s, t, h)), fb.read(i, ("u", s, t, h)))
                            turn(fc, i, ("hT", s, t, h), [(P, j * P, ha[s][:, t * H_FFN + (4 * h + j) * P:t * H_FFN + (4 * h + j + 1) * P])
                                                          for j in range(4)], ident)
                for s in range(2):
                    for t in range(T):
                        for h in range(2):
                            pe.wait_ge(fc.drained(("hT", s, t, h)), fc.read(i, ("hT", s, t, h)))
                            pe.wait_ge(fc.drained(("had", s, t, h)), fc.empty(i, ("had", s, t, h)))
                            v = fc.slot(("had", s, t, h))
                            for j in range(4):
                                at = t * H_FFN + (4 * h + j) * P
                                mm = pe.matmul(v[:, j * P:(j + 1) * P], hb[s][:, at:at + P], hadamard, start=True, stop=True)
                            mm.then_inc(fc.filled, 1)
                for s in range(2):
                    for t in range(T):
                        pe.wait_ge(yq_ready.sem, yq_ready.count(2 * i + s, t + 1))
                        turn(fa, i, ("yT", s, t), [(P, c * P, yqb[s][:, t * H_FFN + c * P:t * H_FFN + (c + 1) * P])
                                                   for c in range(HC)], identb, BF16)
                for s in range(2):
                    pe.wait_ge(fa.drained(("dn", s)), fa.empty(i, ("dn", s)))
                    v = fa.slot(("dn", s))
                    for t in range(T):
                        pe.wait_ge(fa.drained(("yT", s, t)), fa.read(i, ("yT", s, t)))
                        for c in range(HC):
                            at = t * H_FFN + c * P
                            mm = pe.matmul(v[:, t * D:(t + 1) * D], yqT[s][:, at:at + P], wdT[:, c * D:(c + 1) * D],
                                           start=(c == 0), stop=(c == HC - 1))
                    mm.then_inc(fa.filled, 1)

            banks_free("prep2b")
            f = pl["prep2b"]["A"]
            pe.wait_ge(ld["w12"], 16)
            for k in range(8):
                c, q = k // 4, k % 4
                turn(f, 0, ("w12", k), [(P, j * P, raw_w12[:, (4 * q + j) * D + c * P:(4 * q + j) * D + (c + 1) * P])
                                        for j in range(4)], ident)
            pe.wait_ge(ld["w3"], 16 * 4)
            for k in range(4):
                turn(f, 0, ("w3", k), [(P, j * P, raw_w3[:, (4 * k + j) * P:(4 * k + j + 1) * P]) for j in range(4)], ident)
            turn(f, 0, ("r",), [(P, c * E, raw_r2[:, c * P:(c + 1) * P]) for c in range(DC)]
                 + [(P, DC * E + c * (E + 1), raw_r3[:, c * P:(c + 1) * P]) for c in range(DC)], ident)

            def logits(f, i, s, wT, n):
                pe.wait_ge(f.drained(("xT", s)), f.read(i, ("xT", s)))
                pe.wait_ge(f.drained(("gate", s)), f.empty(i, ("gate", s)))
                v = f.slot(("gate", s))
                for t in range(T):
                    for c in range(DC):
                        mm = pe.matmul(v[:, t * n:(t + 1) * n], xnT[s][:, c * S + t * P:c * S + (t + 1) * P],
                                       wT[:, c * n:(c + 1) * n], start=(c == 0), stop=(c == DC - 1))
                mm.then_inc(f.filled, 1)

            def shared_up(f, i, s, j, rows, gate_at, up_at, w_g, w_u, width):
                pe.wait_ge(f.drained(("sh", s, j)), f.empty(i, ("sh", s, j)))
                v = f.slot(("sh", s, j))
                for half, wT, at in ((0, w_g, gate_at), (1, w_u, up_at)):
                    for c in range(DC):
                        mm = pe.matmul(v[0:rows, half * S:(half + 1) * S], wT[:, c * width + at:c * width + at + rows],
                                       xnT[s][:, c * S:(c + 1) * S], start=(c == 0), stop=(c == DC - 1))
                mm.then_inc(f.filled, 1)

            banks_free("l2f")
            fa, fb = pl["l2f"]["A"], pl["l2f"]["B"]
            with pe.Fori(0, TURNS) as i:
                for s in range(2):
                    pe.wait_ge(xn_ready["l2f"].sem, xn_ready["l2f"].count(2 * i + s))
                    turn_x(fa, i, s, ("xT", s), xn[s])
                for s in range(2):
                    logits(fa, i, s, r2T, E)
                def turn_hidden(s):
                    for t in range(T):
                        pe.wait_ge(fb.drained(("ro", s, t, E // 2 - 1)), fb.read(i, ("ro", s, t, E // 2 - 1)))
                        for k in range(2):
                            turn(fa, i, ("hrT", s, t, k), [(P, j * P, hr2[t][:, (4 * k + j) * P:(4 * k + j + 1) * P])
                                                           for j in range(4)], ident)

                for s in range(2):
                    for j in range(HC):
                        shared_up(fb, i, s, j, P, j * P, j * P, sw1T, sw2T, H_FFN)
                    if s == 1:
                        turn_hidden(0)
                    for t in range(T):
                        for k in range(E // 2):
                            pe.wait_ge(fb.drained(("ro", s, t, k)), fb.empty(i, ("ro", s, t, k)))
                            v = fb.slot(("ro", s, t, k))
                            for c in range(DC):
                                at = c * E * 2 * H_R2 + k * BANK
                                mm = pe.matmul(v, xnT[s][:, c * S + t * P:c * S + (t + 1) * P], w12T[:, at:at + BANK],
                                               start=(c == 0), stop=(c == DC - 1))
                            mm.then_inc(fb.filled, 1)
                for s in range(2):
                    if s == 1:
                        turn_hidden(1)
                    pe.wait_ge(fa.drained(("dn", s)), fa.empty(i, ("dn", s)))
                    v = fa.slot(("dn", s))
                    pe.wait_ge(fb.drained(("sh", s, HC - 1)), fb.read(i, ("sh", s, HC - 1)))
                    pe.wait_ge(fa.drained(("hrT", s, 1, 0)), fa.read(i, ("hrT", s, 1, 0)))
                    pe.wait_ge(fa.drained(("hrT", s, 1, 1)), fa.read(i, ("hrT", s, 1, 1)))
                    for t in range(T):
                        o = v[:, t * D:(t + 1) * D]
                        for j in range(HC):
                            pe.matmul(o, hsT2[s][:, j * S + t * P:j * S + (t + 1) * P], sw3T[:, j * D:(j + 1) * D],
                                      start=(j == 0), stop=False)
                        for e in range(E):
                            mm = pe.matmul(o, hrT2[s][:, (t * E + e) * P:(t * E + e + 1) * P], w3T[:, e * D:(e + 1) * D],
                                           start=False, stop=(e == E - 1))
                    mm.then_inc(fa.filled, 1)

            banks_free("l3x")
            fa, fb = pl["l3x"]["A"], pl["l3x"]["B"]

            def max3(i, s, k):
                pe.wait_ge(fa.drained(("max", s, k)), fa.empty(i, ("max", s, k)))
                v = fa.slot(("max", s, k))
                t, j, r = k // 16, k % 16 // 2, 64 * (k % 2)
                for a in range(2):
                    hh = 2 * j + a
                    mm = pe.matmul(v[:, a * S:(a + 1) * S], qT3[s][r:r + K3, hh * S + t * P:hh * S + (t + 1) * P],
                                   kT3[s][r:r + K3, j * S:(j + 1) * S], start=True, stop=True)
                mm.then_inc(fa.filled, 1)

            def exp3(i, s, m):
                pe.wait_ge(fb.drained(("sc", s, m)), fb.empty(i, ("sc", s, m)))
                v = fb.slot(("sc", s, m))
                j, r = m // 2, 64 * (m % 2)
                for u in range(T):
                    mm = pe.matmul(v[:, u * BANK:(u + 1) * BANK], kT3[s][r:r + K3 + 2, j * S + u * P:j * S + (u + 1) * P],
                                   qT3[s][r:r + K3 + 2, 2 * j * S:(2 * j + 2) * S], start=True, stop=True)
                mm.then_inc(fb.filled, 1)

            def values3(s, m):
                pv, p, w = pl["l3x"]["V"].slot(("pv", s)), pexp3[m % 2], HD3 + 1
                j, par = m // 2, m % 2
                for a in range(2):
                    h = 2 * (2 * j + a) + par
                    for t in range(T):
                        for u in range(T):
                            mm = pe.matmul(pv[:, t * BANK + h * w:t * BANK + (h + 1) * w],
                                           p[:, u * BANK + a * S + t * P:u * BANK + a * S + (t + 1) * P],
                                           vt3[s][:, (u * KV3 + j) * w:(u * KV3 + j + 1) * w],
                                           start=(u == 0), stop=(u == T - 1))
                return mm

            with pe.Fori(0, TURNS) as i:
                for s in range(2):
                    pe.wait_ge(qstack_ready["l3x"].sem, qstack_ready["l3x"].count(2 * i + s))
                    pe.wait_ge(third_ready["l3x"].sem, third_ready["l3x"].count(2 * i + s, 1))
                    for k in range(4):
                        turn(fa, i, ("qsT", s, k), [(P, j * S + t * P, qs3[:, (t * 16 + 4 * k + j) * P:(t * 16 + 4 * k + j + 1) * P])
                                                    for j in range(4) for t in range(T)], identb, BF16)
                    pe.wait_ge(kstack_ready["l3x"].sem, kstack_ready["l3x"].count(2 * i + s))
                    pe.wait_ge(third_ready["l3x"].sem, third_ready["l3x"].count(2 * i + s, 2))
                    for k in range(2):
                        turn(fa, i, ("ksT", s, k), [(P, j * S + t * P, ks3[:, (t * KV3 + 4 * k + j) * P:(t * KV3 + 4 * k + j + 1) * P])
                                                    for j in range(4) for t in range(T)], identb, BF16)
                for s in range(2):
                    pe.wait_ge(fa.drained(("ksT", s, 0)), fa.read(i, ("ksT", s, 0)))
                    pe.wait_ge(fa.drained(("ksT", s, 1)), fa.read(i, ("ksT", s, 1)))
                attention("l3x", i, max3, 32, 2 * NH3, sh3, exp3, values3, NH3 // 2)

            banks_free("l3f")
            fa, fb = pl["l3f"]["A"], pl["l3f"]["B"]
            pe.wait_ge(ld["l3"], 16 * 6)
            with pe.Fori(0, TURNS) as i:
                for s in range(2):
                    pe.wait_ge(xn_ready["l3f"].sem, xn_ready["l3f"].count(2 * i + s))
                    turn_x(fa, i, s, ("xT", s), xn[s])
                for s in range(2):
                    logits(fa, i, s, r3T, E + 1)
                def turn_hidden(s):
                    for t in range(T):
                        pe.wait_ge(fb.drained(("ro", s, t, E - 1)), fb.read(i, ("ro", s, t, E - 1)))
                        for k in range(3):
                            turn(fa, i, ("hrT", s, t, k), [(P, (j - 4 * k) * P, hr3[t][:, j * P:(j + 1) * P])
                                                           for j in range(4 * k, min(4 * k + 4, RC3))], ident)

                for s in range(2):
                    for j in range(SC3):
                        shared_up(fb, i, s, j, min(P, H_S3 - j * P), j * P, H_S3 + j * P, ws_gu, ws_gu, 2 * H_S3)
                    if s == 1:
                        turn_hidden(0)
                    for t in range(T):
                        for e in range(E):
                            pe.wait_ge(fb.drained(("ro", s, t, e)), fb.empty(i, ("ro", s, t, e)))
                            v = fb.slot(("ro", s, t, e))
                            for c in range(DC):
                                at = (c * E + e) * 2 * H_R3
                                mm = pe.matmul(v[:, 0:2 * H_R3], xnT[s][:, c * S + t * P:c * S + (t + 1) * P],
                                               we_gu[:, at:at + 2 * H_R3], start=(c == 0), stop=(c == DC - 1))
                            mm.then_inc(fb.filled, 1)
                for s in range(2):
                    if s == 1:
                        turn_hidden(1)
                    pe.wait_ge(fa.drained(("dnS", s)), fa.empty(i, ("dnS", s)))
                    v = fa.slot(("dnS", s))
                    pe.wait_ge(fb.drained(("sh", s, SC3 - 1)), fb.read(i, ("sh", s, SC3 - 1)))
                    for t in range(T):
                        for j in range(SC3):
                            r = min(P, H_S3 - j * P)
                            mm = pe.matmul(v[:, t * D:(t + 1) * D], hsT3[s][0:r, j * S + t * P:j * S + (t + 1) * P],
                                           ws_dn[0:r, j * D:(j + 1) * D], start=(j == 0), stop=(j == SC3 - 1))
                    mm.then_inc(fa.filled, 1)
                    pe.wait_ge(fa.drained(("dnR", s)), fa.empty(i, ("dnR", s)))
                    v = fa.slot(("dnR", s))
                    pe.wait_ge(fa.drained(("hrT", s, 1, 1)), fa.read(i, ("hrT", s, 1, 1)))
                    pe.wait_ge(fa.drained(("hrT", s, 1, 2)), fa.read(i, ("hrT", s, 1, 2)))
                    for t in range(T):
                        for j in range(RC3):
                            mm = pe.matmul(v[:, t * D:(t + 1) * D], hrT3[s][:, (t * RC3 + j) * P:(t * RC3 + j + 1) * P],
                                           we_dn[:, j * D:(j + 1) * D], start=(j == 0), stop=(j == RC3 - 1))
                    mm.then_inc(fa.filled, 1)

        @block.scalar
        def _(act):
            def first_rstd(layer, n, s, eps, scale=1.0):
                act.wait_ge(stats_ready[layer].sem, stats_ready[layer].count(n))
                act.activation(lnv[s], mv[s][:, :, 1], ACT.Ln, bias=eps, scale=scale)
                act.drain()
                act.activation(y0[s], lnv[s], ACT.Exp, scale=-0.5).then_inc(rstd_ready[layer].sem, 1)

            def move(f, i, key, dst, view, scale=1.0):
                act.wait_ge(f.filled, f.full(i, key))
                v = f.slot(key)
                act.activation(dst, view(v), ACT.Copy, scale=scale).then_inc(f.drained(key), 1)

            def whole(v):
                return v

            act.wait_ge(ld["cols"], 16 * 14)
            act.activation(gt, graw, ACT.Tanh).then_inc(tanh_ready, 1)
            act.activation(gam_s, gam, ACT.Tanh, scale=0.5).then_inc(egam_ready, 1)
            move(pl["prep0"]["A"], 0, ("w64",), wT64, lambda v: v[0:C, 0:3 * C])
            act.wait_ge(const_ready, 1)

            f = pl["l0x"]["A"]
            with act.Fori(0, TURNS) as i:
                for s in range(2):
                    first_rstd("l0x", 2 * i + s, s, eps5)
                for s in range(2):
                    move(f, i, ("xT", s), xnT[s], whole)
                for s in range(2):
                    move(f, i, ("cT", s), ctxT[s], lambda v: v[0:C, 0:S])
                for s in range(2):
                    move(f, i, ("oT", s), oT0[s], lambda v: v[0:C, 0:S])
                for s in range(2):
                    first_rstd("l0s", 2 * i + s, s, eps6, 1.0 / S)
                for s in range(2):
                    act.wait_ge(l0_z_ready.sem, l0_z_ready.count(2 * i + s))
                    for t in range(T):
                        last = act.activation(e0[s][:, t * S:(t + 1) * S], z0[s][:, t * S:(t + 1) * S], ACT.Exp,
                                              bias=c1[s][:, t:t + 1], accum_out=c2[s][:, t:t + 1])
                    last.then_inc(l0_e_ready.sem, 1)

            act.wait_ge(ld["l1f"], 16 * 3)
            for w in range(3):
                last = act.activation(tern[w], raw_f1[w], ACT.Abs, accum_out=wsum[:, w:w + 1])
            last.then_inc(wsum_ready, 1)

            fa, fb, fc = (pl["l0f"][g] for g in "ABC")
            with act.Fori(0, TURNS) as i:
                for s in range(2):
                    first_rstd("l0f", 2 * i + s, s, eps5)
                for s in range(2):
                    move(fa, i, ("xT", s), xnT[s], whole)
                for s in range(2):
                    move(fc, i, ("cT", s), ctxT[s], lambda v: v[0:C, 0:S])
                for s in range(2):
                    move(fc, i, ("qk", s), qkT[s], lambda v: v[0:C, :])
                for s in range(2):
                    act.wait_ge(fc.filled, fc.full(i, ("sim", s)))
                    v = fc.slot(("sim", s))
                    act.activation(sim[s], v, ACT.Copy, scale=1.0 / 16)
                    act.activation(th[s], v, ACT.Tanh, scale=1.0 / 32).then_inc(fc.drained(("sim", s)), 1)
                for s in range(2):
                    n = 2 * i + s
                    act.wait_ge(l0_pick_ready.sem, l0_pick_ready.count(n))
                    for t in range(T):
                        act.wait_ge(rexp_free.sem, rexp_free.free(n, t))
                        for k in range(E // 2):
                            act.wait_ge(fb.filled, fb.full(i, ("ex", s, t, k)))
                            v = fb.slot(("ex", s, t, k))
                            for a in range(2):
                                e = 2 * k + a
                                last = act.activation(rexp[t][:, e * D:(e + 1) * D], v[:, a * D:(a + 1) * D], ACT.Relu,
                                                      scale=pick[s][:, t, e:e + 1])
                            last.then_inc(fb.drained(("ex", s, t, k)), 1)

            f = pl["prep1"]["A"]
            move(f, 0, ("wq",), wq1T, whole)
            move(f, 0, ("wkv",), wkv1T, lambda v: v[0:C, :])
            move(f, 0, ("wout",), wout1T, whole)

            def stacks(layer, i, s, nq, nk, rows_q, rows_k, qT, kT):
                f = pl[layer]["A"]
                for name, m, rows, dst in (("qsT", nq, rows_q, qT), ("ksT", nk, rows_k, kT)):
                    for k in range(m):
                        move(f, i, (name, s, k), dst[s][0:rows, k * 1024:(k + 1) * 1024],
                             lambda v: v[0:rows, :].bitcast(BF16))

            fa, fb = pl["l1x"]["A"], pl["l1x"]["B"]
            with act.Fori(0, TURNS) as i:
                for s in range(2):
                    first_rstd("l1x", 2 * i + s, s, eps5)
                for s in range(2):
                    move(fa, i, ("xT", s), xnT[s], whole)
                for s in range(2):
                    move(fa, i, ("cT", s), ctxT[s], lambda v: v[0:C, 0:S])
                for s in range(2):
                    stacks("l1x", i, s, 4, 4, K1, K1 + 2, qT1, kT1)
                for s in range(2):
                    for m in range(NH1 // 2):
                        act.wait_ge(fb.filled, fb.full(i, ("sc", s, m)))
                        v = fb.slot(("sc", s, m))
                        act.wait_ge(pv_done["l1x"].sem, pv_done["l1x"].free(2 * i + s, m))
                        act.activation(q3d(pexp1[m % 2], 2, S + P), q3d(v, 2, BANK)[:, :, 0:S + P], ACT.Exp,
                                       scale=HD1 ** -0.5).then_inc(fb.drained(("sc", s, m)), 1)
                for s in range(2):
                    move(fa, i, ("oT", s), xnT[s], whole)

            f = pl["prep1b"]["A"]
            for w, dst in ((0, wgT), (1, wuT), (2, wdT)):
                for k in range(2):
                    move(f, 0, ("tern", w, k), dst[:, k * H_FFN:(k + 1) * H_FFN], lambda v: v.bitcast(BF16))
            f = pl["prep2a"]["A"]
            for w, dst in ((0, sw1T), (1, sw2T), (2, sw3T)):
                for k in range(0, 4, 2):
                    move(f, 0, ("sw", w, k), dst[:, k * BANK:(k + 1) * BANK], whole)

            fa, fb, fc = (pl["l1f"][g] for g in "ABC")
            with act.Fori(0, TURNS) as i:
                for s in range(2):
                    first_rstd("l1f", 2 * i + s, s, eps5)
                for s in range(2):
                    move(fa, i, ("xT", s), xqT[s], lambda v: v.bitcast(BF16)[:, 0:W])
                for s in range(2):
                    for t in range(T):
                        for h in range(2):
                            act.wait_ge(fb.filled, fb.full(i, ("g", s, t, h)))
                            v = fb.slot(("g", s, t, h))
                            act.activation(sg1[2 * t + h], v, ACT.Silu, scale=c3[s][:, t:t + 1])\
                               .then_inc(fb.drained(("g", s, t, h)), 1)
                for s in range(2):
                    for t in range(T):
                        for h in range(2):
                            at = t * H_FFN + h * BANK
                            move(fc, i, ("hT", s, t, h), hb[s][:, at:at + BANK], whole)
                for s in range(2):
                    for t in range(T):
                        for h in range(2):
                            at = t * H_FFN + h * BANK
                            move(fc, i, ("had", s, t, h), ha[s][:, at:at + BANK], whole, H_FFN ** -0.5)
                for s in range(2):
                    for t in range(T):
                        move(fa, i, ("yT", s, t), yqT[s][:, t * H_FFN:(t + 1) * H_FFN], lambda v: v.bitcast(BF16))

            f = pl["prep2b"]["A"]
            for k in range(0, 8, 2):
                move(f, 0, ("w12", k), w12T[:, k * BANK:(k + 1) * BANK], whole)
            for k in range(0, 4, 2):
                move(f, 0, ("w3", k), w3T[:, k * BANK:(k + 1) * BANK], whole)
            move(f, 0, ("r",), rT, lambda v: v[:, 0:DC * (2 * E + 1)])

            fa, fb = pl["l2f"]["A"], pl["l2f"]["B"]
            with act.Fori(0, TURNS) as i:
                for s in range(2):
                    first_rstd("l2x", 2 * i + s, s, eps5)
                for s in range(2):
                    first_rstd("l2f", 2 * i + s, s, eps5)
                for s in range(2):
                    move(fa, i, ("xT", s), xnT[s], whole)
                for s in range(2):
                    act.wait_ge(fa.filled, fa.full(i, ("gate", s)))
                    v = fa.slot(("gate", s))
                    act.activation(lg[s], q3d(v[:, 0:T * E], T, E), ACT.Exp, scale=-1.0).then_inc(fa.drained(("gate", s)), 1)
                def move_hidden(s):
                    for t in range(T):
                        for k in range(2):
                            at = (t * E + 4 * k) * P
                            move(fa, i, ("hrT", s, t, k), hrT2[s][:, at:at + 4 * P], whole)

                for s in range(2):
                    for j in range(HC):
                        act.wait_ge(fb.filled, fb.full(i, ("sh", s, j)))
                        v = fb.slot(("sh", s, j))
                        act.activation(sg2[fb.index[("sh", s, j)] % 4], v[:, 0:S], ACT.Silu).then_inc(sg2_ready.sem, 1)
                    if s == 1:
                        move_hidden(0)
                    for t in range(T):
                        for k in range(E // 2):
                            act.wait_ge(fb.filled, fb.full(i, ("ro", s, t, k)))
                            v = fb.slot(("ro", s, t, k))
                            act.activation(q3d(sg2[fb.index[("ro", s, t, k)] % 4], 2, H_R2),
                                           q3d(v, 2, 2 * H_R2)[:, :, 0:H_R2], ACT.Silu).then_inc(sg2_ready.sem, 1)
                move_hidden(1)

            fa, fb = pl["l3x"]["A"], pl["l3x"]["B"]
            with act.Fori(0, TURNS) as i:
                for s in range(2):
                    first_rstd("l3x", 2 * i + s, s, eps5)
                for s in range(2):
                    stacks("l3x", i, s, 4, 2, P, P, qT3, kT3)
                for s in range(2):
                    for m in range(NH3 // 2):
                        act.wait_ge(fb.filled, fb.full(i, ("sc", s, m)))
                        v = fb.slot(("sc", s, m))
                        act.wait_ge(pv_done["l3x"].sem, pv_done["l3x"].free(2 * i + s, m))
                        act.activation(pexp3[m % 2], v, ACT.Exp, scale=HD3 ** -0.5).then_inc(fb.drained(("sc", s, m)), 1)

            fa, fb = pl["l3f"]["A"], pl["l3f"]["B"]
            with act.Fori(0, TURNS) as i:
                for s in range(2):
                    first_rstd("l3f", 2 * i + s, s, eps5)
                for s in range(2):
                    move(fa, i, ("xT", s), xnT[s], whole)
                for s in range(2):
                    act.wait_ge(lg3_ready.sem, lg3_ready.count(2 * i + s))
                    for t in range(T):
                        act.activation(cw[s][:, t, :], lg[s][:, t, :], ACT.Exp, bias=c1[s][:, t:t + 1],
                                       accum_out=c2[s][:, t:t + 1])
                    act.activation(c4[s], c3[s], ACT.Exp, scale=-1.0).then_inc(sc3_ready.sem, 1)
                def move_hidden(s):
                    for t in range(T):
                        for k in range(3):
                            n, at = min(4, RC3 - 4 * k) * P, (t * RC3 + 4 * k) * P
                            move(fa, i, ("hrT", s, t, k), hrT3[s][:, at:at + n], lambda v: v[:, 0:n])

                for s in range(2):
                    for j in range(SC3):
                        act.wait_ge(fb.filled, fb.full(i, ("sh", s, j)))
                        v, r = fb.slot(("sh", s, j)), min(P, H_S3 - j * P)
                        act.activation(sg3[fb.index[("sh", s, j)] % 4][0:r, :], v[0:r, 0:S], ACT.Silu)\
                           .then_inc(sg3_ready.sem, 1)
                    if s == 1:
                        move_hidden(0)
                    for t in range(T):
                        for e in range(E):
                            act.wait_ge(fb.filled, fb.full(i, ("ro", s, t, e)))
                            v = fb.slot(("ro", s, t, e))
                            act.activation(sg3[fb.index[("ro", s, t, e)] % 4][:, 0:H_R3], v[:, 0:H_R3], ACT.Silu)\
                               .then_inc(sg3_ready.sem, 1)
                move_hidden(1)

        @block.vector
        def _(dve):
            def stats(layer, n, s, src):
                for t in range(T):
                    dve.bn_stats(st[s][:, t, :], src(t))
                dve.drain()
                for t in range(T):
                    last = dve.bn_aggr(mv[s][:, t, :], st[s][:, t, :])
                last.then_inc(stats_ready[layer].sem, 1)

            def finish_rstd(layer, n, s, eps, var_scale=1.0, times=1.0):
                dve.wait_ge(rstd_ready[layer].sem, rstd_ready[layer].count(n))
                dve.tensor_tensor(ya[s], y0[s], y0[s], ALU.mult)
                dve.tensor_scalar(yb[s], mv[s][:, :, 1], var_scale, eps, ALU.mult, ALU.add)
                dve.drain()
                dve.tensor_tensor(ya[s], ya[s], yb[s], ALU.mult)
                dve.drain()
                dve.tensor_scalar(ya[s], ya[s], -0.5 * times, 1.5 * times, ALU.mult, ALU.add)
                dve.drain()
                dve.tensor_tensor(rstd[s], ya[s], y0[s], ALU.mult)
                dve.drain()

            def normalised(s, t, dst, src):
                return dve.tensor_scalar(dst[:, t * D:(t + 1) * D], src, mv[s][:, t, 0:1], rstd[s][:, t:t + 1],
                                         ALU.subtract, ALU.mult)

            def x_tile(n):
                return lambda t: xs[:, n, t * D:(t + 1) * D]

            def norm_x(layer, n, s):
                finish_rstd(layer, n, s, EPS)
                for t in range(T):
                    last = normalised(s, t, xn[s], xs[:, n, t * D:(t + 1) * D])
                last.then_inc(xn_ready[layer].sem, 1)

            def take_context(layer, n, s):
                dve.tensor_copy(cx[s], ctx_all[:, n, :]).then_inc(cx_ready[layer].sem, 1)

            def two_largest(s, scores):
                for t in range(T):
                    dve.max(m8[s][:, t, :], scores[:, t, :])
                dve.drain()
                for t in range(T):
                    dve.max_index(idx[s][:, t, :], m8[s][:, t, :], scores[:, t, :])
                dve.drain()
                dve.tensor_copy(idf[s], idx[s][:, :, 0:2])
                dve.drain()
                for t in range(T):
                    dve.tensor_scalar(oh[s][:, t, :], iota8, idf[s][:, t, 0:1], None, ALU.is_equal)
                dve.drain()
                for t in range(T):
                    last = dve.scalar_tensor_tensor(pick[s][:, t, :], iota8, idf[s][:, t, 1:2], oh[s][:, t, :],
                                                    ALU.is_equal, ALU.add)
                return last

            dve.wait_ge(ld["cols"], 16 * 14)
            dve.wait_ge(ld["con"], 16)
            dve.tensor_copy(bias_p[0], bias_f)
            dve.drain()
            dve.tensor_tensor(bias_r, bias_f, bias_p[0], ALU.subtract)
            dve.drain()
            dve.tensor_copy(bias_p[1], bias_r)
            dve.drain()
            dve.tensor_tensor(bias_r, bias_r, bias_p[1], ALU.subtract)
            dve.drain()
            dve.tensor_copy(bias_p[2], bias_r).then_inc(bias_ready, 1)
            dve.wait_ge(tanh_ready, 1)
            dve.wait_ge(egam_ready, 1)
            dve.tensor_scalar(gt0_half, gt[:, 4:5], 0.5, None, ALU.mult)
            dve.tensor_scalar(gam_s, gam_s, 0.5, 0.5, ALU.mult, ALU.add)
            dve.drain()
            dve.tensor_scalar(keep_a, gam_s, gt[:, 2:3], 0.25, ALU.mult, ALU.mult)
            dve.tensor_scalar(keep_x, gam_s, -1.0, 1.0, ALU.mult, ALU.add)
            dve.drain()
            dve.tensor_scalar(keep_x, keep_x, gt[:, 2:3], None, ALU.mult)
            dve.wait_ge(ld["ctx"], 16)
            dve.wait_ge(ld["x"], 16)

            f = pl["l0x"]["A"]
            with dve.Fori(0, TURNS) as i:
                for s in range(2):
                    stats("l0x", 2 * i + s, s, x_tile(2 * i + s))
                    take_context("l0x", 2 * i + s, s)
                for s in range(2):
                    norm_x("l0x", 2 * i + s, s)
                for s in range(2):
                    dve.wait_ge(f.filled, f.full(i, ("kv", s)))
                    v = f.slot(("kv", s))
                    dve.tensor_tensor(q3d(kv0[s], T, C), q3d(v[:, 0:T * C], T, C),
                                      bk_row.unsqueeze(1).broadcast_to([P, T, C]), ALU.add)
                    dve.tensor_scalar(kvT0[s], v[0:C, S:2 * S], bk_col, None, ALU.add).then_inc(f.drained(("kv", s)), 1)
                for s in range(2):
                    dve.wait_ge(f.filled, f.full(i, ("sim", s)))
                    v = f.slot(("sim", s))
                    stats("l0s", 2 * i + s, s, lambda t: v[:, t * S:(t + 1) * S])
                for s in range(2):
                    n, v = 2 * i + s, f.slot(("sim", s))
                    finish_rstd("l0s", n, s, EPS0, 1.0 / S, S ** -0.5)
                    for t in range(T):
                        last = normalised(s, t, z0[s], v[:, t * S:(t + 1) * S])
                    last.then_inc(f.drained(("sim", s)), 1)
                    dve.drain()
                    z = q3d(z0[s], T, S)
                    dve.tensor_tensor(z, z, lng.unsqueeze(1).broadcast_to([P, T, S]), ALU.mult)
                    dve.drain()
                    dve.tensor_tensor(z, z, lnb.unsqueeze(1).broadcast_to([P, T, S]), ALU.add)
                    dve.drain()
                    dve.tensor_reduce(c1[s], z, X, ALU.max, negate=True).then_inc(l0_z_ready.sem, 1)
                for s in range(2):
                    n = 2 * i + s
                    dve.wait_ge(l0_e_ready.sem, l0_e_ready.count(n))
                    dve.reciprocal(c3[s], c2[s])
                    dve.drain()
                    dve.tensor_scalar(c3[s], c3[s], gt[:, 0:1], None, ALU.mult)
                    dve.drain()
                    for t in range(T):
                        xt = xs[:, n, t * D:(t + 1) * D]
                        dve.scalar_tensor_tensor(xt, e0[s][:, t * S:(t + 1) * S], c3[s][:, t:t + 1], xt, ALU.mult, ALU.add)
                dve.drain()

            dve.wait_ge(wsum_ready, 2)
            dve.tensor_scalar(wmean, wmean, 1.0 / (H_FFN * D), EPS, ALU.mult, ALU.max)
            dve.drain()
            dve.reciprocal(wscale, wmean).then_inc(wsum_ready, 1)

            fa, fb, fc = (pl["l0f"][g] for g in "ABC")
            with dve.Fori(0, TURNS) as i:
                for s in range(2):
                    stats("l0f", 2 * i + s, s, x_tile(2 * i + s))
                    take_context("l0f", 2 * i + s, s)
                for s in range(2):
                    norm_x("l0f", 2 * i + s, s)
                for s in range(2):
                    dve.wait_ge(fa.filled, fa.full(i, ("gate", s)))
                    v = fa.slot(("gate", s))
                    dve.tensor_tensor(lg[s], q3d(v[:, 0:T * E], T, E), gate0_b.unsqueeze(1).broadcast_to([P, T, E]),
                                      ALU.add).then_inc(fa.drained(("gate", s)), 1)
                    dve.drain()
                    two_largest(s, lg[s]).then_inc(l0_pick_ready.sem, 1)
                for s in range(2):
                    n = 2 * i + s
                    dve.wait_ge(fc.drained(("sim", s)), fc.read(i, ("sim", s)))
                    dve.tensor_scalar(th[s], th[s], 1.0, None, ALU.add)
                    rounds = -(-TOPK_ROW // 8)
                    for r in range(rounds):
                        cur = sim[s] if r == 0 else work[s]
                        for t in range(T):
                            dve.max(m8[s][:, t, :], cur[:, t * S:(t + 1) * S])
                        dve.drain()
                        if r < rounds - 1:
                            for t in range(T):
                                dve.match_replace(work[s][:, t * S:(t + 1) * S], m8[s][:, t, :],
                                                  cur[:, t * S:(t + 1) * S], -3.0e38)
                            dve.drain()
                    k = (TOPK_ROW - 1) % 8
                    for t in range(T):
                        o = slice(t * S, (t + 1) * S)
                        last = dve.scalar_tensor_tensor(aa[s][:, o], sim[s][:, o], m8[s][:, t, k:k + 1], th[s][:, o],
                                                        ALU.is_ge, ALU.mult)
                    last.then_inc(aa_ready.sem, 1)
                    for t in range(T):
                        dve.wait_ge(fb.drained(("ex", s, t, E // 2 - 1)), fb.read(i, ("ex", s, t, E // 2 - 1)))
                        dve.tensor_reduce(acc0[s][:, t * D:(t + 1) * D], rexp[t].rearrange("p (e d) -> p d e", e=E), X,
                                          ALU.add).then_inc(rexp_free.sem, 1)
                    dve.drain()
                    dve.scalar_tensor_tensor(xs[:, n, :], acc0[s], gt0_half, xs[:, n, :], ALU.mult, ALU.add)
                    dve.wait_ge(fc.filled, fc.full(i, ("AT", s)))
                    v = fc.slot(("AT", s))
                    dve.tensor_tensor(adj[:, n, :], v, aa[s], ALU.add).then_inc(fc.drained(("AT", s)), 1)
                dve.drain()

            def splits(layer, i, s, hd, src_q, src_k, qs, ks, pitch_q, pitch_k, dup, q1, q2, qr, k1, k2, kr, done_q, done_k):
                n, f = 2 * i + s, pl[layer]["A"]
                if s == 1:
                    dve.wait_ge(qstack_ready[layer].sem, qstack_ready[layer].count(2 * i))
                for src, p1 in src_q(q1):
                    last = dve.tensor_copy(p1, src)
                last.then_inc(split_q1[layer].sem, 1)
                dve.drain()
                for (src, p1), (_, r) in zip(src_q(q1), src_q(qr)):
                    dve.tensor_tensor(r, src, p1, ALU.subtract)
                done_q()
                dve.drain()
                dve.tensor_copy(q2, qr).then_inc(split_q2[layer].sem, 1)
                dve.drain()
                if s == 1:
                    dve.wait_ge(f.filled, f.full(i, ("qsT", 0, 3)))
                qv = qs.rearrange("p (h k) -> p h k", k=pitch_q)
                dve.tensor_tensor(qv[:, :, 5 * hd:6 * hd], qr.rearrange("p (h k) -> p h k", k=hd),
                                  q2.rearrange("p (h k) -> p h k", k=hd), ALU.subtract).then_inc(third_ready[layer].sem, 1)
                if s == 1:
                    dve.wait_ge(kstack_ready[layer].sem, kstack_ready[layer].count(2 * i))
                for src, p1 in src_k(k1):
                    last = dve.tensor_copy(p1, src)
                last.then_inc(split_k1[layer].sem, 1)
                dve.drain()
                for (src, p1), (_, r) in zip(src_k(k1), src_k(kr)):
                    dve.tensor_tensor(r, src, p1, ALU.subtract)
                done_k()
                dve.drain()
                dve.tensor_copy(k2, kr).then_inc(split_k2[layer].sem, 1)
                dve.drain()
                if s == 1:
                    dve.wait_ge(f.filled, f.full(i, ("ksT", 0, 3 if layer == "l1x" else 1)))
                kv = ks.rearrange("p (h u k) -> p h u k", u=dup, k=pitch_k)
                for u in range(dup):
                    last = dve.tensor_tensor(kv[:, :, u, 2 * hd:3 * hd], kr.rearrange("p (h k) -> p h k", k=hd),
                                             k2.rearrange("p (h k) -> p h k", k=hd), ALU.subtract)
                last.then_inc(third_ready[layer].sem, 1)

            def maxima(layer, i, s, n_max, reduce, nmax, hi, lo, shT):
                f = pl[layer]["A"]
                for k in range(n_max):
                    dst, heads = reduce(k)
                    dve.wait_ge(f.filled, f.full(i, ("max", s, k)))
                    v = f.slot(("max", s, k))
                    dve.tensor_reduce(dst, heads(v), X, ALU.max, negate=True).then_inc(f.drained(("max", s, k)), 1)
                dve.drain()
                for t in range(T):
                    dve.tensor_copy(hi(t), nmax(t))
                dve.drain()
                for t in range(T):
                    last = dve.tensor_tensor(lo(t), nmax(t), hi(t), ALU.subtract)
                last.then_inc(shift_ready[layer].sem, 1)
                dve.wait_ge(f.filled, f.full(i, ("shT", s)))
                v = f.slot(("shT", s))
                dve.tensor_copy(shT, v[0:shT.shape[0], 0:S // 2].bitcast(BF16)).then_inc(f.drained(("shT", s)), 1)

            def weighted(layer, i, s, nh, hd, rec):
                f, w = pl[layer]["V"], hd + 1
                dve.wait_ge(pv_done[layer].sem, pv_done[layer].count(2 * i + s))
                pv = q3d(f.slot(("pv", s)), T, BANK)[:, :, 0:nh * w].rearrange("p t (h k) -> p t h k", k=w)
                r = q3d(rec[s], T, nh)
                dve.reciprocal(r, pv[:, :, :, hd])
                dve.drain()
                dve.tensor_tensor(xn[s].rearrange("p (t h k) -> p t h k", t=T, h=nh), pv[:, :, :, 0:hd],
                                  r.unsqueeze(3).broadcast_to([P, T, nh, hd]), ALU.mult).then_inc(f.drained(("pv", s)), 1)

            fa, fb = pl["l1x"]["A"], pl["l1x"]["B"]
            with dve.Fori(0, TURNS) as i:
                for s in range(2):
                    stats("l1x", 2 * i + s, s, x_tile(2 * i + s))
                    take_context("l1x", 2 * i + s, s)
                for s in range(2):
                    norm_x("l1x", 2 * i + s, s)
                for s in range(2):
                    vq, vkv = fb.slot(("q", s))[:, 0:W], q3d(fb.slot(("kv", s)), T, BANK)

                    def q_parts(dst):
                        return [(vq, dst)]

                    def k_parts(dst):
                        return [(vkv[:, :, 0:D], q3d(dst, T, D))]

                    def q_done():
                        dve.drain().then_inc(fb.drained(("q", s)), 1)
                        dve.wait_ge(fb.filled, fb.full(i, ("kv", s)))
                        own_instruction(dve)

                    def k_done():
                        dve.tensor_copy(vt1[s].rearrange("p (t h k) -> p t h k", t=T, k=HD1 + 1)[:, :, :, 0:HD1],
                                        vkv[:, :, D:2 * D].rearrange("p t (h k) -> p t h k", k=HD1))\
                           .then_inc(fb.drained(("kv", s)), 1)

                    dve.wait_ge(fb.filled, fb.full(i, ("q", s)))
                    splits("l1x", i, s, HD1, q_parts, k_parts, qs1, ks1, K1, K1 + 2, 1, q1a, q2a, qra, k1a, k2a, kra,
                           q_done, k_done)
                for s in range(2):
                    def reduce1(k):
                        nm = q3d(nmax1[s], T, NH1)
                        if k < 4:
                            return nm[:, 0, 4 * k:4 * k + 4], lambda v: q3d(v, 4, P)
                        return nm[:, 1, 2 * k - 8:2 * k - 6], lambda v: q3d(v, 2, S)

                    sh = sh1[s].rearrange("p (t r h) -> p t r h", t=T, r=2)
                    maxima("l1x", i, s, 12, reduce1, lambda t: q3d(nmax1[s], T, NH1)[:, t], lambda t: sh[:, t, 0],
                           lambda t: sh[:, t, 1], shT1[s])
                for s in range(2):
                    weighted("l1x", i, s, NH1, HD1, rec1)
                for s in range(2):
                    dve.wait_ge(fa.filled, fa.full(i, ("out", s)))
                    n, v = 2 * i + s, fa.slot(("out", s))
                    dve.scalar_tensor_tensor(xs[:, n, :], v, gt[:, 1:2], xs[:, n, :], ALU.mult, ALU.add)\
                       .then_inc(fa.drained(("out", s)), 1)
                dve.drain()

            f = pl["prep2a"]["A"]
            for w, dst in ((0, sw1T), (1, sw2T), (2, sw3T)):
                for k in range(1, 4, 2):
                    dve.wait_ge(f.filled, f.full(0, ("sw", w, k)))
                    v = f.slot(("sw", w, k))
                    dve.tensor_copy(dst[:, k * BANK:(k + 1) * BANK], v).then_inc(f.drained(("sw", w, k)), 1)

            fa, fb, fc = (pl["l1f"][g] for g in "ABC")
            with dve.Fori(0, TURNS) as i:
                for s in range(2):
                    stats("l1f", 2 * i + s, s, x_tile(2 * i + s))
                for s in range(2):
                    n = 2 * i + s
                    norm_x("l1f", n, s)
                    dve.drain()
                    dve.tensor_reduce(c1[s], q3d(xn[s], T, D), X, ALU.max, apply_absolute_value=True)
                    dve.drain()
                    dve.tensor_scalar(c1[s], c1[s], EPS, None, ALU.max)
                    dve.drain()
                    dve.reciprocal(c2[s], c1[s])
                    dve.tensor_scalar(c3[s], c1[s], wmean[:, 0:1], 1.0 / QB, ALU.mult, ALU.mult)
                    dve.tensor_scalar(c4[s], c1[s], wmean[:, 1:2], 1.0 / QB, ALU.mult, ALU.mult)
                    dve.drain()
                    dve.tensor_scalar(c2[s], c2[s], QB, None, ALU.mult)
                    dve.drain()
                    for t in range(T):
                        o = xn[s][:, t * D:(t + 1) * D]
                        dve.tensor_scalar(o, o, c2[s][:, t:t + 1], ROUND, ALU.mult, ALU.add)
                    dve.drain()
                    dve.tensor_scalar(xq[s], xn[s], ROUND, QB - 1, ALU.subtract, ALU.min).then_inc(xq_ready.sem, 1)
                for s in range(2):
                    for t in range(T):
                        for h in range(2):
                            dve.wait_ge(fb.filled, fb.full(i, ("u", s, t, h)))
                            at, v = t * H_FFN + h * BANK, fb.slot(("u", s, t, h))
                            dve.wait_ge(fb.drained(("g", s, t, h)), fb.read(i, ("g", s, t, h)))
                            dve.scalar_tensor_tensor(ha[s][:, at:at + BANK], v, c4[s][:, t:t + 1], sg1[2 * t + h],
                                                     ALU.mult, ALU.mult).then_inc(fb.drained(("u", s, t, h)), 1)
                for s in range(2):
                    for t in range(T):
                        for h in range(2):
                            dve.wait_ge(fc.drained(("had", s, t, h)), fc.read(i, ("had", s, t, h)))
                        y, z = ha[s][:, t * H_FFN:(t + 1) * H_FFN], bfly
                        for src, dst, width in ((y, z, 4 * P), (z, y, 2 * P), (y, z, P)):
                            a = src.rearrange("p (n two w) -> p n two w", two=2, w=width)
                            b = dst.rearrange("p (n two w) -> p n two w", two=2, w=width)
                            dve.tensor_tensor(b[:, :, 0], a[:, :, 0], a[:, :, 1], ALU.add)
                            dve.tensor_tensor(b[:, :, 1], a[:, :, 0], a[:, :, 1], ALU.subtract)
                            dve.drain()
                        k = slice(t, t + 1)
                        dve.tensor_reduce(c1[s][:, k], z, X, ALU.max, apply_absolute_value=True)
                        dve.drain()
                        dve.tensor_scalar(c1[s][:, k], c1[s][:, k], EPS, None, ALU.max)
                        dve.drain()
                        dve.reciprocal(c2[s][:, k], c1[s][:, k])
                        dve.tensor_scalar(c3[s][:, k], c1[s][:, k], wmean[:, 2:3], 1.0 / QB, ALU.mult, ALU.mult)
                        dve.drain()
                        dve.tensor_scalar(c2[s][:, k], c2[s][:, k], QB, None, ALU.mult)
                        dve.tensor_scalar(c3[s][:, k], c3[s][:, k], gt[:, 5:6], None, ALU.mult)
                        dve.drain()
                        dve.tensor_scalar(y, z, c2[s][:, k], ROUND, ALU.mult, ALU.add)
                        dve.drain()
                        dve.tensor_scalar(yqb[s][:, t * H_FFN:(t + 1) * H_FFN], y, ROUND, QB - 1, ALU.subtract, ALU.min)\
                           .then_inc(yq_ready.sem, 1)
                for s in range(2):
                    dve.wait_ge(fa.filled, fa.full(i, ("dn", s)))
                    n, v = 2 * i + s, fa.slot(("dn", s))
                    for t in range(T):
                        xt = xs[:, n, t * D:(t + 1) * D]
                        last = dve.scalar_tensor_tensor(xt, v[:, t * D:(t + 1) * D], c3[s][:, t:t + 1], xt, ALU.mult, ALU.add)
                    last.then_inc(fa.drained(("dn", s)), 1)
                dve.drain()

            f = pl["prep2b"]["A"]
            for name, m, dst in (("w12", 8, w12T), ("w3", 4, w3T)):
                for k in range(1, m, 2):
                    dve.wait_ge(f.filled, f.full(0, (name, k)))
                    v = f.slot((name, k))
                    dve.tensor_copy(dst[:, k * BANK:(k + 1) * BANK], v).then_inc(f.drained((name, k)), 1)

            fa, fb = pl["l2f"]["A"], pl["l2f"]["B"]
            with dve.Fori(0, TURNS) as i:
                for s in range(2):
                    stats("l2x", 2 * i + s, s, x_tile(2 * i + s))
                for s in range(2):
                    n = 2 * i + s
                    norm_x("l2x", n, s)
                    dve.drain()
                    dve.scalar_tensor_tensor(xs[:, n, :], xn[s], keep_x, xs[:, n, :], ALU.mult, ALU.add)
                    dve.drain()
                    dve.scalar_tensor_tensor(xs[:, n, :], adj[:, n, :], keep_a, xs[:, n, :], ALU.mult, ALU.add)
                    dve.drain()
                    stats("l2f", n, s, x_tile(n))
                for s in range(2):
                    norm_x("l2f", 2 * i + s, s)
                for s in range(2):
                    dve.wait_ge(fa.drained(("gate", s)), fa.read(i, ("gate", s)))
                    dve.tensor_scalar(cw[s], lg[s], 1.0, None, ALU.add)
                    dve.drain()
                    dve.reciprocal(cw[s], cw[s])
                    dve.drain()
                    dve.tensor_tensor(lg[s], cw[s], ebias.unsqueeze(1).broadcast_to([P, T, E]), ALU.add)
                    dve.drain()
                    two_largest(s, lg[s])
                    dve.drain()
                    dve.tensor_tensor(cw[s], cw[s], pick[s], ALU.mult)
                    dve.drain()
                    dve.tensor_reduce(c1[s], cw[s], X, ALU.add)
                    dve.drain()
                    dve.tensor_scalar(c1[s], c1[s], 1e-9, None, ALU.add)
                    dve.drain()
                    dve.reciprocal(c2[s], c1[s])
                    dve.drain()
                    for t in range(T):
                        dve.tensor_scalar(cw[s][:, t, :], cw[s][:, t, :], c2[s][:, t:t + 1], None, ALU.mult)
                    dve.drain()
                for s in range(2):
                    n = 2 * i + s
                    for j in range(HC):
                        dve.wait_ge(fb.filled, fb.full(i, ("sh", s, j)))
                        v = fb.slot(("sh", s, j))
                        dve.wait_ge(sg2_ready.sem, sg2_ready.count(n, j + 1))
                        dve.tensor_tensor(hsT2[s][:, j * S:(j + 1) * S], v[:, S:2 * S], sg2[fb.index[("sh", s, j)] % 4],
                                          ALU.mult).then_inc(fb.drained(("sh", s, j)), 1)
                    for t in range(T):
                        if s == 1:
                            dve.wait_ge(fa.filled, fa.full(i, ("hrT", 0, t, 1)))
                        for k in range(E // 2):
                            dve.wait_ge(fb.filled, fb.full(i, ("ro", s, t, k)))
                            v, sg = fb.slot(("ro", s, t, k)), sg2[fb.index[("ro", s, t, k)] % 4]
                            dve.wait_ge(sg2_ready.sem, sg2_ready.count(n, HC + t * E // 2 + k + 1))
                            for a in range(2):
                                e = 2 * k + a
                                last = dve.scalar_tensor_tensor(hr2[t][:, e * H_R2:(e + 1) * H_R2],
                                                                v[:, (2 * a + 1) * H_R2:(2 * a + 2) * H_R2], cw[s][:, t, e:e + 1],
                                                                sg[:, a * H_R2:(a + 1) * H_R2], ALU.mult, ALU.mult)
                            last.then_inc(fb.drained(("ro", s, t, k)), 1)
                for s in range(2):
                    dve.wait_ge(fa.filled, fa.full(i, ("dn", s)))
                    n, v = 2 * i + s, fa.slot(("dn", s))
                    dve.scalar_tensor_tensor(xs[:, n, :], v, gt[:, 6:7], xs[:, n, :], ALU.mult, ALU.add)\
                       .then_inc(fa.drained(("dn", s)), 1)
                dve.drain()

            with dve.Fori(0, TURNS) as i:
                for s in range(2):
                    stats("l3x", 2 * i + s, s, x_tile(2 * i + s))
                    take_context("l3x", 2 * i + s, s)
                for s in range(2):
                    norm_x("l3x", 2 * i + s, s)
                    dve.drain()
                for s in range(2):
                    splits("l3x", i, s, HD3, lambda dst: [(xn[s], dst)], lambda dst: [(cx[s], dst)], qs3, ks3, 64, 64, 2,
                           q1b, q2b, qrb, k1b, k2b, krb, lambda: None, lambda: None)
                for s in range(2):
                    nm = q3d(nmax3[s], T, NH3)
                    sh = sh3[s].rearrange("p (t r u h) -> p t r u h", t=T, r=2, u=2)

                    def reduce3(k):
                        j, par = k % 16 // 2, k % 2
                        return nm[:, k // 16].rearrange("p (j a u) -> p j a u", a=2, u=2)[:, j, :, par], lambda v: q3d(v, 2, S)

                    maxima("l3x", i, s, 32, reduce3, lambda t: nm[:, t].rearrange("p (h u) -> p u h", u=2), lambda t: sh[:, t, 0],
                           lambda t: sh[:, t, 1], shT3[s])
                for s in range(2):
                    n = 2 * i + s
                    weighted("l3x", i, s, NH3, HD3, rec3)
                    dve.drain()
                    dve.scalar_tensor_tensor(xs[:, n, :], xn[s], gt[:, 3:4], xs[:, n, :], ALU.mult, ALU.add)
                dve.drain()

            fa, fb = pl["l3f"]["A"], pl["l3f"]["B"]
            with dve.Fori(0, TURNS) as i:
                for s in range(2):
                    stats("l3f", 2 * i + s, s, x_tile(2 * i + s))
                for s in range(2):
                    norm_x("l3f", 2 * i + s, s)
                for s in range(2):
                    dve.wait_ge(fa.filled, fa.full(i, ("gate", s)))
                    v = fa.slot(("gate", s))
                    v = q3d(v[:, 0:T * (E + 1)], T, E + 1)
                    dve.tensor_copy(c3[s], v[:, :, E])
                    dve.tensor_copy(lg[s], v[:, :, 0:E]).then_inc(fa.drained(("gate", s)), 1)
                    dve.drain()
                    dve.tensor_reduce(c1[s], lg[s], X, ALU.max, negate=True).then_inc(lg3_ready.sem, 1)
                for s in range(2):
                    dve.wait_ge(sc3_ready.sem, sc3_ready.count(2 * i + s))
                    dve.reciprocal(c1[s], c2[s])
                    dve.tensor_scalar(c4[s], c4[s], 1.0, None, ALU.add)
                    dve.drain()
                    dve.reciprocal(c3[s], c4[s])
                    for t in range(T):
                        dve.tensor_scalar(lg[s][:, t, :], cw[s][:, t, :], c1[s][:, t:t + 1], None, ALU.mult)
                    dve.drain()
                    dve.tensor_scalar(c3[s], c3[s], gt[:, 7:8], None, ALU.mult)
                    two_largest(s, lg[s])
                    dve.drain()
                    dve.tensor_tensor(cw[s], lg[s], pick[s], ALU.mult)
                    dve.drain()
                for s in range(2):
                    n = 2 * i + s
                    for j in range(SC3):
                        dve.wait_ge(fb.filled, fb.full(i, ("sh", s, j)))
                        r, v = min(P, H_S3 - j * P), fb.slot(("sh", s, j))
                        dve.wait_ge(sg3_ready.sem, sg3_ready.count(n, j + 1))
                        dve.tensor_tensor(hsT3[s][0:r, j * S:(j + 1) * S], v[0:r, S:2 * S],
                                          sg3[fb.index[("sh", s, j)] % 4][0:r, :], ALU.mult).then_inc(fb.drained(("sh", s, j)), 1)
                    for t in range(T):
                        if s == 1:
                            dve.wait_ge(fa.filled, fa.full(i, ("hrT", 0, t, 2)))
                        for e in range(E):
                            dve.wait_ge(fb.filled, fb.full(i, ("ro", s, t, e)))
                            v, sg = fb.slot(("ro", s, t, e)), sg3[fb.index[("ro", s, t, e)] % 4]
                            dve.wait_ge(sg3_ready.sem, sg3_ready.count(n, SC3 + t * E + e + 1))
                            dve.scalar_tensor_tensor(hr3[t][:, e * H_R3:(e + 1) * H_R3], v[:, H_R3:2 * H_R3],
                                                     cw[s][:, t, e:e + 1], sg[:, 0:H_R3], ALU.mult, ALU.mult)\
                               .then_inc(fb.drained(("ro", s, t, e)), 1)
                for s in range(2):
                    dve.wait_ge(fa.filled, fa.full(i, ("dnS", s)))
                    n, v = 2 * i + s, fa.slot(("dnS", s))
                    for t in range(T):
                        xt = xs[:, n, t * D:(t + 1) * D]
                        last = dve.scalar_tensor_tensor(xt, v[:, t * D:(t + 1) * D], c3[s][:, t:t + 1], xt, ALU.mult, ALU.add)
                    last.then_inc(fa.drained(("dnS", s)), 1)
                    dve.drain()
                    dve.wait_ge(fa.filled, fa.full(i, ("dnR", s)))
                    v = fa.slot(("dnR", s))
                    dve.scalar_tensor_tensor(xs[:, n, :], v, gt[:, 7:8], xs[:, n, :], ALU.mult, ALU.add)\
                       .then_inc(fa.drained(("dnR", s)), 1)
                    dve.drain().then_inc(x_done.sem, 1)


_INS = ['x', 'ctx_512', 'g_xattn', 'g_ffn', 'L0_xattn_W_k', 'L0_xattn_b_k', 'L0_xattn_ln_gamma', 'L0_xattn_ln_beta',
        'L0_ffn_gate_w', 'L0_ffn_gate_b', 'L0_ffn_expert_w', 'L0_ffn_expert_b', 'L1_xattn_Wq', 'L1_xattn_Wkv_expand',
        'L1_xattn_Wout', 'L1_ffn_w_gate', 'L1_ffn_w_up', 'L1_ffn_w_down', 'L2_xattn_Wq', 'L2_xattn_Wk',
        'L2_xattn_gamma_raw', 'L2_ffn_w12', 'L2_ffn_w3', 'L2_ffn_router_w', 'L2_ffn_expert_bias', 'L2_ffn_sw1',
        'L2_ffn_sw2', 'L2_ffn_sw3', 'L3_ffn_W_router', 'L3_ffn_W_sgate', 'L3_ffn_Ws_gate_up', 'L3_ffn_Ws_down',
        'L3_ffn_We_gate_up', 'L3_ffn_We_down']


def kernel(**inputs):
    import numpy as _np
    import concourse.bacc as _bacc
    from concourse import mybir as _mybir
    from concourse.bass_utils import run_bass_kernel_spmd as _run

    nc = _bacc.Bacc("TRN2", target_bir_lowering=False, num_devices=1)
    arrays, args = {}, []

    def give(name, a):
        arrays[name] = a
        args.append(nc.dram_tensor(name, a.shape, _mybir.dt.from_np(a.dtype), kind="ExternalInput").ap())

    for name in _INS:
        a = _np.ascontiguousarray(inputs[name])
        give(f"in_{name}", a.reshape(1) if a.ndim == 0 else a)
    had = _np.ones((1, 1), _np.float32)
    while had.shape[0] < P:
        had = _np.block([[had, had], [had, -had]])
    row = _np.arange(P)
    later = _np.where(row[None, :] > row[:, None], NEG, 0.0)
    give("consts", _np.concatenate([_np.eye(P), had, later, later.T, _np.tile(_np.arange(E), (P, 1))], 1)
         .astype(_np.float32))
    args.append(nc.dram_tensor("out_0", (B, S, D), _mybir.dt.float32, kind="ExternalOutput").ap())
    flamingo_gated(nc, *args)
    r = _run(nc, [arrays], core_ids=[0])
    return r.results[0]["out_0"]
```

```python
from contextlib import ExitStack

import concourse.bass as bass
from concourse import mybir

F32 = mybir.dt.float32
BF16 = mybir.dt.bfloat16
U32 = mybir.dt.uint32
ALU = mybir.AluOpType
ACT = mybir.ActivationFunctionType
X = mybir.AxisListType.X

P = 128
B, S, D, C = 4, 256, 256, 64
T = S // P
DC = D // P
W = T * D
E = 8
H_FFN = 1024
HC = H_FFN // P
H_R2 = 128
H_S3, H_R3 = 704, 176
SC3, RC3 = -(-H_S3 // P), E * H_R3 // P
NH1, HD1 = 16, 16
NH3, KV3, HD3 = 32, 8, 8
K1 = 6 * HD1
K3 = 6 * HD3
G1 = 4
M1, M3 = G1 * (HD1 + 1), KV3 * (HD3 + 1)
TOPK_ROW = max(1, int(S * 0.3))
TURNS = B // 2
BANK = 512
ROUND = 1.5 * 2.0 ** 23
QB = 128.0
NEG = -1e30
EPS, EPS0 = 1e-5, 1e-6


class Signal:

    def __init__(self, sem, per=1, credit=0):
        self.sem, self.per, self.credit = sem, per, credit

    def count(self, n, k=None):
        return n * self.per + (self.per if k is None else k) + self.credit

    def free(self, n, k=0):
        return n * self.per + k + 1


class Fills:

    def __init__(self, filled, filled_before, slots, drained, drained_before, keys, turns):
        self.filled, self.filled_before, self.slots = filled, filled_before, slots
        self.banks_drained, self.drained_before = drained, drained_before
        self.index = {key: j for j, key in enumerate(keys)}
        self.per = len(keys)
        assert len(self.index) == self.per and (turns == 1 or self.per % len(slots) == 0)

    def slot(self, key):
        return self.slots[self.index[key] % len(self.slots)]

    def drained(self, key):
        return self.banks_drained[self.index[key] % len(self.slots)]

    def empty(self, i, key):
        j, m = self.index[key], len(self.slots)
        return self.drained_before[j % m] + i * (self.per // m) + j // m

    def full(self, i, key):
        return self.filled_before + i * self.per + self.index[key] + 1

    def read(self, i, key):
        return self.empty(i, key) + 1


class Space:

    def __init__(self, tensor, at=0):
        self.tensor, self.at = tensor, at

    def take(self, n, dt=F32, parts=P):
        words = n if dt is F32 else (n + 1) // 2
        view = self.tensor[0:parts, self.at:self.at + words]
        self.at += words
        assert self.at <= self.tensor.shape[1], (self.at, self.tensor.shape)
        return view if dt is F32 else view.bitcast(dt)


def flamingo_gated(nc, x, ctx_512, g_xattn, g_ffn, W_k0, b_k0, ln_gamma, ln_beta, gate_w, gate_b, expert_w, expert_b,
                   Wq1, Wkv1, Wout1, w_gate, w_up, w_down, Wq2, Wk2, gamma_raw, w12, w3, router_w, expert_bias,
                   sw1, sw2, sw3, W_router, W_sgate, Ws_gate_up, Ws_down, We_gate_up, We_down, consts, out):
    with ExitStack() as ctx:
        def sb(name, shape, dt=F32):
            return ctx.enter_context(nc.sbuf_tensor(name, shape, dt))

        def sem(name):
            return ctx.enter_context(nc.semaphore(name))

        psum = ctx.enter_context(nc.psum_tensor("psum", [P, 8 * BANK], F32))

        xs = sb("xs", [P, B, W])
        adj = sb("adj", [P, B, T * S])
        ctx_all = sb("ctx_all", [P, B, T * C])
        con = sb("con", [P, 4 * P + E])
        ident, hadamard, iota8 = con[:, 0:P], con[:, P:2 * P], con[:, 4 * P:4 * P + E]
        conb = sb("conb", [P, 4 * P], BF16)
        identb, mask_q, mask_k, onesb = (conb[:, k * P:(k + 1) * P] for k in range(4))
        bias3 = sb("bias3", [3, E * D], BF16)
        small = Space(sb("small", [P, 1600]))
        eps5, eps6, onecol = small.take(1), small.take(1), small.take(1)
        graw, gt, gt0_half = small.take(8), small.take(8), small.take(1)
        gam, gam_s, keep_x, keep_a = (small.take(1) for _ in range(4))
        lng, lnb = small.take(S), small.take(S)
        bk_row, bk_col = small.take(C), small.take(1, parts=C)
        gate0, gate0_b = small.take(DC * E), small.take(E)
        bias_f, bias_r = small.take(E * D // P), small.take(E * D // P)
        bias_p = [small.take(E * D // P, BF16) for _ in range(3)]
        raw64 = small.take(3 * C, parts=C)
        wT64 = small.take(3 * C, parts=C)
        wk0T, wq2T, wk2T = (wT64[:, k * C:(k + 1) * C] for k in range(3))
        wsum, wmean, wscale = small.take(3), small.take(3), small.take(3)
        ebias = small.take(E)
        rT = small.take(DC * (2 * E + 1))
        r2T, r3T = rT[:, 0:DC * E], rT[:, DC * E:]

        early = sb("early", [P, 12800])
        sp0 = Space(early)
        ex_w = sp0.take(DC * E * D)
        wgT, wuT = sp0.take(DC * H_FFN, BF16), sp0.take(DC * H_FFN, BF16)
        wdT = sp0.take(HC * D, BF16)
        wq1T, wout1T, wkv1T = sp0.take(DC * D), sp0.take(DC * D), sp0.take(2 * D, parts=C)
        sp0 = Space(early, 8704)
        raw_sw = [sp0.take(2048), sp0.take(2048), early[:, 0:2048]]
        raw_w12, raw_w3 = early[:, 8704:12800], early[:, 0:2048]
        raw_r2, raw_r3 = early[0:E, 2048:2048 + D], early[0:E + 1, 2048 + D:2048 + 2 * D]
        sp3 = Space(early)
        we_gu, ws_gu = sp3.take(DC * E * 2 * H_R3), sp3.take(DC * 2 * H_S3)
        we_dn, ws_dn = sp3.take(RC3 * D), sp3.take(SC3 * D)

        late = sb("late", [P, 12288])
        sp2 = Space(late)
        raw_wq1, raw_wkv1, raw_wout1 = sp2.take(W), sp2.take(4 * C), sp2.take(W)
        raw_f1 = [sp2.take(2048) for _ in range(3)]
        tern = [sp2.take(2048, BF16) for _ in range(3)]
        sp2 = Space(late)
        w12T, w3T = sp2.take(DC * E * 2 * H_R2), sp2.take(E * D)
        sw1T, sw2T, sw3T = sp2.take(DC * H_FFN), sp2.take(DC * H_FFN), sp2.take(HC * D)

        shared = sb("shared", [P, 6912])
        arena = [sb(f"arena{s}", [P, 6400]) for s in range(2)]

        def cols(n, k):
            return [small.take(n * k).rearrange("p (n k) -> p n k", n=n) for _ in range(2)]

        st, mv, m8, idf = cols(T, 6), cols(T, 2), cols(T, 8), cols(T, 2)
        idx = [v.bitcast(U32) for v in cols(T, 8)]
        lg, oh, pick, cw = cols(T, E), cols(T, E), cols(T, E), cols(T, E)
        lnv, y0, ya, yb, rstd, c1, c2, c3, c4 = ([small.take(T) for _ in range(2)] for _ in range(9))

        def carve(*parts):
            made = []
            for s in range(2):
                sp = Space(arena[s])
                made.append([sp.take(*p) for p in parts])
            return [list(v) for v in zip(*made)]

        xn, xnT, cx, ctxT = carve((W,), (W,), (T * C,), (S, F32, C))
        base = (W + W + T * C + S,)
        _, kv0, kvT0, oT0, z0, e0 = carve(base, (T * C,), (S, F32, C), (S, F32, C), (T * S,), (T * S,))
        _, acc0, qkT, sim, work, th, aa = carve(base, (W,), (2 * S, F32, C), (T * S,), (T * S,), (T * S,), (T * S,))
        rexp = [shared[:, t * 2048:(t + 1) * 2048] for t in range(T)]
        _, qT1, kT1, nmax1, sh1, shT1, rec1 = carve(base, (NH1 * S, BF16), (NH1 * S, BF16), (T * NH1,),
                                                    (T * 2 * NH1, BF16), (S, BF16, 2 * NH1), (T * NH1,))
        sph = Space(shared)
        qs1 = [sph.take(T * NH1 * K1, BF16) for _ in range(2)]
        ks1 = [sph.take(T * NH1 * (K1 + 2), BF16) for _ in range(2)]
        rest1 = [late[:, k * W:(k + 1) * W] for k in range(2)]
        sp1 = Space(late, 2 * W + 4 * C)
        vpad1 = [sp1.take(T * NH1 * M1) for _ in range(2)]
        pexp1 = [late[:, 12288 - (k + 1) * 768:12288 - k * 768] for k in range(2)]
        _, qT3, kT3, vpad3, nmax3, sh3, shT3, rec3 = carve(base, (NH3 // 2 * S, BF16), (KV3 * S, BF16),
                                                           (T * KV3 * M3 + M3,), (T * NH3,), (T * 2 * NH3, BF16),
                                                           (S, BF16, 2 * NH3), (T * NH3,))
        sph = Space(shared)
        qs3 = [sph.take(T * NH3 * 64, BF16) for _ in range(2)]
        ks3 = [sph.take(T * KV3 * P, BF16) for _ in range(2)]
        sp3 = Space(late)
        rest3 = [sp3.take(W) for _ in range(2)]
        pexp3 = [sp3.take(2 * BANK) for _ in range(2)]
        oT13 = [arena[s][:, base[0]:base[0] + 2 * BANK] for s in range(2)]
        _, xq, xqT, ha, hb, yqT = carve((W,), (W, BF16), (W, BF16), (T * H_FFN,), (T * H_FFN,), (T * H_FFN, BF16))
        sph = Space(shared)
        sg1 = [sph.take(BANK) for _ in range(4)]
        bfly, yqb = sph.take(H_FFN), [sph.take(T * H_FFN, BF16) for _ in range(2)]
        _, hsT2, hrT2 = carve(base, (HC * S,), (T * E * P,))
        sph = Space(shared)
        sg2 = [sph.take(S) for _ in range(4)]
        hr2 = [sph.take(E * H_R2) for _ in range(T)]
        _, hsT3, hrT3 = carve(base, (SC3 * S,), (T * RC3 * P,))
        sph = Space(shared)
        sg3 = [sph.take(S) for _ in range(4)]
        hr3 = [sph.take(E * H_R3) for _ in range(T)]

        ld = {n: sem("ld_" + n) for n in ("x", "ctx", "con", "cols", "ex", "bias", "l1a", "l1f", "sw12", "sw3",
                                          "w12", "w3", "l3")}
        stored = sem("stored")
        const_ready, gates_ready, bias_ready = sem("const_ready"), sem("gates_ready"), sem("bias_ready")
        tanh_ready, egam_ready, wsum_ready, tern_ready = (sem("tanh_ready"), sem("egam_ready"), sem("wsum_ready"),
                                                          sem("tern_ready"))
        bank_drained = [sem(f"bank{k}_drained") for k in range(8)]
        filled = {g: sem("filled_" + g) for g in "ABC"}

        def sig(name, per=1, credit=0):
            return Signal(sem(name), per, credit)

        ln_names = ("l0x", "l0s", "l0f", "l1x", "l1f", "l2x", "l2f", "l3x", "l3f")
        stats_ready = {l: sig(f"{l}_stats_ready") for l in ln_names}
        rstd_ready = {l: sig(f"{l}_rstd_ready") for l in ln_names}
        xn_ready = {l: sig(f"{l}_xn_ready") for l in ln_names}
        cx_ready = {l: sig(f"{l}_cx_ready") for l in ("l0x", "l0f", "l1x", "l3x")}
        l0_z_ready, l0_e_ready = sig("l0_z_ready"), sig("l0_e_ready")
        l0_pick_ready, rexp_free = sig("l0_pick_ready"), sig("rexp_free", T, 2)
        aa_ready = sig("aa_ready")
        q1_ready, k1_ready = ({l: sig(f"{l}_{n}") for l in ("l1x", "l3x")}
                              for n in ("q1_ready", "k1_ready"))
        qparts_ready, kparts_ready = ({l: sig(f"{l}_{n}") for l in ("l1x", "l3x")}
                                      for n in ("qparts_ready", "kparts_ready"))
        vpad_ready, pads_ready = sem("vpad_ready"), sem("pads_ready")
        shift_ready = {l: sig(f"{l}_shift_ready") for l in ("l1x", "l3x")}
        shift_in = {"l1x": sig("l1x_shift_in", 32), "l3x": sig("l3x_shift_in", 64)}
        v_ready = sig("l3x_v_ready")
        pv_done = {"l1x": sig("l1x_pv_done", NH1 // 2, 2), "l3x": sig("l3x_pv_done", NH3 // 2, 2)}
        xq_ready, yq_ready = sig("xq_ready"), sig("yq_ready", T)
        sg2_ready, sg3_ready = sig("sg2_ready", HC + T * E // 2), sig("sg3_ready", SC3 + T * E)
        lg3_ready, sc3_ready = sig("lg3_ready"), sig("sc3_ready")
        x_done = sig("x_done")
        with_credit = (rexp_free, pv_done["l1x"], pv_done["l3x"])

        counts, drains, loop_start = {g: 0 for g in "ABCV"}, [1] * 8, {}

        def plan(loop, turns, **groups):
            loop_start[loop] = list(drains)
            made = {}
            for g, (firsts, wide, keys) in groups.items():
                made[g] = Fills(filled.get(g), counts[g], [psum[:, k * BANK:(k + wide) * BANK] for k in firsts],
                                [bank_drained[k] for k in firsts], [drains[k] for k in firsts], keys, turns)
                counts[g] += turns * len(keys)
                for j in range(len(keys)):
                    drains[firsts[j % len(firsts)]] += turns
            return made

        def streams(*stages):
            return [(k[0], s, *k[1:]) for stage in stages for s in range(2) for k in stage]

        pl = {}
        pl["prep0"] = plan("prep0", 1, A=([0], 1, [("w64",)]))
        pl["l0x"] = plan("l0x", TURNS, A=([0, 1, 2, 3, 4], 1, streams([("xT",)], [("cT",)], [("kv",)], [("oT",)], [("sim",)])))
        pl["l0f"] = plan("l0f", TURNS,
                         A=([6, 7], 1, streams([("xT",)], [("gate",)])),
                         B=([0, 1, 2, 3], 1, streams([("ex", t, k) for t in range(T) for k in range(E // 2)])),
                         C=([4, 5], 1, streams([("cT",)], [("qk",)], [("sim",)], [("AT",)])))
        pl["prep1"] = plan("prep1", 1, A=([0, 1, 2, 3], 1, [("wq",), ("wkv",), ("wout",)]))
        pl["l1x"] = plan("l1x", TURNS,
                         A=([4, 5], 1, streams([("xT",)], [("cT",)],
                                               [("qsT", k) for k in range(4)] + [("ksT", k) for k in range(4)],
                                               [("max", k) for k in range(12)] + [("shT",)], [("tok", t) for t in range(T)],
                                               [("oT",)], [("out",)])),
                         B=([0, 2], 2, streams([("q",), ("kv",)], [("sc", k) for k in range(NH1 // 2)])),
                         V=([6], 2, streams([("pv",)])))
        pl["prep1b"] = plan("prep1b", 1, A=([0, 1, 2, 3], 1, [("tern", w, k) for w in range(3) for k in range(2)]))
        pl["prep2a"] = plan("prep2a", 1, A=([0, 1, 2, 3], 1, [("sw", w, k) for w in range(3) for k in range(4)]))
        pl["l1f"] = plan("l1f", TURNS,
                         A=([6, 7], 1, streams([("xT",)], [("yT", 0), ("yT", 1)], [("dn",)])),
                         B=([0, 1, 2, 3], 1, streams([(w, t, h) for t in range(T) for h in range(2) for w in "gu"])),
                         C=([4, 5], 1, streams([("hT", t, h) for t in range(T) for h in range(2)],
                                               [("had", t, h) for t in range(T) for h in range(2)])))
        pl["prep2b"] = plan("prep2b", 1, A=([0, 1, 2, 3], 1, [("w12", k) for k in range(8)] + [("w3", k) for k in range(4)]
                                           + [("r",)]))
        pl["l2f"] = plan("l2f", TURNS,
                         A=([6, 7], 1, streams([("xT",)], [("gate",)], [("hrT", t, k) for t in range(T) for k in range(2)]
                                               + [("dn",)])),
                         B=([0, 1, 2, 3], 1, streams([("sh", j) for j in range(HC)]
                                                     + [("ro", t, k) for t in range(T) for k in range(E // 2)])))
        pl["l3x"] = plan("l3x", TURNS,
                         A=([4, 5], 1, streams([("qsT", k) for k in range(4)] + [("ksT", k) for k in range(2)],
                                               [("max", k) for k in range(32)] + [("shT",)], [("tok", t) for t in range(T)])),
                         B=([0, 2], 2, streams([("sc", k) for k in range(NH3 // 2)])),
                         V=([6], 2, streams([("pv",)])))
        pl["l3f"] = plan("l3f", TURNS,
                         A=([6, 7], 1, streams([("xT",)], [("gate",)], [("hrT", t, k) for t in range(T) for k in range(3)]
                                               + [("dnS",), ("dnR",)])),
                         B=([0, 1, 2, 3], 1, streams([("sh", j) for j in range(SC3)]
                                                     + [("ro", t, k) for t in range(T) for k in range(E)])))

        def q3d(v, *dims):
            names = "abcd"[:len(dims)]
            return v.rearrange(f"p ({' '.join(names)}) -> p {' '.join(names)}", **dict(zip(names, dims)))

        waits_passed = sem("waits_passed")

        def own_instruction(eng):
            eng.sem_inc(waits_passed, 1)

        block = ctx.enter_context(nc.Block())

        @block.sync
        def _(sp):
            def load(dst, src, name):
                sp.dma_start(dst, src).then_inc(ld[name], 16)

            load(con[:], consts, "con")
            load(ctx_all[:].rearrange("p b (t c) -> p (b t) c", t=T), ctx_512.rearrange("b (t p) c -> p (b t) c", p=P), "ctx")
            load(xs[:].rearrange("p b (t d) -> p (b t) d", t=T), x.rearrange("b (t p) d -> p (b t) d", p=P), "x")
            for k, w in enumerate((W_k0, Wq2, Wk2)):
                load(raw64[:, k * C:(k + 1) * C], w, "cols")
            load(graw[:, 0:4], g_xattn.partition_broadcast(P), "cols")
            load(graw[:, 4:8], g_ffn.partition_broadcast(P), "cols")
            load(gam, gamma_raw.partition_broadcast(P), "cols")
            load(lng, ln_gamma.partition_broadcast(P), "cols")
            load(lnb, ln_beta.partition_broadcast(P), "cols")
            load(bk_row, b_k0.partition_broadcast(P), "cols")
            load(bk_col, b_k0.rearrange("(c a) -> c a", a=1), "cols")
            load(gate0_b, gate_b.partition_broadcast(P), "cols")
            load(ebias, expert_bias.partition_broadcast(P), "cols")
            load(q3d(gate0, DC, E), gate_w.rearrange("(c p) e -> p c e", p=P), "cols")
            load(bias_f, expert_b.rearrange("e (q k) -> (e q) k", k=E * D // P), "cols")
            for c in range(DC):
                load(q3d(ex_w, DC, E, D)[:, c], expert_w.rearrange("e (c p) o -> c p e o", p=P)[c], "ex")
            load(q3d(raw_wq1, T, D), Wq1.rearrange("(o p) i -> p o i", p=P), "l1a")
            load(q3d(raw_wkv1, 4, C), Wkv1.rearrange("(o p) i -> p o i", p=P), "l1a")
            load(q3d(raw_wout1, T, D), Wout1.rearrange("(o p) i -> p o i", p=P), "l1a")
            load(q3d(raw_f1[0], HC, D), w_gate.rearrange("(o p) i -> p o i", p=P), "l1f")
            load(q3d(raw_f1[1], HC, D), w_up.rearrange("(o p) i -> p o i", p=P), "l1f")
            load(q3d(raw_f1[2], T, H_FFN), w_down.rearrange("(o p) i -> p o i", p=P), "l1f")
            load(q3d(raw_sw[0], HC, D), sw1.rearrange("(o p) i -> p o i", p=P), "sw12")
            load(q3d(raw_sw[1], HC, D), sw2.rearrange("(o p) i -> p o i", p=P), "sw12")
            sp.wait_ge(bias_ready, 1)
            for k in range(3):
                load(bias3[k:k + 1, :], bias_p[k], "bias")
            sp.wait_ge(pl["l0f"]["B"].filled, pl["l0f"]["B"].full(TURNS - 1, ("ex", 1, T - 1, E // 2 - 1)))
            load(q3d(raw_sw[2], T, H_FFN), sw3.rearrange("(o p) i -> p o i", p=P), "sw3")

            f = pl["l1x"]["A"]
            with sp.Fori(0, TURNS) as i:
                for s in range(2):
                    sp.wait_ge(f.drained(("shT", s)), f.read(i, ("shT", s)))
                    for r in range(2):
                        sp.dma_start(qT1[s][K1 + r:K1 + r + 1, :], shT1[s][r * NH1:(r + 1) * NH1, :])\
                          .then_inc(shift_in["l1x"].sem, 16)

            sp.wait_ge(pl["prep2a"]["A"].filled, pl["prep2a"]["A"].full(0, ("sw", 1, 3)))
            load(q3d(raw_w12, E * 2, D), w12.rearrange("e (h p) d -> p (e h) d", p=P), "w12")
            sp.wait_ge(pl["prep2a"]["A"].filled, pl["prep2a"]["A"].full(0, ("sw", 2, 3)))
            load(q3d(raw_w3, E * 2, H_R2), w3.rearrange("e (d p) h -> p (e d) h", p=P), "w3")
            load(raw_r2, router_w, "w3")
            load(raw_r3[0:E, :], W_router, "w3")
            load(raw_r3[E:E + 1, :], W_sgate, "w3")
            sp.wait_ge(pl["l1f"]["A"].filled, pl["l1f"]["A"].full(TURNS - 1, ("dn", 1)))
            sp.wait_ge(pl["prep2b"]["A"].filled, pl["prep2b"]["A"].full(0, ("r",)))
            load(q3d(ws_gu, DC, 2 * H_S3), Ws_gate_up.rearrange("(c p) h -> p c h", p=P), "l3")
            load(q3d(ws_dn, SC3, D)[:, 0:SC3 - 1], Ws_down[0:(SC3 - 1) * P, :].rearrange("(j p) o -> p j o", p=P), "l3")
            load(q3d(ws_dn, SC3, D)[0:H_S3 - (SC3 - 1) * P, SC3 - 1], Ws_down[(SC3 - 1) * P:H_S3, :], "l3")
            for c in range(DC):
                load(q3d(we_gu, DC, E, 2 * H_R3)[:, c], We_gate_up.rearrange("e (c p) h -> c p e h", p=P)[c], "l3")
            load(q3d(we_dn, RC3, D), We_down.rearrange("e i o -> (e i) o").rearrange("(j p) o -> p j o", p=P), "l3")

            f = pl["l3x"]["A"]
            with sp.Fori(0, TURNS) as i:
                for s in range(2):
                    sp.wait_ge(f.drained(("shT", s)), f.read(i, ("shT", s)))
                    for r in range(2):
                        for par in range(2):
                            row, src = 64 * par + K3 + r, (2 * r + par) * (NH3 // 2)
                            sp.dma_start(qT3[s][row:row + 1, :], shT3[s][src:src + NH3 // 2, :])\
                              .then_inc(shift_in["l3x"].sem, 16)

            out_v = out.rearrange("b (t p) d -> b p t d", p=P)
            with sp.Fori(0, TURNS) as i:
                for s in range(2):
                    n = 2 * i + s
                    sp.wait_ge(x_done.sem, x_done.count(n))
                    sp.dma_start(out_v[n], q3d(xs[:, n, :], T, D)).then_inc(stored, 16)
            sp.wait_ge(stored, 16 * B)

        @block.gpsimd
        def _(pool):
            for signal in with_credit:
                pool.sem_inc(signal.sem, signal.credit)
            for k in range(8):
                pool.sem_inc(bank_drained[k], 1)
            pool.memset(eps5, EPS)
            pool.memset(eps6, EPS0)
            pool.memset(onecol, 1.0)
            pool.memset(onesb, 1.0)
            pool.wait_ge(ld["con"], 16)
            pool.tensor_copy(identb, ident)
            pool.tensor_copy(conb[:, P:3 * P], con[:, 2 * P:4 * P])
            pool.drain().then_inc(const_ready, 1)
            pool.wait_ge(wsum_ready, 1)
            pool.partition_all_reduce(wmean, wsum, P, bass.bass_isa.ReduceOp.add).then_inc(wsum_ready, 1)
            pool.wait_ge(wsum_ready, 3)
            for w in range(3):
                pool.tensor_scalar(raw_f1[w], raw_f1[w], wscale[:, w:w + 1], ROUND, ALU.mult, ALU.add)
            pool.drain()
            for w in range(3):
                pool.tensor_scalar(raw_f1[w], raw_f1[w], -ROUND, 1.0, ALU.add, ALU.mult)
            pool.drain()
            for w in range(3):
                last = pool.tensor_scalar(tern[w], raw_f1[w], 1.0, -1.0, ALU.min, ALU.max)
            last.then_inc(tern_ready, 1)

            pool.drain()
            for s in range(2):
                pool.memset(vpad1[s], 0.0)
            pool.drain()
            for s in range(2):
                v = vpad1[s].rearrange("p (n x) -> p n x", x=G1 * M1)
                for k in range(G1):
                    at = k * (M1 + HD1 + 1) + HD1
                    pool.memset(v[:, :, at:at + 1], 1.0)
            pool.wait_ge(rexp_free.sem, rexp_free.count(B - 1))
            for s in range(2):
                pool.memset(ks1[s].rearrange("p (h k) -> p h k", k=K1 + 2)[:, :, K1:], 1.0)
            pool.drain().then_inc(vpad_ready, 1)

            def diagonal3(s, t):
                return vpad3[s][:, t * KV3 * M3:(t + 1) * KV3 * M3 + M3].rearrange("p (j x) -> p j x", x=M3 + HD3 + 1)

            pool.wait_ge(pl["l2f"]["A"].filled, pl["l2f"]["A"].full(TURNS - 1, ("dn", 1)))
            for s in range(2):
                pool.memset(vpad3[s], 0.0)
                pool.memset(qs3[s].rearrange("p (h k) -> p h k", k=64)[:, :, K3:], 0.0)
                kv = ks3[s].rearrange("p (h k) -> p h k", k=64)
                pool.memset(kv[:, :, K3:K3 + 2], 1.0)
                pool.memset(kv[:, :, K3 + 2:], 0.0)
            pool.drain()
            for s in range(2):
                for t in range(T):
                    pool.memset(diagonal3(s, t)[:, :, HD3:HD3 + 1], 1.0)
            pool.drain().then_inc(pads_ready, 1)
            with pool.Fori(0, TURNS) as i:
                for s in range(2):
                    n = 2 * i + s
                    pool.wait_ge(cx_ready["l3x"].sem, cx_ready["l3x"].count(n))
                    own_instruction(pool)
                    for t in range(T):
                        pool.tensor_copy(diagonal3(s, t)[:, :, 0:HD3],
                                         cx[s][:, t * C:(t + 1) * C].rearrange("p (j k) -> p j k", k=HD3))
                    pool.drain().then_inc(v_ready.sem, 1)

        @block.tensor
        def _(pe):
            def banks_free(loop):
                for k in range(8):
                    pe.wait_ge(bank_drained[k], loop_start[loop][k])

            def turn(f, i, key, blocks, idn, dt=F32):
                pe.wait_ge(f.drained(key), f.empty(i, key))
                v = f.slot(key)
                v = v if dt is F32 else v.bitcast(dt)
                if blocks[0][2].shape[1] < P:
                    own_instruction(pe)
                for parts, at, src in blocks:
                    k = src.shape[0]
                    last = pe.transpose(v[0:parts, at:at + k], src, idn[0:k, 0:k])
                last.then_inc(f.filled, 1)

            def turn_x(f, i, s, key, src, idn=ident, dt=F32):
                turn(f, i, key, [(P, c * S + t * P, src[:, t * D + c * P:t * D + (c + 1) * P])
                                 for c in range(DC) for t in range(T)], idn, dt)

            def turn_cx(f, i, s):
                turn(f, i, ("cT", s), [(C, t * P, cx[s][:, t * C:(t + 1) * C]) for t in range(T)], ident)

            pe.wait_ge(ld["con"], 16)
            pe.wait_ge(ld["cols"], 16 * 14)
            pe.wait_ge(const_ready, 1)
            turn(pl["prep0"]["A"], 0, ("w64",), [(C, k * C, raw64[:, k * C:(k + 1) * C]) for k in range(3)], ident)

            banks_free("l0x")
            f = pl["l0x"]["A"]
            with pe.Fori(0, TURNS) as i:
                for s in range(2):
                    pe.wait_ge(xn_ready["l0x"].sem, xn_ready["l0x"].count(2 * i + s))
                    turn_x(f, i, s, ("xT", s), xn[s])
                for s in range(2):
                    pe.wait_ge(cx_ready["l0x"].sem, cx_ready["l0x"].count(2 * i + s))
                    turn_cx(f, i, s)
                for s in range(2):
                    pe.wait_ge(f.drained(("cT", s)), f.read(i, ("cT", s)))
                    pe.wait_ge(f.drained(("kv", s)), f.empty(i, ("kv", s)))
                    v = f.slot(("kv", s))
                    for t in range(T):
                        pe.matmul(v[:, t * C:(t + 1) * C], ctxT[s][:, t * P:(t + 1) * P], wk0T, start=True, stop=True)
                    pe.matmul(v[0:C, S:2 * S], wk0T, ctxT[s], start=True, stop=True).then_inc(f.filled, 1)
                for s in range(2):
                    pe.wait_ge(f.drained(("kv", s)), f.read(i, ("kv", s)))
                    pe.wait_ge(f.drained(("xT", s)), f.read(i, ("xT", s)))
                    pe.wait_ge(f.drained(("oT", s)), f.empty(i, ("oT", s)))
                    v = f.slot(("oT", s))
                    for t in range(T):
                        mm = pe.matmul(v[0:C, 0:S], kv0[s][:, t * C:(t + 1) * C], xnT[s][:, t * S:(t + 1) * S],
                                       start=(t == 0), stop=(t == T - 1))
                    mm.then_inc(f.filled, 1)
                for s in range(2):
                    pe.wait_ge(f.drained(("oT", s)), f.read(i, ("oT", s)))
                    pe.wait_ge(f.drained(("sim", s)), f.empty(i, ("sim", s)))
                    v = f.slot(("sim", s))
                    for t in range(T):
                        mm = pe.matmul(v[:, t * S:(t + 1) * S], oT0[s][:, t * P:(t + 1) * P], kvT0[s], start=True, stop=True)
                    mm.then_inc(f.filled, 1)

            banks_free("l0f")
            fa, fb, fc = (pl["l0f"][g] for g in "ABC")
            pe.wait_ge(ld["ex"], 16 * DC)
            pe.wait_ge(ld["bias"], 16 * 3)
            with pe.Fori(0, TURNS) as i:
                for s in range(2):
                    pe.wait_ge(xn_ready["l0f"].sem, xn_ready["l0f"].count(2 * i + s))
                    turn_x(fa, i, s, ("xT", s), xn[s])
                for s in range(2):
                    pe.wait_ge(cx_ready["l0f"].sem, cx_ready["l0f"].count(2 * i + s))
                    turn_cx(fc, i, s)
                for s in range(2):
                    pe.wait_ge(fa.drained(("xT", s)), fa.read(i, ("xT", s)))
                    pe.wait_ge(fa.drained(("gate", s)), fa.empty(i, ("gate", s)))
                    v = fa.slot(("gate", s))
                    for t in range(T):
                        for c in range(DC):
                            mm = pe.matmul(v[:, t * E:(t + 1) * E], xnT[s][:, c * S + t * P:c * S + (t + 1) * P],
                                           gate0[:, c * E:(c + 1) * E], start=(c == 0), stop=(c == DC - 1))
                    mm.then_inc(fa.filled, 1)
                for s in range(2):
                    pe.wait_ge(fc.drained(("cT", s)), fc.read(i, ("cT", s)))
                    pe.wait_ge(fc.drained(("qk", s)), fc.empty(i, ("qk", s)))
                    v = fc.slot(("qk", s))
                    own_instruction(pe)
                    pe.matmul(v[0:C, 0:S], wq2T, ctxT[s], start=True, stop=True)
                    pe.matmul(v[0:C, S:2 * S], wk2T, ctxT[s], start=True, stop=True).then_inc(fc.filled, 1)
                for s in range(2):
                    pe.wait_ge(fc.drained(("qk", s)), fc.read(i, ("qk", s)))
                    pe.wait_ge(fc.drained(("sim", s)), fc.empty(i, ("sim", s)))
                    v = fc.slot(("sim", s))
                    for t in range(T):
                        mm = pe.matmul(v[:, t * S:(t + 1) * S], qkT[s][:, t * P:(t + 1) * P], qkT[s][:, S:2 * S],
                                       start=True, stop=True)
                    mm.then_inc(fc.filled, 1)
                for s in range(2):
                    for t in range(T):
                        for k in range(E // 2):
                            pe.wait_ge(fb.drained(("ex", s, t, k)), fb.empty(i, ("ex", s, t, k)))
                            v = fb.slot(("ex", s, t, k))
                            for c in range(DC):
                                at = c * E * D + k * 2 * D
                                pe.matmul(v, xnT[s][:, c * S + t * P:c * S + (t + 1) * P], ex_w[:, at:at + 2 * D],
                                          start=(c == 0), stop=False)
                            pe.matmul(v, onesb[0:3, :], bias3[:, k * 2 * D:(k + 1) * 2 * D],
                                      start=False, stop=True).then_inc(fb.filled, 1)
                    pe.wait_ge(aa_ready.sem, aa_ready.count(2 * i + s))
                    turn(fc, i, ("AT", s), [(P, t * S + u * P, aa[s][:, u * S + t * P:u * S + (t + 1) * P])
                                            for t in range(T) for u in range(T)], ident)

            banks_free("prep1")
            f = pl["prep1"]["A"]
            pe.wait_ge(ld["l1a"], 16 * 3)
            for key, raw in ((("wq",), raw_wq1), (("wout",), raw_wout1)):
                if key == ("wout",):
                    turn(f, 0, ("wkv",), [(C, o * P, raw_wkv1[:, o * C:(o + 1) * C]) for o in range(4)], ident)
                turn_x(f, 0, 0, key, raw)
            def attention(layer, i, score_max, n_max, nshift, sh, score_exp, values, n_exp, token_blocks):
                fm, fe = pl[layer]["A"], pl[layer]["B"]

                def shift(s):
                    pe.wait_ge(shift_ready[layer].sem, shift_ready[layer].count(2 * i + s))
                    turn(fm, i, ("shT", s), [(nshift, t * P, sh[s][:, t * nshift:(t + 1) * nshift]) for t in range(T)],
                         identb, BF16)

                def tokens(s):
                    fv = pl[layer]["V"]
                    pe.wait_ge(fv.drained(("pv", s)), fv.read(i, ("pv", s)))
                    for t in range(T):
                        turn(fm, i, ("tok", s, t), token_blocks(s, t), ident)

                def exponentials(s, between):
                    pe.wait_ge(shift_in[layer].sem, shift_in[layer].count(2 * i + s))
                    for m in range(n_exp + 1):
                        if m < n_exp:
                            score_exp(i, s, m)
                        for k in between[m]:
                            score_max(i, 1, k)
                        if s == 1 and m == 2:
                            tokens(0)
                        if m == 0:
                            pe.wait_ge(pl[layer]["V"].drained(("pv", s)), pl[layer]["V"].empty(i, ("pv", s)))
                            if layer == "l3x":
                                pe.wait_ge(v_ready.sem, v_ready.count(2 * i + s))
                        else:
                            pe.wait_ge(fe.drained(("sc", s, m - 1)), fe.read(i, ("sc", s, m - 1)))
                            values(s, m - 1).then_inc(pv_done[layer].sem, 1)

                for k in range(n_max):
                    score_max(i, 0, k)
                shift(0)
                head = min(4, n_max)
                for k in range(head):
                    score_max(i, 1, k)
                rest = list(range(head, n_max))
                cut = [len(rest) * m // (n_exp + 1) for m in range(n_exp + 2)]
                exponentials(0, [rest[cut[m]:cut[m + 1]] for m in range(n_exp + 1)])
                shift(1)
                exponentials(1, [[]] * (n_exp + 1))
                tokens(1)

            banks_free("l1x")
            fa, fb = pl["l1x"]["A"], pl["l1x"]["B"]

            def max1(i, s, k):
                pe.wait_ge(fa.drained(("max", s, k)), fa.empty(i, ("max", s, k)))
                v = fa.slot(("max", s, k))
                t, heads, nk = (0, range(4 * k, 4 * k + 4), P) if k < 4 else (1, range(2 * k - 8, 2 * k - 6), S)
                for j, h in enumerate(heads):
                    pe.matmul(v[:, j * nk:(j + 1) * nk], qT1[s][0:K1, h * S + t * P:h * S + (t + 1) * P],
                              kT1[s][0:K1, h * S:h * S + nk], start=True, stop=True)
                    mm = pe.matmul(v[:, (j + 1) * nk - P:(j + 1) * nk], identb, mask_q, start=False, stop=True,
                                   skip_group_check=True)
                mm.then_inc(fa.filled, 1)

            def exp1(i, s, m):
                pe.wait_ge(fb.drained(("sc", s, m)), fb.empty(i, ("sc", s, m)))
                v = fb.slot(("sc", s, m))
                for j in range(2):
                    h, o = 2 * m + j, j * BANK
                    for t, at, nq in ((0, o, S), (1, o + S, P)):
                        pe.matmul(v[:, at:at + nq], kT1[s][0:K1 + 2, h * S + t * P:h * S + (t + 1) * P],
                                  qT1[s][0:K1 + 2, h * S + t * P:(h + 1) * S], start=True, stop=True)
                        mm = pe.matmul(v[:, at:at + P], identb, mask_k, start=False, stop=True, skip_group_check=True)
                mm.then_inc(fb.filled, 1)

            def values1(s, m):
                pv, p = pl["l1x"]["V"].slot(("pv", s)), pexp1[m % 2]
                for j in range(2):
                    h, o = 2 * m + j, j * (S + P)
                    g, first, last = h // G1, h % G1 == 0, h % G1 == G1 - 1
                    pe.matmul(pv[0:M1, g * S:(g + 1) * S], vpad1[s][:, h * M1:(h + 1) * M1], p[:, o:o + S],
                              start=first, stop=last)
                    mm = pe.matmul(pv[0:M1, g * S + P:(g + 1) * S], vpad1[s][:, (NH1 + h) * M1:(NH1 + h + 1) * M1],
                                   p[:, o + S:o + S + P], start=False, stop=last, skip_group_check=True)
                return mm

            def token_blocks1(s, t):
                return [(P, g * M1, oT13[s][0:M1, g * S + t * P:g * S + (t + 1) * P]) for g in range(NH1 // G1)]

            with pe.Fori(0, TURNS) as i:
                for s in range(2):
                    pe.wait_ge(xn_ready["l1x"].sem, xn_ready["l1x"].count(2 * i + s))
                    turn_x(fa, i, s, ("xT", s), xn[s])
                for s in range(2):
                    pe.wait_ge(cx_ready["l1x"].sem, cx_ready["l1x"].count(2 * i + s))
                    turn_cx(fa, i, s)
                for s in range(2):
                    pe.wait_ge(fa.drained(("xT", s)), fa.read(i, ("xT", s)))
                    pe.wait_ge(fb.drained(("q", s)), fb.empty(i, ("q", s)))
                    v = fb.slot(("q", s))
                    for t in range(T):
                        for c in range(DC):
                            mm = pe.matmul(v[:, t * D:(t + 1) * D], xnT[s][:, c * S + t * P:c * S + (t + 1) * P],
                                           wq1T[:, c * D:(c + 1) * D], start=(c == 0), stop=(c == DC - 1))
                    mm.then_inc(fb.filled, 1)
                    pe.wait_ge(fa.drained(("cT", s)), fa.read(i, ("cT", s)))
                    pe.wait_ge(fb.drained(("kv", s)), fb.empty(i, ("kv", s)))
                    v = fb.slot(("kv", s))
                    for t in range(T):
                        mm = pe.matmul(v[:, t * BANK:(t + 1) * BANK], ctxT[s][:, t * P:(t + 1) * P], wkv1T,
                                       start=True, stop=True)
                    mm.then_inc(fb.filled, 1)
                for s in range(2):
                    for name, ready, stack, pitch in (("qsT", qparts_ready, qs1, K1), ("ksT", kparts_ready, ks1, K1 + 2)):
                        pe.wait_ge(ready["l1x"].sem, ready["l1x"].count(2 * i + s))
                        for k in range(4):
                            turn(fa, i, (name, s, k), [(pitch, j * S + t * P, stack[s][:, (t * NH1 + 4 * k + j) * pitch:
                                                                                       (t * NH1 + 4 * k + j + 1) * pitch])
                                                       for j in range(4) for t in range(T)], identb, BF16)
                for s in range(2):
                    pe.wait_ge(fa.drained(("ksT", s, 3)), fa.read(i, ("ksT", s, 3)))
                    pe.wait_ge(fa.drained(("ksT", s, 2)), fa.read(i, ("ksT", s, 2)))
                attention("l1x", i, max1, 12, 2 * NH1, sh1, exp1, values1, NH1 // 2, token_blocks1)
                for s in range(2):
                    for t in range(T):
                        pe.wait_ge(fa.drained(("tok", s, t)), fa.read(i, ("tok", s, t)))
                    turn_x(fa, i, s, ("oT", s), xn[s])
                for s in range(2):
                    pe.wait_ge(fa.drained(("oT", s)), fa.read(i, ("oT", s)))
                    pe.wait_ge(fa.drained(("out", s)), fa.empty(i, ("out", s)))
                    v = fa.slot(("out", s))
                    for t in range(T):
                        for c in range(DC):
                            mm = pe.matmul(v[:, t * D:(t + 1) * D], xnT[s][:, c * S + t * P:c * S + (t + 1) * P],
                                           wout1T[:, c * D:(c + 1) * D], start=(c == 0), stop=(c == DC - 1))
                    mm.then_inc(fa.filled, 1)

            banks_free("prep1b")
            f = pl["prep1b"]["A"]
            pe.wait_ge(tern_ready, 1)
            for w in range(2):
                for c in range(DC):
                    turn(f, 0, ("tern", w, c), [(P, o * P, tern[w][:, o * D + c * P:o * D + (c + 1) * P])
                                                for o in range(HC)], identb, BF16)
            for k in range(2):
                turn(f, 0, ("tern", 2, k), [(P, (c % 4) * D + o * P, tern[2][:, o * H_FFN + c * P:o * H_FFN + (c + 1) * P])
                                            for c in range(4 * k, 4 * k + 4) for o in range(T)], identb, BF16)
            f = pl["prep2a"]["A"]
            pe.wait_ge(ld["sw12"], 16 * 2)
            for w in range(2):
                for k in range(4):
                    c, half = k // 2, k % 2
                    turn(f, 0, ("sw", w, k), [(P, j * P, raw_sw[w][:, (4 * half + j) * D + c * P:(4 * half + j) * D + (c + 1) * P])
                                              for j in range(4)], ident)
            pe.wait_ge(ld["sw3"], 16)
            for k in range(4):
                turn(f, 0, ("sw", 2, k), [(P, j * D + o * P, raw_sw[2][:, o * H_FFN + (2 * k + j) * P:o * H_FFN + (2 * k + j + 1) * P])
                                          for j in range(2) for o in range(T)], ident)

            banks_free("l1f")
            fa, fb, fc = (pl["l1f"][g] for g in "ABC")
            with pe.Fori(0, TURNS) as i:
                for s in range(2):
                    pe.wait_ge(xq_ready.sem, xq_ready.count(2 * i + s))
                    turn_x(fa, i, s, ("xT", s), xq[s], identb, BF16)
                for s in range(2):
                    pe.wait_ge(fa.drained(("xT", s)), fa.read(i, ("xT", s)))
                    for t in range(T):
                        for h in range(2):
                            for w, wT in (("g", wgT), ("u", wuT)):
                                pe.wait_ge(fb.drained((w, s, t, h)), fb.empty(i, (w, s, t, h)))
                                v = fb.slot((w, s, t, h))
                                for c in range(DC):
                                    at = c * H_FFN + h * BANK
                                    mm = pe.matmul(v, xqT[s][:, c * S + t * P:c * S + (t + 1) * P], wT[:, at:at + BANK],
                                                   start=(c == 0), stop=(c == DC - 1))
                                mm.then_inc(fb.filled, 1)
                for s in range(2):
                    for t in range(T):
                        for h in range(2):
                            pe.wait_ge(fb.drained(("u", s, t, h)), fb.read(i, ("u", s, t, h)))
                            turn(fc, i, ("hT", s, t, h), [(P, j * P, ha[s][:, t * H_FFN + (4 * h + j) * P:t * H_FFN + (4 * h + j + 1) * P])
                                                          for j in range(4)], ident)
                for s in range(2):
                    for t in range(T):
                        for h in range(2):
                            pe.wait_ge(fc.drained(("hT", s, t, h)), fc.read(i, ("hT", s, t, h)))
                            pe.wait_ge(fc.drained(("had", s, t, h)), fc.empty(i, ("had", s, t, h)))
                            v = fc.slot(("had", s, t, h))
                            for j in range(4):
                                at = t * H_FFN + (4 * h + j) * P
                                mm = pe.matmul(v[:, j * P:(j + 1) * P], hb[s][:, at:at + P], hadamard, start=True, stop=True)
                            mm.then_inc(fc.filled, 1)
                for s in range(2):
                    for t in range(T):
                        pe.wait_ge(yq_ready.sem, yq_ready.count(2 * i + s, t + 1))
                        turn(fa, i, ("yT", s, t), [(P, c * P, yqb[s][:, t * H_FFN + c * P:t * H_FFN + (c + 1) * P])
                                                   for c in range(HC)], identb, BF16)
                for s in range(2):
                    pe.wait_ge(fa.drained(("dn", s)), fa.empty(i, ("dn", s)))
                    v = fa.slot(("dn", s))
                    for t in range(T):
                        pe.wait_ge(fa.drained(("yT", s, t)), fa.read(i, ("yT", s, t)))
                        for c in range(HC):
                            at = t * H_FFN + c * P
                            mm = pe.matmul(v[:, t * D:(t + 1) * D], yqT[s][:, at:at + P], wdT[:, c * D:(c + 1) * D],
                                           start=(c == 0), stop=(c == HC - 1))
                    mm.then_inc(fa.filled, 1)

            banks_free("prep2b")
            f = pl["prep2b"]["A"]
            pe.wait_ge(ld["w12"], 16)
            for k in range(8):
                c, q = k // 4, k % 4
                turn(f, 0, ("w12", k), [(P, j * P, raw_w12[:, (4 * q + j) * D + c * P:(4 * q + j) * D + (c + 1) * P])
                                        for j in range(4)], ident)
            pe.wait_ge(ld["w3"], 16 * 4)
            for k in range(4):
                turn(f, 0, ("w3", k), [(P, j * P, raw_w3[:, (4 * k + j) * P:(4 * k + j + 1) * P]) for j in range(4)], ident)
            turn(f, 0, ("r",), [(P, c * E, raw_r2[:, c * P:(c + 1) * P]) for c in range(DC)]
                 + [(P, DC * E + c * (E + 1), raw_r3[:, c * P:(c + 1) * P]) for c in range(DC)], ident)

            def logits(f, i, s, wT, n):
                pe.wait_ge(f.drained(("xT", s)), f.read(i, ("xT", s)))
                pe.wait_ge(f.drained(("gate", s)), f.empty(i, ("gate", s)))
                v = f.slot(("gate", s))
                for t in range(T):
                    for c in range(DC):
                        mm = pe.matmul(v[:, t * n:(t + 1) * n], xnT[s][:, c * S + t * P:c * S + (t + 1) * P],
                                       wT[:, c * n:(c + 1) * n], start=(c == 0), stop=(c == DC - 1))
                mm.then_inc(f.filled, 1)

            def shared_up(f, i, s, j, rows, gate_at, up_at, w_g, w_u, width):
                pe.wait_ge(f.drained(("sh", s, j)), f.empty(i, ("sh", s, j)))
                v = f.slot(("sh", s, j))
                for half, wT, at in ((0, w_g, gate_at), (1, w_u, up_at)):
                    for c in range(DC):
                        mm = pe.matmul(v[0:rows, half * S:(half + 1) * S], wT[:, c * width + at:c * width + at + rows],
                                       xnT[s][:, c * S:(c + 1) * S], start=(c == 0), stop=(c == DC - 1))
                mm.then_inc(f.filled, 1)

            banks_free("l2f")
            fa, fb = pl["l2f"]["A"], pl["l2f"]["B"]
            with pe.Fori(0, TURNS) as i:
                for s in range(2):
                    pe.wait_ge(xn_ready["l2f"].sem, xn_ready["l2f"].count(2 * i + s))
                    turn_x(fa, i, s, ("xT", s), xn[s])
                for s in range(2):
                    logits(fa, i, s, r2T, E)
                def turn_hidden(s):
                    for t in range(T):
                        pe.wait_ge(fb.drained(("ro", s, t, E // 2 - 1)), fb.read(i, ("ro", s, t, E // 2 - 1)))
                        for k in range(2):
                            turn(fa, i, ("hrT", s, t, k), [(P, j * P, hr2[t][:, (4 * k + j) * P:(4 * k + j + 1) * P])
                                                           for j in range(4)], ident)

                for s in range(2):
                    for j in range(HC):
                        shared_up(fb, i, s, j, P, j * P, j * P, sw1T, sw2T, H_FFN)
                    if s == 1:
                        turn_hidden(0)
                    for t in range(T):
                        for k in range(E // 2):
                            pe.wait_ge(fb.drained(("ro", s, t, k)), fb.empty(i, ("ro", s, t, k)))
                            v = fb.slot(("ro", s, t, k))
                            for c in range(DC):
                                at = c * E * 2 * H_R2 + k * BANK
                                mm = pe.matmul(v, xnT[s][:, c * S + t * P:c * S + (t + 1) * P], w12T[:, at:at + BANK],
                                               start=(c == 0), stop=(c == DC - 1))
                            mm.then_inc(fb.filled, 1)
                for s in range(2):
                    if s == 1:
                        turn_hidden(1)
                    pe.wait_ge(fa.drained(("dn", s)), fa.empty(i, ("dn", s)))
                    v = fa.slot(("dn", s))
                    pe.wait_ge(fb.drained(("sh", s, HC - 1)), fb.read(i, ("sh", s, HC - 1)))
                    pe.wait_ge(fa.drained(("hrT", s, 1, 0)), fa.read(i, ("hrT", s, 1, 0)))
                    pe.wait_ge(fa.drained(("hrT", s, 1, 1)), fa.read(i, ("hrT", s, 1, 1)))
                    for t in range(T):
                        o = v[:, t * D:(t + 1) * D]
                        for j in range(HC):
                            pe.matmul(o, hsT2[s][:, j * S + t * P:j * S + (t + 1) * P], sw3T[:, j * D:(j + 1) * D],
                                      start=(j == 0), stop=False)
                        for e in range(E):
                            mm = pe.matmul(o, hrT2[s][:, (t * E + e) * P:(t * E + e + 1) * P], w3T[:, e * D:(e + 1) * D],
                                           start=False, stop=(e == E - 1))
                    mm.then_inc(fa.filled, 1)

            banks_free("l3x")
            fa, fb = pl["l3x"]["A"], pl["l3x"]["B"]

            def max3(i, s, k):
                pe.wait_ge(fa.drained(("max", s, k)), fa.empty(i, ("max", s, k)))
                v = fa.slot(("max", s, k))
                t, j, r = k // 16, k % 16 // 2, 64 * (k % 2)
                for a in range(2):
                    hh = 2 * j + a
                    mm = pe.matmul(v[:, a * S:(a + 1) * S], qT3[s][r:r + K3, hh * S + t * P:hh * S + (t + 1) * P],
                                   kT3[s][r:r + K3, j * S:(j + 1) * S], start=True, stop=True)
                mm.then_inc(fa.filled, 1)

            def exp3(i, s, m):
                pe.wait_ge(fb.drained(("sc", s, m)), fb.empty(i, ("sc", s, m)))
                v = fb.slot(("sc", s, m))
                j, r = m // 2, 64 * (m % 2)
                for u in range(T):
                    mm = pe.matmul(v[:, u * BANK:(u + 1) * BANK], kT3[s][r:r + K3 + 2, j * S + u * P:j * S + (u + 1) * P],
                                   qT3[s][r:r + K3 + 2, 2 * j * S:(2 * j + 2) * S], start=True, stop=True)
                mm.then_inc(fb.filled, 1)

            def values3(s, m):
                pv, p = pl["l3x"]["V"].slot(("pv", s)), pexp3[m % 2]
                j, par = m // 2, m % 2
                for u in range(T):
                    mm = pe.matmul(pv[0:M3, par * BANK:(par + 1) * BANK],
                                   vpad3[s][:, (u * KV3 + j) * M3:(u * KV3 + j + 1) * M3], p[:, u * BANK:(u + 1) * BANK],
                                   start=(j == 0 and u == 0), stop=(j == KV3 - 1 and u == T - 1))
                return mm

            def token_blocks3(s, t):
                return [(P, (2 * a + par) * M3, oT13[s][0:M3, par * BANK + a * S + t * P:par * BANK + a * S + (t + 1) * P])
                        for a in range(2) for par in range(2)]

            pe.wait_ge(pads_ready, 1)
            with pe.Fori(0, TURNS) as i:
                for s in range(2):
                    pe.wait_ge(qparts_ready["l3x"].sem, qparts_ready["l3x"].count(2 * i + s))
                    for k in range(4):
                        turn(fa, i, ("qsT", s, k), [(P, j * S + t * P, qs3[s][:, (t * 16 + 4 * k + j) * P:(t * 16 + 4 * k + j + 1) * P])
                                                    for j in range(4) for t in range(T)], identb, BF16)
                    pe.wait_ge(kparts_ready["l3x"].sem, kparts_ready["l3x"].count(2 * i + s))
                    for k in range(2):
                        turn(fa, i, ("ksT", s, k), [(P, j * S + t * P, ks3[s][:, (t * KV3 + 4 * k + j) * P:(t * KV3 + 4 * k + j + 1) * P])
                                                    for j in range(4) for t in range(T)], identb, BF16)
                for s in range(2):
                    pe.wait_ge(fa.drained(("ksT", s, 0)), fa.read(i, ("ksT", s, 0)))
                    pe.wait_ge(fa.drained(("ksT", s, 1)), fa.read(i, ("ksT", s, 1)))
                attention("l3x", i, max3, 32, 2 * NH3, sh3, exp3, values3, NH3 // 2, token_blocks3)

            banks_free("l3f")
            fa, fb = pl["l3f"]["A"], pl["l3f"]["B"]
            pe.wait_ge(ld["l3"], 16 * 6)
            with pe.Fori(0, TURNS) as i:
                for s in range(2):
                    pe.wait_ge(xn_ready["l3f"].sem, xn_ready["l3f"].count(2 * i + s))
                    turn_x(fa, i, s, ("xT", s), xn[s])
                for s in range(2):
                    logits(fa, i, s, r3T, E + 1)
                def turn_hidden(s):
                    for t in range(T):
                        pe.wait_ge(fb.drained(("ro", s, t, E - 1)), fb.read(i, ("ro", s, t, E - 1)))
                        for k in range(3):
                            turn(fa, i, ("hrT", s, t, k), [(P, (j - 4 * k) * P, hr3[t][:, j * P:(j + 1) * P])
                                                           for j in range(4 * k, min(4 * k + 4, RC3))], ident)

                for s in range(2):
                    for j in range(SC3):
                        shared_up(fb, i, s, j, min(P, H_S3 - j * P), j * P, H_S3 + j * P, ws_gu, ws_gu, 2 * H_S3)
                    if s == 1:
                        turn_hidden(0)
                    for t in range(T):
                        for e in range(E):
                            pe.wait_ge(fb.drained(("ro", s, t, e)), fb.empty(i, ("ro", s, t, e)))
                            v = fb.slot(("ro", s, t, e))
                            for c in range(DC):
                                at = (c * E + e) * 2 * H_R3
                                mm = pe.matmul(v[:, 0:2 * H_R3], xnT[s][:, c * S + t * P:c * S + (t + 1) * P],
                                               we_gu[:, at:at + 2 * H_R3], start=(c == 0), stop=(c == DC - 1))
                            mm.then_inc(fb.filled, 1)
                for s in range(2):
                    if s == 1:
                        turn_hidden(1)
                    pe.wait_ge(fa.drained(("dnS", s)), fa.empty(i, ("dnS", s)))
                    v = fa.slot(("dnS", s))
                    pe.wait_ge(fb.drained(("sh", s, SC3 - 1)), fb.read(i, ("sh", s, SC3 - 1)))
                    for t in range(T):
                        for j in range(SC3):
                            r = min(P, H_S3 - j * P)
                            mm = pe.matmul(v[:, t * D:(t + 1) * D], hsT3[s][0:r, j * S + t * P:j * S + (t + 1) * P],
                                           ws_dn[0:r, j * D:(j + 1) * D], start=(j == 0), stop=(j == SC3 - 1))
                    mm.then_inc(fa.filled, 1)
                    pe.wait_ge(fa.drained(("dnR", s)), fa.empty(i, ("dnR", s)))
                    v = fa.slot(("dnR", s))
                    pe.wait_ge(fa.drained(("hrT", s, 1, 1)), fa.read(i, ("hrT", s, 1, 1)))
                    pe.wait_ge(fa.drained(("hrT", s, 1, 2)), fa.read(i, ("hrT", s, 1, 2)))
                    for t in range(T):
                        for j in range(RC3):
                            mm = pe.matmul(v[:, t * D:(t + 1) * D], hrT3[s][:, (t * RC3 + j) * P:(t * RC3 + j + 1) * P],
                                           we_dn[:, j * D:(j + 1) * D], start=(j == 0), stop=(j == RC3 - 1))
                    mm.then_inc(fa.filled, 1)

        @block.scalar
        def _(act):
            def first_rstd(layer, n, s, eps, scale=1.0):
                act.wait_ge(stats_ready[layer].sem, stats_ready[layer].count(n))
                act.activation(lnv[s], mv[s][:, :, 1], ACT.Ln, bias=eps, scale=scale)
                act.drain()
                act.activation(y0[s], lnv[s], ACT.Exp, scale=-0.5).then_inc(rstd_ready[layer].sem, 1)

            def move(f, i, key, dst, view, scale=1.0):
                act.wait_ge(f.filled, f.full(i, key))
                v = f.slot(key)
                act.activation(dst, view(v), ACT.Copy, scale=scale).then_inc(f.drained(key), 1)

            def whole(v):
                return v

            act.wait_ge(ld["cols"], 16 * 14)
            act.activation(gt, graw, ACT.Tanh).then_inc(tanh_ready, 1)
            act.activation(gam_s, gam, ACT.Tanh, scale=0.5).then_inc(egam_ready, 1)
            move(pl["prep0"]["A"], 0, ("w64",), wT64, lambda v: v[0:C, 0:3 * C])
            act.wait_ge(const_ready, 1)

            f = pl["l0x"]["A"]
            with act.Fori(0, TURNS) as i:
                for s in range(2):
                    first_rstd("l0x", 2 * i + s, s, eps5)
                for s in range(2):
                    move(f, i, ("xT", s), xnT[s], whole)
                for s in range(2):
                    move(f, i, ("cT", s), ctxT[s], lambda v: v[0:C, 0:S])
                for s in range(2):
                    move(f, i, ("oT", s), oT0[s], lambda v: v[0:C, 0:S])
                for s in range(2):
                    first_rstd("l0s", 2 * i + s, s, eps6, 1.0 / S)
                for s in range(2):
                    act.wait_ge(l0_z_ready.sem, l0_z_ready.count(2 * i + s))
                    for t in range(T):
                        last = act.activation(e0[s][:, t * S:(t + 1) * S], z0[s][:, t * S:(t + 1) * S], ACT.Exp,
                                              bias=c1[s][:, t:t + 1], accum_out=c2[s][:, t:t + 1])
                    last.then_inc(l0_e_ready.sem, 1)

            act.wait_ge(ld["l1f"], 16 * 3)
            for w in range(3):
                last = act.activation(tern[w], raw_f1[w], ACT.Abs, accum_out=wsum[:, w:w + 1])
            last.then_inc(wsum_ready, 1)

            fa, fb, fc = (pl["l0f"][g] for g in "ABC")
            with act.Fori(0, TURNS) as i:
                for s in range(2):
                    first_rstd("l0f", 2 * i + s, s, eps5)
                for s in range(2):
                    move(fa, i, ("xT", s), xnT[s], whole)
                for s in range(2):
                    move(fc, i, ("cT", s), ctxT[s], lambda v: v[0:C, 0:S])
                for s in range(2):
                    move(fc, i, ("qk", s), qkT[s], lambda v: v[0:C, :])
                for s in range(2):
                    act.wait_ge(fc.filled, fc.full(i, ("sim", s)))
                    v = fc.slot(("sim", s))
                    act.activation(sim[s], v, ACT.Copy, scale=1.0 / 16)
                    act.activation(th[s], v, ACT.Tanh, scale=1.0 / 32).then_inc(fc.drained(("sim", s)), 1)
                for s in range(2):
                    n = 2 * i + s
                    act.wait_ge(l0_pick_ready.sem, l0_pick_ready.count(n))
                    for t in range(T):
                        act.wait_ge(rexp_free.sem, rexp_free.free(n, t))
                        for k in range(E // 2):
                            act.wait_ge(fb.filled, fb.full(i, ("ex", s, t, k)))
                            v = fb.slot(("ex", s, t, k))
                            for a in range(2):
                                e = 2 * k + a
                                last = act.activation(rexp[t][:, e * D:(e + 1) * D], v[:, a * D:(a + 1) * D], ACT.Relu,
                                                      scale=pick[s][:, t, e:e + 1])
                            last.then_inc(fb.drained(("ex", s, t, k)), 1)

            f = pl["prep1"]["A"]
            move(f, 0, ("wq",), wq1T, whole)
            move(f, 0, ("wkv",), wkv1T, lambda v: v[0:C, :])
            move(f, 0, ("wout",), wout1T, whole)

            def first_parts(places, src, hd, at, n):
                step = 1 if n < 3 else 2
                heads = src.rearrange("p (h k) -> p h k", k=hd)
                dst = places[:, :, at * hd:(at + n * step) * hd].rearrange("p h (a k) -> p h a k", a=n)[:, :, :, 0:hd]
                return act.activation(dst, heads.unsqueeze(2).broadcast_to([P, heads.shape[1], n, hd]), ACT.Copy)

            def turned_queries(layer, i, s, rows, qT):
                f = pl[layer]["A"]
                for k in range(4):
                    move(f, i, ("qsT", s, k), qT[s][0:rows, k * 1024:(k + 1) * 1024], lambda v: v[0:rows, :].bitcast(BF16))

            fa, fb = pl["l1x"]["A"], pl["l1x"]["B"]
            with act.Fori(0, TURNS) as i:
                for s in range(2):
                    first_rstd("l1x", 2 * i + s, s, eps5)
                for s in range(2):
                    move(fa, i, ("xT", s), xnT[s], whole)
                for s in range(2):
                    move(fa, i, ("cT", s), ctxT[s], lambda v: v[0:C, 0:S])
                for s in range(2):
                    qv = qs1[s].rearrange("p (h k) -> p h k", k=K1)
                    kv = ks1[s].rearrange("p (t h k) -> p t h k", t=T, k=K1 + 2)
                    act.wait_ge(fb.filled, fb.full(i, ("q", s)))
                    v = fb.slot(("q", s))[:, 0:W]
                    first_parts(qv, v, HD1, 0, 2)
                    first_parts(qv, v, HD1, 5, 1).then_inc(q1_ready["l1x"].sem, 1)
                    act.wait_ge(fb.filled, fb.full(i, ("kv", s)))
                    v = fb.slot(("kv", s))
                    for t in range(T):
                        last = first_parts(kv[:, t], v[:, t * BANK:t * BANK + D], HD1, 0, 3)
                    last.then_inc(k1_ready["l1x"].sem, 1)
                for s in range(2):
                    turned_queries("l1x", i, s, K1, qT1)
                for s in range(2):
                    for m in range(NH1 // 2):
                        act.wait_ge(fb.filled, fb.full(i, ("sc", s, m)))
                        v = fb.slot(("sc", s, m))
                        act.wait_ge(pv_done["l1x"].sem, pv_done["l1x"].free(2 * i + s, m))
                        act.activation(q3d(pexp1[m % 2], 2, S + P), q3d(v, 2, BANK)[:, :, 0:S + P], ACT.Exp,
                                       scale=HD1 ** -0.5).then_inc(fb.drained(("sc", s, m)), 1)
                for s in range(2):
                    move(fa, i, ("oT", s), xnT[s], whole)

            f = pl["prep1b"]["A"]
            for w, dst in ((0, wgT), (1, wuT), (2, wdT)):
                for k in range(2):
                    move(f, 0, ("tern", w, k), dst[:, k * H_FFN:(k + 1) * H_FFN], lambda v: v.bitcast(BF16))
            f = pl["prep2a"]["A"]
            for w, dst in ((0, sw1T), (1, sw2T), (2, sw3T)):
                for k in range(0, 4, 2):
                    move(f, 0, ("sw", w, k), dst[:, k * BANK:(k + 1) * BANK], whole)

            fa, fb, fc = (pl["l1f"][g] for g in "ABC")
            with act.Fori(0, TURNS) as i:
                for s in range(2):
                    first_rstd("l1f", 2 * i + s, s, eps5)
                for s in range(2):
                    move(fa, i, ("xT", s), xqT[s], lambda v: v.bitcast(BF16)[:, 0:W])
                for s in range(2):
                    for t in range(T):
                        for h in range(2):
                            act.wait_ge(fb.filled, fb.full(i, ("g", s, t, h)))
                            v = fb.slot(("g", s, t, h))
                            act.activation(sg1[2 * t + h], v, ACT.Silu, scale=c3[s][:, t:t + 1])\
                               .then_inc(fb.drained(("g", s, t, h)), 1)
                for s in range(2):
                    for t in range(T):
                        for h in range(2):
                            at = t * H_FFN + h * BANK
                            move(fc, i, ("hT", s, t, h), hb[s][:, at:at + BANK], whole)
                for s in range(2):
                    for t in range(T):
                        for h in range(2):
                            at = t * H_FFN + h * BANK
                            move(fc, i, ("had", s, t, h), ha[s][:, at:at + BANK], whole, H_FFN ** -0.5)
                for s in range(2):
                    for t in range(T):
                        move(fa, i, ("yT", s, t), yqT[s][:, t * H_FFN:(t + 1) * H_FFN], lambda v: v.bitcast(BF16))

            f = pl["prep2b"]["A"]
            for k in range(0, 8, 2):
                move(f, 0, ("w12", k), w12T[:, k * BANK:(k + 1) * BANK], whole)
            for k in range(0, 4, 2):
                move(f, 0, ("w3", k), w3T[:, k * BANK:(k + 1) * BANK], whole)
            move(f, 0, ("r",), rT, lambda v: v[:, 0:DC * (2 * E + 1)])

            fa, fb = pl["l2f"]["A"], pl["l2f"]["B"]
            with act.Fori(0, TURNS) as i:
                for s in range(2):
                    first_rstd("l2x", 2 * i + s, s, eps5)
                for s in range(2):
                    first_rstd("l2f", 2 * i + s, s, eps5)
                for s in range(2):
                    move(fa, i, ("xT", s), xnT[s], whole)
                for s in range(2):
                    act.wait_ge(fa.filled, fa.full(i, ("gate", s)))
                    v = fa.slot(("gate", s))
                    act.activation(lg[s], q3d(v[:, 0:T * E], T, E), ACT.Exp, scale=-1.0).then_inc(fa.drained(("gate", s)), 1)
                def move_hidden(s):
                    for t in range(T):
                        for k in range(2):
                            at = (t * E + 4 * k) * P
                            move(fa, i, ("hrT", s, t, k), hrT2[s][:, at:at + 4 * P], whole)

                for s in range(2):
                    for j in range(HC):
                        act.wait_ge(fb.filled, fb.full(i, ("sh", s, j)))
                        v = fb.slot(("sh", s, j))
                        act.activation(sg2[fb.index[("sh", s, j)] % 4], v[:, 0:S], ACT.Silu).then_inc(sg2_ready.sem, 1)
                    if s == 1:
                        move_hidden(0)
                    for t in range(T):
                        for k in range(E // 2):
                            act.wait_ge(fb.filled, fb.full(i, ("ro", s, t, k)))
                            v = fb.slot(("ro", s, t, k))
                            act.activation(q3d(sg2[fb.index[("ro", s, t, k)] % 4], 2, H_R2),
                                           q3d(v, 2, 2 * H_R2)[:, :, 0:H_R2], ACT.Silu).then_inc(sg2_ready.sem, 1)
                move_hidden(1)

            fa, fb = pl["l3x"]["A"], pl["l3x"]["B"]
            with act.Fori(0, TURNS) as i:
                for s in range(2):
                    first_rstd("l3x", 2 * i + s, s, eps5)
                for s in range(2):
                    qv = qs3[s].rearrange("p (h k) -> p h k", k=64)
                    kv = ks3[s].rearrange("p (h u k) -> p h u k", u=2, k=64)
                    act.wait_ge(xn_ready["l3x"].sem, xn_ready["l3x"].count(2 * i + s))
                    first_parts(qv, xn[s], HD3, 0, 2)
                    first_parts(qv, xn[s], HD3, 5, 1).then_inc(q1_ready["l3x"].sem, 1)
                    for u in range(2):
                        last = first_parts(kv[:, :, u], cx[s], HD3, 0, 3)
                    last.then_inc(k1_ready["l3x"].sem, 1)
                for s in range(2):
                    turned_queries("l3x", i, s, P, qT3)
                for s in range(2):
                    for m in range(NH3 // 2):
                        act.wait_ge(fb.filled, fb.full(i, ("sc", s, m)))
                        v = fb.slot(("sc", s, m))
                        act.wait_ge(pv_done["l3x"].sem, pv_done["l3x"].free(2 * i + s, m))
                        act.activation(pexp3[m % 2], v, ACT.Exp, scale=HD3 ** -0.5).then_inc(fb.drained(("sc", s, m)), 1)

            fa, fb = pl["l3f"]["A"], pl["l3f"]["B"]
            with act.Fori(0, TURNS) as i:
                for s in range(2):
                    first_rstd("l3f", 2 * i + s, s, eps5)
                for s in range(2):
                    move(fa, i, ("xT", s), xnT[s], whole)
                for s in range(2):
                    act.wait_ge(lg3_ready.sem, lg3_ready.count(2 * i + s))
                    for t in range(T):
                        act.activation(cw[s][:, t, :], lg[s][:, t, :], ACT.Exp, bias=c1[s][:, t:t + 1],
                                       accum_out=c2[s][:, t:t + 1])
                    act.activation(c4[s], c3[s], ACT.Exp, scale=-1.0).then_inc(sc3_ready.sem, 1)
                def move_hidden(s):
                    for t in range(T):
                        for k in range(3):
                            n, at = min(4, RC3 - 4 * k) * P, (t * RC3 + 4 * k) * P
                            move(fa, i, ("hrT", s, t, k), hrT3[s][:, at:at + n], lambda v: v[:, 0:n])

                for s in range(2):
                    for j in range(SC3):
                        act.wait_ge(fb.filled, fb.full(i, ("sh", s, j)))
                        v, r = fb.slot(("sh", s, j)), min(P, H_S3 - j * P)
                        act.activation(sg3[fb.index[("sh", s, j)] % 4][0:r, :], v[0:r, 0:S], ACT.Silu)\
                           .then_inc(sg3_ready.sem, 1)
                    if s == 1:
                        move_hidden(0)
                    for t in range(T):
                        for e in range(E):
                            act.wait_ge(fb.filled, fb.full(i, ("ro", s, t, e)))
                            v = fb.slot(("ro", s, t, e))
                            act.activation(sg3[fb.index[("ro", s, t, e)] % 4][:, 0:H_R3], v[:, 0:H_R3], ACT.Silu)\
                               .then_inc(sg3_ready.sem, 1)
                move_hidden(1)

        @block.vector
        def _(dve):
            def stats(layer, n, s, src):
                for t in range(T):
                    dve.bn_stats(st[s][:, t, :], src(t))
                dve.drain()
                for t in range(T):
                    last = dve.bn_aggr(mv[s][:, t, :], st[s][:, t, :])
                last.then_inc(stats_ready[layer].sem, 1)

            def finish_rstd(layer, n, s, eps, var_scale=1.0, times=1.0):
                dve.wait_ge(rstd_ready[layer].sem, rstd_ready[layer].count(n))
                dve.tensor_tensor(ya[s], y0[s], y0[s], ALU.mult)
                dve.tensor_scalar(yb[s], mv[s][:, :, 1], var_scale, eps, ALU.mult, ALU.add)
                dve.drain()
                dve.tensor_tensor(ya[s], ya[s], yb[s], ALU.mult)
                dve.drain()
                dve.tensor_scalar(ya[s], ya[s], -0.5 * times, 1.5 * times, ALU.mult, ALU.add)
                dve.drain()
                dve.tensor_tensor(rstd[s], ya[s], y0[s], ALU.mult)
                dve.drain()

            def normalised(s, t, dst, src):
                return dve.tensor_scalar(dst[:, t * D:(t + 1) * D], src, mv[s][:, t, 0:1], rstd[s][:, t:t + 1],
                                         ALU.subtract, ALU.mult)

            def x_tile(n):
                return lambda t: xs[:, n, t * D:(t + 1) * D]

            def norm_x(layer, n, s):
                finish_rstd(layer, n, s, EPS)
                for t in range(T):
                    last = normalised(s, t, xn[s], xs[:, n, t * D:(t + 1) * D])
                last.then_inc(xn_ready[layer].sem, 1)

            def take_context(layer, n, s):
                dve.tensor_copy(cx[s], ctx_all[:, n, :]).then_inc(cx_ready[layer].sem, 1)

            def two_largest(s, scores):
                for t in range(T):
                    dve.max(m8[s][:, t, :], scores[:, t, :])
                dve.drain()
                for t in range(T):
                    dve.max_index(idx[s][:, t, :], m8[s][:, t, :], scores[:, t, :])
                dve.drain()
                dve.tensor_copy(idf[s], idx[s][:, :, 0:2])
                dve.drain()
                for t in range(T):
                    dve.tensor_scalar(oh[s][:, t, :], iota8, idf[s][:, t, 0:1], None, ALU.is_equal)
                dve.drain()
                for t in range(T):
                    last = dve.scalar_tensor_tensor(pick[s][:, t, :], iota8, idf[s][:, t, 1:2], oh[s][:, t, :],
                                                    ALU.is_equal, ALU.add)
                return last

            dve.wait_ge(ld["cols"], 16 * 14)
            dve.wait_ge(ld["con"], 16)
            dve.tensor_copy(bias_p[0], bias_f)
            dve.drain()
            dve.tensor_tensor(bias_r, bias_f, bias_p[0], ALU.subtract)
            dve.drain()
            dve.tensor_copy(bias_p[1], bias_r)
            dve.drain()
            dve.tensor_tensor(bias_r, bias_r, bias_p[1], ALU.subtract)
            dve.drain()
            dve.tensor_copy(bias_p[2], bias_r).then_inc(bias_ready, 1)
            dve.wait_ge(tanh_ready, 1)
            dve.wait_ge(egam_ready, 1)
            dve.tensor_scalar(gt0_half, gt[:, 4:5], 0.5, None, ALU.mult)
            dve.tensor_scalar(gam_s, gam_s, 0.5, 0.5, ALU.mult, ALU.add)
            dve.drain()
            dve.tensor_scalar(keep_a, gam_s, gt[:, 2:3], 0.25, ALU.mult, ALU.mult)
            dve.tensor_scalar(keep_x, gam_s, -1.0, 1.0, ALU.mult, ALU.add)
            dve.drain()
            dve.tensor_scalar(keep_x, keep_x, gt[:, 2:3], None, ALU.mult)
            dve.wait_ge(ld["ctx"], 16)
            dve.wait_ge(ld["x"], 16)

            f = pl["l0x"]["A"]
            with dve.Fori(0, TURNS) as i:
                for s in range(2):
                    stats("l0x", 2 * i + s, s, x_tile(2 * i + s))
                    take_context("l0x", 2 * i + s, s)
                for s in range(2):
                    norm_x("l0x", 2 * i + s, s)
                for s in range(2):
                    dve.wait_ge(f.filled, f.full(i, ("kv", s)))
                    v = f.slot(("kv", s))
                    dve.tensor_tensor(q3d(kv0[s], T, C), q3d(v[:, 0:T * C], T, C),
                                      bk_row.unsqueeze(1).broadcast_to([P, T, C]), ALU.add)
                    dve.tensor_scalar(kvT0[s], v[0:C, S:2 * S], bk_col, None, ALU.add).then_inc(f.drained(("kv", s)), 1)
                for s in range(2):
                    dve.wait_ge(f.filled, f.full(i, ("sim", s)))
                    v = f.slot(("sim", s))
                    stats("l0s", 2 * i + s, s, lambda t: v[:, t * S:(t + 1) * S])
                for s in range(2):
                    n, v = 2 * i + s, f.slot(("sim", s))
                    finish_rstd("l0s", n, s, EPS0, 1.0 / S, S ** -0.5)
                    for t in range(T):
                        last = normalised(s, t, z0[s], v[:, t * S:(t + 1) * S])
                    last.then_inc(f.drained(("sim", s)), 1)
                    dve.drain()
                    z = q3d(z0[s], T, S)
                    dve.tensor_tensor(z, z, lng.unsqueeze(1).broadcast_to([P, T, S]), ALU.mult)
                    dve.drain()
                    dve.tensor_tensor(z, z, lnb.unsqueeze(1).broadcast_to([P, T, S]), ALU.add)
                    dve.drain()
                    dve.tensor_reduce(c1[s], z, X, ALU.max, negate=True).then_inc(l0_z_ready.sem, 1)
                for s in range(2):
                    n = 2 * i + s
                    dve.wait_ge(l0_e_ready.sem, l0_e_ready.count(n))
                    dve.reciprocal(c3[s], c2[s])
                    dve.drain()
                    dve.tensor_scalar(c3[s], c3[s], gt[:, 0:1], None, ALU.mult)
                    dve.drain()
                    for t in range(T):
                        xt = xs[:, n, t * D:(t + 1) * D]
                        dve.scalar_tensor_tensor(xt, e0[s][:, t * S:(t + 1) * S], c3[s][:, t:t + 1], xt, ALU.mult, ALU.add)
                dve.drain()

            dve.wait_ge(wsum_ready, 2)
            dve.tensor_scalar(wmean, wmean, 1.0 / (H_FFN * D), EPS, ALU.mult, ALU.max)
            dve.drain()
            dve.reciprocal(wscale, wmean).then_inc(wsum_ready, 1)

            fa, fb, fc = (pl["l0f"][g] for g in "ABC")
            with dve.Fori(0, TURNS) as i:
                for s in range(2):
                    stats("l0f", 2 * i + s, s, x_tile(2 * i + s))
                    take_context("l0f", 2 * i + s, s)
                for s in range(2):
                    norm_x("l0f", 2 * i + s, s)
                for s in range(2):
                    dve.wait_ge(fa.filled, fa.full(i, ("gate", s)))
                    v = fa.slot(("gate", s))
                    dve.tensor_tensor(lg[s], q3d(v[:, 0:T * E], T, E), gate0_b.unsqueeze(1).broadcast_to([P, T, E]),
                                      ALU.add).then_inc(fa.drained(("gate", s)), 1)
                    dve.drain()
                    two_largest(s, lg[s]).then_inc(l0_pick_ready.sem, 1)
                for s in range(2):
                    n = 2 * i + s
                    dve.wait_ge(fc.drained(("sim", s)), fc.read(i, ("sim", s)))
                    dve.tensor_scalar(th[s], th[s], 1.0, None, ALU.add)
                    rounds = -(-TOPK_ROW // 8)
                    for r in range(rounds):
                        cur = sim[s] if r == 0 else work[s]
                        for t in range(T):
                            dve.max(m8[s][:, t, :], cur[:, t * S:(t + 1) * S])
                        dve.drain()
                        if r < rounds - 1:
                            for t in range(T):
                                dve.match_replace(work[s][:, t * S:(t + 1) * S], m8[s][:, t, :],
                                                  cur[:, t * S:(t + 1) * S], -3.0e38)
                            dve.drain()
                    k = (TOPK_ROW - 1) % 8
                    for t in range(T):
                        o = slice(t * S, (t + 1) * S)
                        last = dve.scalar_tensor_tensor(aa[s][:, o], sim[s][:, o], m8[s][:, t, k:k + 1], th[s][:, o],
                                                        ALU.is_ge, ALU.mult)
                    last.then_inc(aa_ready.sem, 1)
                    for t in range(T):
                        dve.wait_ge(fb.drained(("ex", s, t, E // 2 - 1)), fb.read(i, ("ex", s, t, E // 2 - 1)))
                        dve.tensor_reduce(acc0[s][:, t * D:(t + 1) * D], rexp[t].rearrange("p (e d) -> p d e", e=E), X,
                                          ALU.add).then_inc(rexp_free.sem, 1)
                    dve.drain()
                    dve.scalar_tensor_tensor(xs[:, n, :], acc0[s], gt0_half, xs[:, n, :], ALU.mult, ALU.add)
                    dve.wait_ge(fc.filled, fc.full(i, ("AT", s)))
                    v = fc.slot(("AT", s))
                    dve.tensor_tensor(adj[:, n, :], v, aa[s], ALU.add).then_inc(fc.drained(("AT", s)), 1)
                dve.drain()

            def rest_of_parts(hd, src, first, second, third, rest, read):
                last = dve.tensor_tensor(rest, src, first, ALU.subtract)
                if read is not None:
                    last.then_inc(read, 1)
                dve.drain()
                for dst in second:
                    dve.tensor_copy(dst, rest)
                dve.drain()
                return dve.tensor_tensor(third, rest, second[0], ALU.subtract)

            def turned_keys(layer, i, s, n, rows, kT):
                f = pl[layer]["A"]
                for k in range(n):
                    dve.wait_ge(f.filled, f.full(i, ("ksT", s, k)))
                    v = f.slot(("ksT", s, k))
                    dve.tensor_copy(kT[s][0:rows, k * 1024:(k + 1) * 1024], v[0:rows, :].bitcast(BF16))\
                       .then_inc(f.drained(("ksT", s, k)), 1)

            def maxima(layer, i, s, n_max, reduce, nmax, hi, lo, shT):
                f = pl[layer]["A"]
                for k in range(n_max):
                    dst, heads = reduce(k)
                    dve.wait_ge(f.filled, f.full(i, ("max", s, k)))
                    v = f.slot(("max", s, k))
                    dve.tensor_reduce(dst, heads(v), X, ALU.max, negate=True).then_inc(f.drained(("max", s, k)), 1)
                dve.drain()
                for t in range(T):
                    dve.tensor_copy(hi(t), nmax(t))
                dve.drain()
                for t in range(T):
                    last = dve.tensor_tensor(lo(t), nmax(t), hi(t), ALU.subtract)
                last.then_inc(shift_ready[layer].sem, 1)
                dve.wait_ge(f.filled, f.full(i, ("shT", s)))
                v = f.slot(("shT", s))
                dve.tensor_copy(shT, v[0:shT.shape[0], 0:S // 2].bitcast(BF16)).then_inc(f.drained(("shT", s)), 1)

            def sums_of_values(layer, i, s, rows):
                f = pl[layer]["V"]
                dve.wait_ge(pv_done[layer].sem, pv_done[layer].count(2 * i + s))
                dve.tensor_copy(oT13[s][0:rows, :], f.slot(("pv", s))[0:rows, :]).then_inc(f.drained(("pv", s)), 1)

            def weighted(layer, i, s, kv, hd, rec):
                f, g = pl[layer]["A"], D // kv // hd
                for t in range(T):
                    dve.wait_ge(f.filled, f.full(i, ("tok", s, t)))
                    v = f.slot(("tok", s, t))[:, 0:g * kv * (hd + 1)]
                    r = rec[s][:, t * g * kv:(t + 1) * g * kv]
                    dve.reciprocal(r, v.rearrange("p (h k) -> p h k", k=hd + 1)[:, :, hd])
                    dve.drain()
                    dve.tensor_tensor(xn[s][:, t * D:(t + 1) * D].rearrange("p (j g k) -> p g j k", j=kv, g=g),
                                      v.rearrange("p (g j k) -> p g j k", g=g, k=hd + 1)[:, :, :, 0:hd],
                                      q3d(r, g, kv).unsqueeze(3).broadcast_to([P, g, kv, hd]), ALU.mult)\
                       .then_inc(f.drained(("tok", s, t)), 1)

            fa, fb = pl["l1x"]["A"], pl["l1x"]["B"]
            dve.wait_ge(vpad_ready, 1)
            with dve.Fori(0, TURNS) as i:
                for s in range(2):
                    stats("l1x", 2 * i + s, s, x_tile(2 * i + s))
                    take_context("l1x", 2 * i + s, s)
                for s in range(2):
                    norm_x("l1x", 2 * i + s, s)
                for s in range(2):
                    n = 2 * i + s
                    def place(stack, pitch, a):
                        return stack[s].rearrange("p (t h k) -> p t h k", t=T, k=pitch)[:, :, :, a * HD1:(a + 1) * HD1]

                    rest = rest1[s].rearrange("p (t h k) -> p t h k", t=T, k=HD1)
                    dve.wait_ge(q1_ready["l1x"].sem, q1_ready["l1x"].count(n))
                    vq = fb.slot(("q", s))[:, 0:W].rearrange("p (t h k) -> p t h k", t=T, k=HD1)
                    rest_of_parts(HD1, vq, place(qs1, K1, 0), [place(qs1, K1, a) for a in (2, 3)], place(qs1, K1, 4), rest,
                                  fb.drained(("q", s))).then_inc(qparts_ready["l1x"].sem, 1)
                    dve.wait_ge(k1_ready["l1x"].sem, k1_ready["l1x"].count(n))
                    own_instruction(dve)
                    dve.drain()
                    vkv = q3d(fb.slot(("kv", s)), T, BANK)
                    rest_of_parts(HD1, vkv[:, :, 0:D].rearrange("p t (h k) -> p t h k", k=HD1), place(ks1, K1 + 2, 0),
                                  [place(ks1, K1 + 2, a) for a in (1, 3)], place(ks1, K1 + 2, 5), rest, None)\
                        .then_inc(kparts_ready["l1x"].sem, 1)
                    vd = vpad1[s].rearrange("p (t g x) -> p t g x", t=T, x=G1 * M1)
                    vv = vkv[:, :, D:2 * D].rearrange("p t (g l k) -> p t g l k", l=G1, k=HD1)
                    for l in range(G1):
                        at = l * (M1 + HD1 + 1)
                        last = dve.tensor_copy(vd[:, :, :, at:at + HD1], vv[:, :, :, l])
                    last.then_inc(fb.drained(("kv", s)), 1)
                for s in range(2):
                    turned_keys("l1x", i, s, 4, K1 + 2, kT1)
                for s in range(2):
                    def reduce1(k):
                        nm = q3d(nmax1[s], T, NH1)
                        if k < 4:
                            return nm[:, 0, 4 * k:4 * k + 4], lambda v: q3d(v, 4, P)
                        return nm[:, 1, 2 * k - 8:2 * k - 6], lambda v: q3d(v, 2, S)

                    sh = sh1[s].rearrange("p (t r h) -> p t r h", t=T, r=2)
                    maxima("l1x", i, s, 12, reduce1, lambda t: q3d(nmax1[s], T, NH1)[:, t], lambda t: sh[:, t, 0],
                           lambda t: sh[:, t, 1], shT1[s])
                for s in range(2):
                    sums_of_values("l1x", i, s, M1)
                    weighted("l1x", i, s, NH1, HD1, rec1)
                for s in range(2):
                    dve.wait_ge(fa.filled, fa.full(i, ("out", s)))
                    n, v = 2 * i + s, fa.slot(("out", s))
                    dve.scalar_tensor_tensor(xs[:, n, :], v, gt[:, 1:2], xs[:, n, :], ALU.mult, ALU.add)\
                       .then_inc(fa.drained(("out", s)), 1)
                dve.drain()

            f = pl["prep2a"]["A"]
            for w, dst in ((0, sw1T), (1, sw2T), (2, sw3T)):
                for k in range(1, 4, 2):
                    dve.wait_ge(f.filled, f.full(0, ("sw", w, k)))
                    v = f.slot(("sw", w, k))
                    dve.tensor_copy(dst[:, k * BANK:(k + 1) * BANK], v).then_inc(f.drained(("sw", w, k)), 1)

            fa, fb, fc = (pl["l1f"][g] for g in "ABC")
            with dve.Fori(0, TURNS) as i:
                for s in range(2):
                    stats("l1f", 2 * i + s, s, x_tile(2 * i + s))
                for s in range(2):
                    n = 2 * i + s
                    norm_x("l1f", n, s)
                    dve.drain()
                    dve.tensor_reduce(c1[s], q3d(xn[s], T, D), X, ALU.max, apply_absolute_value=True)
                    dve.drain()
                    dve.tensor_scalar(c1[s], c1[s], EPS, None, ALU.max)
                    dve.drain()
                    dve.reciprocal(c2[s], c1[s])
                    dve.tensor_scalar(c3[s], c1[s], wmean[:, 0:1], 1.0 / QB, ALU.mult, ALU.mult)
                    dve.tensor_scalar(c4[s], c1[s], wmean[:, 1:2], 1.0 / QB, ALU.mult, ALU.mult)
                    dve.drain()
                    dve.tensor_scalar(c2[s], c2[s], QB, None, ALU.mult)
                    dve.drain()
                    for t in range(T):
                        o = xn[s][:, t * D:(t + 1) * D]
                        dve.tensor_scalar(o, o, c2[s][:, t:t + 1], ROUND, ALU.mult, ALU.add)
                    dve.drain()
                    dve.tensor_scalar(xq[s], xn[s], ROUND, QB - 1, ALU.subtract, ALU.min).then_inc(xq_ready.sem, 1)
                for s in range(2):
                    for t in range(T):
                        for h in range(2):
                            dve.wait_ge(fb.filled, fb.full(i, ("u", s, t, h)))
                            at, v = t * H_FFN + h * BANK, fb.slot(("u", s, t, h))
                            dve.wait_ge(fb.drained(("g", s, t, h)), fb.read(i, ("g", s, t, h)))
                            dve.scalar_tensor_tensor(ha[s][:, at:at + BANK], v, c4[s][:, t:t + 1], sg1[2 * t + h],
                                                     ALU.mult, ALU.mult).then_inc(fb.drained(("u", s, t, h)), 1)
                for s in range(2):
                    for t in range(T):
                        for h in range(2):
                            dve.wait_ge(fc.drained(("had", s, t, h)), fc.read(i, ("had", s, t, h)))
                        y, z = ha[s][:, t * H_FFN:(t + 1) * H_FFN], bfly
                        for src, dst, width in ((y, z, 4 * P), (z, y, 2 * P), (y, z, P)):
                            a = src.rearrange("p (n two w) -> p n two w", two=2, w=width)
                            b = dst.rearrange("p (n two w) -> p n two w", two=2, w=width)
                            dve.tensor_tensor(b[:, :, 0], a[:, :, 0], a[:, :, 1], ALU.add)
                            dve.tensor_tensor(b[:, :, 1], a[:, :, 0], a[:, :, 1], ALU.subtract)
                            dve.drain()
                        k = slice(t, t + 1)
                        dve.tensor_reduce(c1[s][:, k], z, X, ALU.max, apply_absolute_value=True)
                        dve.drain()
                        dve.tensor_scalar(c1[s][:, k], c1[s][:, k], EPS, None, ALU.max)
                        dve.drain()
                        dve.reciprocal(c2[s][:, k], c1[s][:, k])
                        dve.tensor_scalar(c3[s][:, k], c1[s][:, k], wmean[:, 2:3], 1.0 / QB, ALU.mult, ALU.mult)
                        dve.drain()
                        dve.tensor_scalar(c2[s][:, k], c2[s][:, k], QB, None, ALU.mult)
                        dve.tensor_scalar(c3[s][:, k], c3[s][:, k], gt[:, 5:6], None, ALU.mult)
                        dve.drain()
                        dve.tensor_scalar(y, z, c2[s][:, k], ROUND, ALU.mult, ALU.add)
                        dve.drain()
                        dve.tensor_scalar(yqb[s][:, t * H_FFN:(t + 1) * H_FFN], y, ROUND, QB - 1, ALU.subtract, ALU.min)\
                           .then_inc(yq_ready.sem, 1)
                for s in range(2):
                    dve.wait_ge(fa.filled, fa.full(i, ("dn", s)))
                    n, v = 2 * i + s, fa.slot(("dn", s))
                    for t in range(T):
                        xt = xs[:, n, t * D:(t + 1) * D]
                        last = dve.scalar_tensor_tensor(xt, v[:, t * D:(t + 1) * D], c3[s][:, t:t + 1], xt, ALU.mult, ALU.add)
                    last.then_inc(fa.drained(("dn", s)), 1)
                dve.drain()

            f = pl["prep2b"]["A"]
            for name, m, dst in (("w12", 8, w12T), ("w3", 4, w3T)):
                for k in range(1, m, 2):
                    dve.wait_ge(f.filled, f.full(0, (name, k)))
                    v = f.slot((name, k))
                    dve.tensor_copy(dst[:, k * BANK:(k + 1) * BANK], v).then_inc(f.drained((name, k)), 1)

            fa, fb = pl["l2f"]["A"], pl["l2f"]["B"]
            with dve.Fori(0, TURNS) as i:
                for s in range(2):
                    stats("l2x", 2 * i + s, s, x_tile(2 * i + s))
                for s in range(2):
                    n = 2 * i + s
                    norm_x("l2x", n, s)
                    dve.drain()
                    dve.scalar_tensor_tensor(xs[:, n, :], xn[s], keep_x, xs[:, n, :], ALU.mult, ALU.add)
                    dve.drain()
                    dve.scalar_tensor_tensor(xs[:, n, :], adj[:, n, :], keep_a, xs[:, n, :], ALU.mult, ALU.add)
                    dve.drain()
                    stats("l2f", n, s, x_tile(n))
                for s in range(2):
                    norm_x("l2f", 2 * i + s, s)
                for s in range(2):
                    dve.wait_ge(fa.drained(("gate", s)), fa.read(i, ("gate", s)))
                    dve.tensor_scalar(cw[s], lg[s], 1.0, None, ALU.add)
                    dve.drain()
                    dve.reciprocal(cw[s], cw[s])
                    dve.drain()
                    dve.tensor_tensor(lg[s], cw[s], ebias.unsqueeze(1).broadcast_to([P, T, E]), ALU.add)
                    dve.drain()
                    two_largest(s, lg[s])
                    dve.drain()
                    dve.tensor_tensor(cw[s], cw[s], pick[s], ALU.mult)
                    dve.drain()
                    dve.tensor_reduce(c1[s], cw[s], X, ALU.add)
                    dve.drain()
                    dve.tensor_scalar(c1[s], c1[s], 1e-9, None, ALU.add)
                    dve.drain()
                    dve.reciprocal(c2[s], c1[s])
                    dve.drain()
                    for t in range(T):
                        dve.tensor_scalar(cw[s][:, t, :], cw[s][:, t, :], c2[s][:, t:t + 1], None, ALU.mult)
                    dve.drain()
                for s in range(2):
                    n = 2 * i + s
                    for j in range(HC):
                        dve.wait_ge(fb.filled, fb.full(i, ("sh", s, j)))
                        v = fb.slot(("sh", s, j))
                        dve.wait_ge(sg2_ready.sem, sg2_ready.count(n, j + 1))
                        dve.tensor_tensor(hsT2[s][:, j * S:(j + 1) * S], v[:, S:2 * S], sg2[fb.index[("sh", s, j)] % 4],
                                          ALU.mult).then_inc(fb.drained(("sh", s, j)), 1)
                    for t in range(T):
                        if s == 1:
                            dve.wait_ge(fa.filled, fa.full(i, ("hrT", 0, t, 1)))
                        for k in range(E // 2):
                            dve.wait_ge(fb.filled, fb.full(i, ("ro", s, t, k)))
                            v, sg = fb.slot(("ro", s, t, k)), sg2[fb.index[("ro", s, t, k)] % 4]
                            dve.wait_ge(sg2_ready.sem, sg2_ready.count(n, HC + t * E // 2 + k + 1))
                            for a in range(2):
                                e = 2 * k + a
                                last = dve.scalar_tensor_tensor(hr2[t][:, e * H_R2:(e + 1) * H_R2],
                                                                v[:, (2 * a + 1) * H_R2:(2 * a + 2) * H_R2], cw[s][:, t, e:e + 1],
                                                                sg[:, a * H_R2:(a + 1) * H_R2], ALU.mult, ALU.mult)
                            last.then_inc(fb.drained(("ro", s, t, k)), 1)
                for s in range(2):
                    dve.wait_ge(fa.filled, fa.full(i, ("dn", s)))
                    n, v = 2 * i + s, fa.slot(("dn", s))
                    dve.scalar_tensor_tensor(xs[:, n, :], v, gt[:, 6:7], xs[:, n, :], ALU.mult, ALU.add)\
                       .then_inc(fa.drained(("dn", s)), 1)
                dve.drain()

            with dve.Fori(0, TURNS) as i:
                for s in range(2):
                    stats("l3x", 2 * i + s, s, x_tile(2 * i + s))
                    take_context("l3x", 2 * i + s, s)
                for s in range(2):
                    norm_x("l3x", 2 * i + s, s)
                    dve.drain()
                for s in range(2):
                    n = 2 * i + s
                    qv = qs3[s].rearrange("p (h k) -> p h k", k=64)
                    kv = ks3[s].rearrange("p (h u k) -> p h u k", u=2, k=64)

                    def place(v, a):
                        return v[:, :, a * HD3:(a + 1) * HD3]

                    dve.wait_ge(q1_ready["l3x"].sem, q1_ready["l3x"].count(n))
                    rest_of_parts(HD3, xn[s].rearrange("p (h k) -> p h k", k=HD3), place(qv, 0),
                                  [place(qv, a) for a in (2, 3)], place(qv, 4), rest3[s].rearrange("p (h k) -> p h k", k=HD3),
                                  None).then_inc(qparts_ready["l3x"].sem, 1)
                    dve.wait_ge(k1_ready["l3x"].sem, k1_ready["l3x"].count(n))
                    own_instruction(dve)
                    dve.drain()
                    rest = rest3[s][:, 0:T * C].rearrange("p (h k) -> p h k", k=HD3)
                    rest_of_parts(HD3, cx[s].rearrange("p (h k) -> p h k", k=HD3), place(kv[:, :, 0], 0),
                                  [place(kv[:, :, u], a) for u in range(2) for a in (1, 3)], place(kv[:, :, 0], 5), rest, None)
                    dve.tensor_tensor(place(kv[:, :, 1], 5), rest, place(kv[:, :, 0], 1), ALU.subtract)\
                       .then_inc(kparts_ready["l3x"].sem, 1)
                for s in range(2):
                    turned_keys("l3x", i, s, 2, P, kT3)
                for s in range(2):
                    nm = q3d(nmax3[s], T, NH3)
                    sh = sh3[s].rearrange("p (t r u h) -> p t r u h", t=T, r=2, u=2)

                    def reduce3(k):
                        j, par = k % 16 // 2, k % 2
                        return nm[:, k // 16].rearrange("p (j a u) -> p j a u", a=2, u=2)[:, j, :, par], lambda v: q3d(v, 2, S)

                    maxima("l3x", i, s, 32, reduce3, lambda t: nm[:, t].rearrange("p (h u) -> p u h", u=2), lambda t: sh[:, t, 0],
                           lambda t: sh[:, t, 1], shT3[s])
                for s in range(2):
                    n = 2 * i + s
                    sums_of_values("l3x", i, s, M3)
                    weighted("l3x", i, s, KV3, HD3, rec3)
                    dve.drain()
                    dve.scalar_tensor_tensor(xs[:, n, :], xn[s], gt[:, 3:4], xs[:, n, :], ALU.mult, ALU.add)
                dve.drain()

            fa, fb = pl["l3f"]["A"], pl["l3f"]["B"]
            with dve.Fori(0, TURNS) as i:
                for s in range(2):
                    stats("l3f", 2 * i + s, s, x_tile(2 * i + s))
                for s in range(2):
                    norm_x("l3f", 2 * i + s, s)
                for s in range(2):
                    dve.wait_ge(fa.filled, fa.full(i, ("gate", s)))
                    v = fa.slot(("gate", s))
                    v = q3d(v[:, 0:T * (E + 1)], T, E + 1)
                    dve.tensor_copy(c3[s], v[:, :, E])
                    dve.tensor_copy(lg[s], v[:, :, 0:E]).then_inc(fa.drained(("gate", s)), 1)
                    dve.drain()
                    dve.tensor_reduce(c1[s], lg[s], X, ALU.max, negate=True).then_inc(lg3_ready.sem, 1)
                for s in range(2):
                    dve.wait_ge(sc3_ready.sem, sc3_ready.count(2 * i + s))
                    dve.reciprocal(c1[s], c2[s])
                    dve.tensor_scalar(c4[s], c4[s], 1.0, None, ALU.add)
                    dve.drain()
                    dve.reciprocal(c3[s], c4[s])
                    for t in range(T):
                        dve.tensor_scalar(lg[s][:, t, :], cw[s][:, t, :], c1[s][:, t:t + 1], None, ALU.mult)
                    dve.drain()
                    dve.tensor_scalar(c3[s], c3[s], gt[:, 7:8], None, ALU.mult)
                    two_largest(s, lg[s])
                    dve.drain()
                    dve.tensor_tensor(cw[s], lg[s], pick[s], ALU.mult)
                    dve.drain()
                for s in range(2):
                    n = 2 * i + s
                    for j in range(SC3):
                        dve.wait_ge(fb.filled, fb.full(i, ("sh", s, j)))
                        r, v = min(P, H_S3 - j * P), fb.slot(("sh", s, j))
                        dve.wait_ge(sg3_ready.sem, sg3_ready.count(n, j + 1))
                        dve.tensor_tensor(hsT3[s][0:r, j * S:(j + 1) * S], v[0:r, S:2 * S],
                                          sg3[fb.index[("sh", s, j)] % 4][0:r, :], ALU.mult).then_inc(fb.drained(("sh", s, j)), 1)
                    for t in range(T):
                        if s == 1:
                            dve.wait_ge(fa.filled, fa.full(i, ("hrT", 0, t, 2)))
                        for e in range(E):
                            dve.wait_ge(fb.filled, fb.full(i, ("ro", s, t, e)))
                            v, sg = fb.slot(("ro", s, t, e)), sg3[fb.index[("ro", s, t, e)] % 4]
                            dve.wait_ge(sg3_ready.sem, sg3_ready.count(n, SC3 + t * E + e + 1))
                            dve.scalar_tensor_tensor(hr3[t][:, e * H_R3:(e + 1) * H_R3], v[:, H_R3:2 * H_R3],
                                                     cw[s][:, t, e:e + 1], sg[:, 0:H_R3], ALU.mult, ALU.mult)\
                               .then_inc(fb.drained(("ro", s, t, e)), 1)
                for s in range(2):
                    dve.wait_ge(fa.filled, fa.full(i, ("dnS", s)))
                    n, v = 2 * i + s, fa.slot(("dnS", s))
                    for t in range(T):
                        xt = xs[:, n, t * D:(t + 1) * D]
                        last = dve.scalar_tensor_tensor(xt, v[:, t * D:(t + 1) * D], c3[s][:, t:t + 1], xt, ALU.mult, ALU.add)
                    last.then_inc(fa.drained(("dnS", s)), 1)
                    dve.drain()
                    dve.wait_ge(fa.filled, fa.full(i, ("dnR", s)))
                    v = fa.slot(("dnR", s))
                    dve.scalar_tensor_tensor(xs[:, n, :], v, gt[:, 7:8], xs[:, n, :], ALU.mult, ALU.add)\
                       .then_inc(fa.drained(("dnR", s)), 1)
                    dve.drain().then_inc(x_done.sem, 1)


_INS = ['x', 'ctx_512', 'g_xattn', 'g_ffn', 'L0_xattn_W_k', 'L0_xattn_b_k', 'L0_xattn_ln_gamma', 'L0_xattn_ln_beta',
        'L0_ffn_gate_w', 'L0_ffn_gate_b', 'L0_ffn_expert_w', 'L0_ffn_expert_b', 'L1_xattn_Wq', 'L1_xattn_Wkv_expand',
        'L1_xattn_Wout', 'L1_ffn_w_gate', 'L1_ffn_w_up', 'L1_ffn_w_down', 'L2_xattn_Wq', 'L2_xattn_Wk',
        'L2_xattn_gamma_raw', 'L2_ffn_w12', 'L2_ffn_w3', 'L2_ffn_router_w', 'L2_ffn_expert_bias', 'L2_ffn_sw1',
        'L2_ffn_sw2', 'L2_ffn_sw3', 'L3_ffn_W_router', 'L3_ffn_W_sgate', 'L3_ffn_Ws_gate_up', 'L3_ffn_Ws_down',
        'L3_ffn_We_gate_up', 'L3_ffn_We_down']


def kernel(**inputs):
    import numpy as _np
    import concourse.bacc as _bacc
    from concourse import mybir as _mybir
    from concourse.bass_utils import run_bass_kernel_spmd as _run

    nc = _bacc.Bacc("TRN2", target_bir_lowering=False, num_devices=1)
    arrays, args = {}, []

    def give(name, a):
        arrays[name] = a
        args.append(nc.dram_tensor(name, a.shape, _mybir.dt.from_np(a.dtype), kind="ExternalInput").ap())

    for name in _INS:
        a = _np.ascontiguousarray(inputs[name])
        give(f"in_{name}", a.reshape(1) if a.ndim == 0 else a)
    had = _np.ones((1, 1), _np.float32)
    while had.shape[0] < P:
        had = _np.block([[had, had], [had, -had]])
    row = _np.arange(P)
    later = _np.where(row[None, :] > row[:, None], NEG, 0.0)
    give("consts", _np.concatenate([_np.eye(P), had, later, later.T, _np.tile(_np.arange(E), (P, 1))], 1)
         .astype(_np.float32))
    args.append(nc.dram_tensor("out_0", (B, S, D), _mybir.dt.float32, kind="ExternalOutput").ap())
    flamingo_gated(nc, *args)
    r = _run(nc, [arrays], core_ids=[0])
    return r.results[0]["out_0"]
```

```python
from contextlib import ExitStack

import concourse.bass as bass
from concourse import mybir

F32 = mybir.dt.float32
BF16 = mybir.dt.bfloat16
U32 = mybir.dt.uint32
ALU = mybir.AluOpType
ACT = mybir.ActivationFunctionType
X = mybir.AxisListType.X

P = 128
B, S, D, C = 4, 256, 256, 64
T = S // P
DC = D // P
W = T * D
E = 8
H_FFN = 1024
HC = H_FFN // P
H_R2 = 128
H_S3, H_R3 = 704, 176
SC3, RC3 = -(-H_S3 // P), E * H_R3 // P
NH1, HD1 = 16, 16
NH3, KV3, HD3 = 32, 8, 8
K1 = 6 * HD1
K3 = 6 * HD3
G1 = 4
M1, M3 = G1 * (HD1 + 1), KV3 * (HD3 + 1)
TOPK_ROW = max(1, int(S * 0.3))
ROUNDS = -(-TOPK_ROW // 8)
TURNS = B // 2
assert TURNS == 2
BANK = 512
ROUND = 1.5 * 2.0 ** 23
QB = 128.0
NEG = -1e30
RSQRT_BITS = float(0x5F3759DF)
EPS, EPS0 = 1e-5, 1e-6


class Signal:

    def __init__(self, sem, per=1, credit=0):
        self.sem, self.per, self.credit = sem, per, credit

    def count(self, n, k=None):
        return n * self.per + (self.per if k is None else k) + self.credit

    def free(self, n, k=0):
        return n * self.per + k + 1


class Fills:

    def __init__(self, filled, filled_before, slots, drained, drained_before, keys, turns):
        self.filled, self.filled_before, self.slots = filled, filled_before, slots
        self.banks_drained, self.drained_before = drained, drained_before
        self.index = {key: j for j, key in enumerate(keys)}
        self.per = len(keys)
        assert len(self.index) == self.per and (turns == 1 or self.per % len(slots) == 0)

    def slot(self, key):
        return self.slots[self.index[key] % len(self.slots)]

    def drained(self, key):
        return self.banks_drained[self.index[key] % len(self.slots)]

    def empty(self, i, key):
        j, m = self.index[key], len(self.slots)
        return self.drained_before[j % m] + i * (self.per // m) + j // m

    def full(self, i, key):
        return self.filled_before + i * self.per + self.index[key] + 1

    def read(self, i, key):
        return self.empty(i, key) + 1


class Space:

    def __init__(self, tensor, at=0):
        self.tensor, self.at = tensor, at

    def take(self, n, dt=F32, parts=P):
        words = n if dt is F32 else (n + 1) // 2
        view = self.tensor[0:parts, self.at:self.at + words]
        self.at += words
        assert self.at <= self.tensor.shape[1], (self.at, self.tensor.shape)
        return view if dt is F32 else view.bitcast(dt)


def flamingo_gated(nc, x, ctx_512, g_xattn, g_ffn, W_k0, b_k0, ln_gamma, ln_beta, gate_w, gate_b, expert_w, expert_b,
                   Wq1, Wkv1, Wout1, w_gate, w_up, w_down, Wq2, Wk2, gamma_raw, w12, w3, router_w, expert_bias,
                   sw1, sw2, sw3, W_router, W_sgate, Ws_gate_up, Ws_down, We_gate_up, We_down, consts, out):
    with ExitStack() as ctx:
        def sb(name, shape, dt=F32):
            return ctx.enter_context(nc.sbuf_tensor(name, shape, dt))

        def sem(name):
            return ctx.enter_context(nc.semaphore(name))

        psum = ctx.enter_context(nc.psum_tensor("psum", [P, 8 * BANK], F32))

        xs = sb("xs", [P, B, W])
        adj = sb("adj", [P, B, T * S])
        ctx_all = sb("ctx_all", [P, B, T * C])
        con = sb("con", [P, 4 * P + E])
        ident, hadamard, iota8 = con[:, 0:P], con[:, P:2 * P], con[:, 4 * P:4 * P + E]
        conb = sb("conb", [P, 4 * P], BF16)
        identb, mask_q, mask_k, onesb = (conb[:, k * P:(k + 1) * P] for k in range(4))
        bias3 = sb("bias3", [3, E * D], BF16)
        small = Space(sb("small", [P, 1600]))
        graw, gt, gt0_half = small.take(8), small.take(8), small.take(1)
        gam, gam_s, keep_x, keep_a = (small.take(1) for _ in range(4))
        lng, lnb = small.take(S), small.take(S)
        bk_row, bk_col = small.take(C), small.take(1, parts=C)
        gate0, gate0_b = small.take(DC * E), small.take(E)
        bias_f, bias_r = small.take(E * D // P), small.take(E * D // P)
        bias_p = [small.take(E * D // P, BF16) for _ in range(3)]
        raw64 = small.take(3 * C, parts=C)
        wT64 = small.take(3 * C, parts=C)
        wk0T, wq2T, wk2T = (wT64[:, k * C:(k + 1) * C] for k in range(3))
        wsum, wsums, wmean, wscale = (small.take(k) for k in (TURNS * 3, TURNS * 3, 3, 3))
        ebias = small.take(E)
        rT = small.take(DC * (2 * E + 1))
        r2T, r3T = rT[:, 0:DC * E], rT[:, DC * E:]

        early = sb("early", [P, 12800])
        sp0 = Space(early)
        ex_w = sp0.take(DC * E * D)
        wgT, wuT = sp0.take(DC * H_FFN, BF16), sp0.take(DC * H_FFN, BF16)
        wdT = sp0.take(HC * D, BF16)
        wq1T, wout1T, wkv1T = sp0.take(DC * D), sp0.take(DC * D), sp0.take(2 * D, parts=C)
        sp0 = Space(early, 8704)
        raw_sw = [sp0.take(2048), sp0.take(2048), early[:, 0:2048]]
        raw_w12, raw_w3 = early[:, 8704:12800], early[:, 0:2048]
        raw_r2, raw_r3 = early[0:E, 2048:2048 + D], early[0:E + 1, 2048 + D:2048 + 2 * D]
        sp3 = Space(early)
        we_gu, ws_gu = sp3.take(DC * E * 2 * H_R3), sp3.take(DC * 2 * H_S3)
        we_dn, ws_dn = sp3.take(RC3 * D), sp3.take(SC3 * D)

        late = sb("late", [P, 12288])
        sp2 = Space(late)
        raw_wq1, raw_wkv1, raw_wout1 = sp2.take(W), sp2.take(4 * C), sp2.take(W)
        raw_f1 = [sp2.take(2048) for _ in range(3)]
        tern = [sp2.take(2048, BF16) for _ in range(3)]
        sp2 = Space(late)
        w12T, w3T = sp2.take(DC * E * 2 * H_R2), sp2.take(E * D)
        sw1T, sw2T, sw3T = sp2.take(DC * H_FFN), sp2.take(DC * H_FFN), sp2.take(HC * D)

        shared = sb("shared", [P, 6912])
        arena = [sb(f"arena{s}", [P, 6400]) for s in range(2)]

        def cols(n, k):
            return [small.take(n * k).rearrange("p (n k) -> p n k", n=n) for _ in range(2)]

        st, mv = small.take(2 * T * 6).rearrange("p (n k) -> p n k", k=6), small.take(2 * T * 2).rearrange("p (n k) -> p n k", k=2)
        var, seed, newton, rstd = (small.take(2 * T) for _ in range(4))
        m8, idf = cols(T, 8), cols(T, 2)
        idx = [v.bitcast(U32) for v in cols(T, 8)]
        lg, oh, pick, cw = cols(T, E), cols(T, E), cols(T, E), cols(T, E)
        c1, c2, c3, c4 = ([small.take(T) for _ in range(2)] for _ in range(4))

        sim1, work1, th1, aa1 = (early[:, 2048 + k * T * S:2048 + (k + 1) * T * S] for k in range(4))

        def carve(*parts):
            made = []
            for s in range(2):
                sp = Space(arena[s])
                made.append([sp.take(*p) for p in parts])
            return [list(v) for v in zip(*made)]

        xn, xnT, cx, ctxT = carve((W,), (W,), (T * C,), (S, F32, C))
        base = (W + W + T * C + S,)
        _, kv0, kvT0, oT0, z0, e0 = carve(base, (T * C,), (S, F32, C), (S, F32, C), (T * S,), (T * S,))
        _, acc0, qkT, sim, work, th, aa = carve(base, (W,), (2 * S, F32, C), (T * S,), (T * S,), (T * S,), (T * S,))
        rexp = [shared[:, t * 2048:(t + 1) * 2048] for t in range(T)]
        _, qT1, kT1, nmax1, sh1, shT1, rec1 = carve(base, (NH1 * S, BF16), (NH1 * S, BF16), (T * NH1,),
                                                    (T * 2 * NH1, BF16), (S, BF16, 2 * NH1), (T * NH1,))
        sph = Space(shared)
        qs1 = [sph.take(T * NH1 * K1, BF16) for _ in range(2)]
        ks1 = [sph.take(T * NH1 * (K1 + 2), BF16) for _ in range(2)]
        rest1 = [late[:, k * W:(k + 1) * W] for k in range(2)]
        sp1 = Space(late, 2 * W + 4 * C)
        vpad1 = [sp1.take(T * NH1 * M1) for _ in range(2)]
        xoT1 = [sp1.take(W) for _ in range(2)]
        pexp1 = [late[:, 12288 - (k + 1) * 768:12288 - k * 768] for k in range(2)]
        _, qT3, kT3, vpad3, nmax3, sh3, shT3, rec3 = carve(base, (NH3 // 2 * S, BF16), (KV3 * S, BF16),
                                                           (T * KV3 * M3 + M3,), (T * NH3,), (T * 2 * NH3, BF16),
                                                           (S, BF16, 2 * NH3), (T * NH3,))
        sph = Space(shared)
        qs3 = [sph.take(T * NH3 * 64, BF16) for _ in range(2)]
        ks3 = [sph.take(T * KV3 * P, BF16) for _ in range(2)]
        sp3 = Space(late)
        rest3 = [sp3.take(W) for _ in range(2)]
        pexp3 = [sp3.take(2 * BANK) for _ in range(2)]
        oT13 = [arena[s][:, base[0]:base[0] + 2 * BANK] for s in range(2)]
        _, xq, ha, hb, yqT = carve((2 * W,), (W, BF16), (T * H_FFN,), (T * H_FFN,), (T * H_FFN, BF16))
        sph = Space(shared)
        sg1 = [sph.take(BANK) for _ in range(4)]
        bfly, yqb = sph.take(H_FFN), [sph.take(T * H_FFN, BF16) for _ in range(2)]
        xqT = [sph.take(W, BF16) for _ in range(2)]
        _, hsT2, hrT2 = carve(base, (HC * S,), (T * E * P,))
        sph = Space(shared)
        sg2 = [sph.take(S) for _ in range(4)]
        hr2 = [sph.take(E * H_R2) for _ in range(T)]
        _, hsT3, hrT3 = carve(base, (SC3 * S,), (T * RC3 * P,))
        sph = Space(shared)
        sg3 = [sph.take(S) for _ in range(4)]
        hr3 = [sph.take(E * H_R3) for _ in range(T)]

        ld = {n: sem("ld_" + n) for n in ("x", "ctx", "con", "cols", "ex", "bias", "l1a", "l1f", "sw12", "sw3",
                                          "w12", "w3", "l3")}
        stored = sem("stored")
        const_ready, gates_ready, bias_ready = sem("const_ready"), sem("gates_ready"), sem("bias_ready")
        tanh_ready, egam_ready, wsum_ready, tern_ready = (sem("tanh_ready"), sem("egam_ready"), sem("wsum_ready"),
                                                          sem("tern_ready"))
        bank_drained = [sem(f"bank{k}_drained") for k in range(8)]
        filled = {g: sem("filled_" + g) for g in "ABC"}

        def sig(name, per=1, credit=0):
            return Signal(sem(name), per, credit)

        normed = {l: k * B for k, l in enumerate(("l0x", "l0f", "l1x", "l1f", "l2f", "l3x", "l3f"))}
        xn_ready = sig("xn_ready")
        cx_ready = {l: sig(f"{l}_cx_ready") for l in ("l0x", "l0f", "l1x", "l3x")}
        l0_z_ready, l0_e_ready = sig("l0_z_ready"), sig("l0_e_ready")
        l0_pick_ready, rexp_free = sig("l0_pick_ready"), sig("rexp_free", T, 2)
        aa_ready, sim1_ready = sig("aa_ready"), sig("sim1_ready")
        q1_ready, k1_ready = ({l: sig(f"{l}_{n}") for l in ("l1x", "l3x")}
                              for n in ("q1_ready", "k1_ready"))
        qparts_ready, kparts_ready = ({l: sig(f"{l}_{n}") for l in ("l1x", "l3x")}
                                      for n in ("qparts_ready", "kparts_ready"))
        vpad_ready, pads_ready = sem("vpad_ready"), sem("pads_ready")
        shift_ready = {l: sig(f"{l}_shift_ready") for l in ("l1x", "l3x")}
        shift_in = {"l1x": sig("l1x_shift_in", 32), "l3x": sig("l3x_shift_in", 64)}
        v_ready = sig("l3x_v_ready")
        pv_done = {"l1x": sig("l1x_pv_done", NH1 // 2, 2), "l3x": sig("l3x_pv_done", NH3 // 2, 2)}
        xq_ready, y_ready = sig("xq_ready"), sig("y_ready", T)
        yq_ready = sig("yq_ready", T)
        sg2_ready, sg3_ready = sig("sg2_ready", HC + T * E // 2), sig("sg3_ready", SC3 + T * E)
        lg3_ready, sc3_ready = sig("lg3_ready"), sig("sc3_ready")
        x_done = sig("x_done")
        with_credit = (rexp_free, pv_done["l1x"], pv_done["l3x"])

        counts, drains, loop_start = {g: 0 for g in "ABCV"}, [1] * 8, {}

        def plan(loop, turns, **groups):
            loop_start[loop] = list(drains)
            made = {}
            for g, (firsts, wide, keys) in groups.items():
                made[g] = Fills(filled.get(g), counts[g], [psum[:, k * BANK:(k + wide) * BANK] for k in firsts],
                                [bank_drained[k] for k in firsts], [drains[k] for k in firsts], keys, turns)
                counts[g] += turns * len(keys)
                for j in range(len(keys)):
                    drains[firsts[j % len(firsts)]] += turns
            return made

        def streams(*stages):
            return [(k[0], s, *k[1:]) for stage in stages for s in range(2) for k in stage]

        pl = {}
        pl["prep0"] = plan("prep0", 1, A=([0, 1, 2], 1, [("w64",), ("xT", 0), ("xT", 1)]))
        pl["l0x"] = plan("l0x", TURNS, A=([0, 1, 2, 3, 4], 1, streams([("cT",)], [("kv",)], [("oT",)], [("sim",)], [("xT",)])))
        pl["l0f"] = plan("l0f", TURNS,
                         A=([6, 7], 1, streams([("gate",)], [("xT",)])),
                         B=([0, 1, 2, 3], 1, streams([("ex", t, k) for t in range(T) for k in range(E // 2)])),
                         C=([4, 5], 1, streams([("cT",)], [("qk",)], [("sim",)]) + [("AT", 0), ("AT", 1)]))
        pl["prep1"] = plan("prep1", 1, A=([0, 1, 2, 3], 1, [("wq",), ("wkv",), ("wout",)]))
        pl["l1x"] = plan("l1x", TURNS,
                         A=([4, 5], 1, streams([("cT",)],
                                               [("qsT", k) for k in range(4)] + [("ksT", k) for k in range(4)]
                                               + [("max", k) for k in range(12)] + [("shT",)])
                            + [("tok", 0, 0), ("tok", 0, 1), ("oT", 0), ("out", 0), ("AT", 0), ("AT", 1), ("xT", 0),
                               ("xT", 1), ("tok", 1, 0), ("tok", 1, 1), ("oT", 1), ("out", 1)]),
                         B=([0, 2], 2, streams([("q",)], [("kv",)], [("sc", k) for k in range(NH1 // 2)])),
                         V=([6], 2, streams([("pv",)])))
        pl["prep1b"] = plan("prep1b", 1, A=([0, 1, 2, 3], 1, [("tern", w, k) for w in range(3) for k in range(2)]))
        pl["prep2a"] = plan("prep2a", 1, A=([0, 1, 2, 3], 1, [("sw", w, k) for w in range(3) for k in range(4)]))
        pl["l1f"] = plan("l1f", TURNS,
                         A=([6, 7], 1, streams([("qT",)], [("xT",)], [("yT", 0), ("yT", 1)], [("dn",)])),
                         B=([0, 1, 2, 3], 1, streams([(w, t, h) for t in range(T) for h in range(2) for w in "gu"])),
                         C=([4, 5], 1, streams([("hT", t, h) for t in range(T) for h in range(2)],
                                               [("had", t, h) for t in range(T) for h in range(2)])))
        pl["prep2b"] = plan("prep2b", 1, A=([0, 1, 2, 3], 1, [("w12", k) for k in range(8)] + [("w3", k) for k in range(4)]
                                           + [("r",)]))
        pl["l2f"] = plan("l2f", TURNS,
                         A=([6, 7], 1, streams([("gate",)]) + [("hrT", 0, t, k) for t in range(T) for k in range(2)]
                            + [("dn", 0), ("xT", 0), ("xT", 1)] + [("hrT", 1, t, k) for t in range(T) for k in range(2)]
                            + [("dn", 1)]),
                         B=([0, 1, 2, 3], 1, streams([("sh", j) for j in range(HC)]
                                                     + [("ro", t, k) for t in range(T) for k in range(E // 2)])))
        pl["l3x"] = plan("l3x", TURNS,
                         A=([4, 5], 1, streams([("qsT", k) for k in range(4)] + [("ksT", k) for k in range(2)]
                                               + [("max", k) for k in range(32)] + [("shT",)])),
                         B=([0, 2], 2, [("sc", 0, k) for k in range(NH3 // 2)] + [("tok", 0)] + [("sc", 1, k) for k in range(2)]
                            + [("xT", 0), ("xT", 1)] + [("sc", 1, k) for k in range(2, NH3 // 2)] + [("tok", 1)]),
                         V=([6], 2, streams([("pv",)])))
        pl["l3f"] = plan("l3f", TURNS,
                         A=([6, 7], 1, streams([("gate",)]) + [("hrT", 0, t, k) for t in range(T) for k in range(3)]
                            + [("dnS", 0), ("dnR", 0), ("xT", 0), ("xT", 1)]
                            + [("hrT", 1, t, k) for t in range(T) for k in range(3)] + [("dnS", 1), ("dnR", 1)]),
                         B=([0, 1, 2, 3], 1, streams([("sh", j) for j in range(SC3)]
                                                     + [("ro", t, k) for t in range(T) for k in range(E)])))

        def q3d(v, *dims):
            names = "abcd"[:len(dims)]
            return v.rearrange(f"p ({' '.join(names)}) -> p {' '.join(names)}", **dict(zip(names, dims)))

        waits_passed = sem("waits_passed")

        def own_instruction(eng):
            eng.sem_inc(waits_passed, 1)

        block = ctx.enter_context(nc.Block())

        @block.sync
        def _(sp):
            def load(dst, src, name):
                sp.dma_start(dst, src).then_inc(ld[name], 16)

            load(con[:], consts, "con")
            load(ctx_all[:].rearrange("p b (t c) -> p (b t) c", t=T), ctx_512.rearrange("b (t p) c -> p (b t) c", p=P), "ctx")
            load(xs[:].rearrange("p b (t d) -> p (b t) d", t=T), x.rearrange("b (t p) d -> p (b t) d", p=P), "x")
            for k, w in enumerate((W_k0, Wq2, Wk2)):
                load(raw64[:, k * C:(k + 1) * C], w, "cols")
            load(graw[:, 0:4], g_xattn.partition_broadcast(P), "cols")
            load(graw[:, 4:8], g_ffn.partition_broadcast(P), "cols")
            load(gam, gamma_raw.partition_broadcast(P), "cols")
            load(lng, ln_gamma.partition_broadcast(P), "cols")
            load(lnb, ln_beta.partition_broadcast(P), "cols")
            load(bk_row, b_k0.partition_broadcast(P), "cols")
            load(bk_col, b_k0.rearrange("(c a) -> c a", a=1), "cols")
            load(gate0_b, gate_b.partition_broadcast(P), "cols")
            load(ebias, expert_bias.partition_broadcast(P), "cols")
            load(q3d(gate0, DC, E), gate_w.rearrange("(c p) e -> p c e", p=P), "cols")
            load(bias_f, expert_b.rearrange("e (q k) -> (e q) k", k=E * D // P), "cols")
            for c in range(DC):
                load(q3d(ex_w, DC, E, D)[:, c], expert_w.rearrange("e (c p) o -> c p e o", p=P)[c], "ex")
            load(q3d(raw_wq1, T, D), Wq1.rearrange("(o p) i -> p o i", p=P), "l1a")
            load(q3d(raw_wkv1, 4, C), Wkv1.rearrange("(o p) i -> p o i", p=P), "l1a")
            load(q3d(raw_wout1, T, D), Wout1.rearrange("(o p) i -> p o i", p=P), "l1a")
            load(q3d(raw_f1[0], HC, D), w_gate.rearrange("(o p) i -> p o i", p=P), "l1f")
            load(q3d(raw_f1[1], HC, D), w_up.rearrange("(o p) i -> p o i", p=P), "l1f")
            load(q3d(raw_f1[2], T, H_FFN), w_down.rearrange("(o p) i -> p o i", p=P), "l1f")
            load(q3d(raw_sw[0], HC, D), sw1.rearrange("(o p) i -> p o i", p=P), "sw12")
            load(q3d(raw_sw[1], HC, D), sw2.rearrange("(o p) i -> p o i", p=P), "sw12")
            sp.wait_ge(bias_ready, 1)
            for k in range(3):
                load(bias3[k:k + 1, :], bias_p[k], "bias")
            sp.wait_ge(pl["l0f"]["B"].filled, pl["l0f"]["B"].full(TURNS - 1, ("ex", 1, T - 1, E // 2 - 1)))
            load(q3d(raw_sw[2], T, H_FFN), sw3.rearrange("(o p) i -> p o i", p=P), "sw3")

            f = pl["l1x"]["A"]
            with sp.Fori(0, TURNS) as i:
                for s in range(2):
                    sp.wait_ge(f.drained(("shT", s)), f.read(i, ("shT", s)))
                    for r in range(2):
                        sp.dma_start(qT1[s][K1 + r:K1 + r + 1, :], shT1[s][r * NH1:(r + 1) * NH1, :])\
                          .then_inc(shift_in["l1x"].sem, 16)

            sp.wait_ge(pl["prep2a"]["A"].filled, pl["prep2a"]["A"].full(0, ("sw", 1, 3)))
            load(q3d(raw_w12, E * 2, D), w12.rearrange("e (h p) d -> p (e h) d", p=P), "w12")
            sp.wait_ge(pl["prep2a"]["A"].filled, pl["prep2a"]["A"].full(0, ("sw", 2, 3)))
            load(q3d(raw_w3, E * 2, H_R2), w3.rearrange("e (d p) h -> p (e d) h", p=P), "w3")
            load(raw_r2, router_w, "w3")
            load(raw_r3[0:E, :], W_router, "w3")
            load(raw_r3[E:E + 1, :], W_sgate, "w3")
            sp.wait_ge(pl["l1f"]["A"].filled, pl["l1f"]["A"].full(TURNS - 1, ("dn", 1)))
            sp.wait_ge(pl["prep2b"]["A"].filled, pl["prep2b"]["A"].full(0, ("r",)))
            load(q3d(ws_gu, DC, 2 * H_S3), Ws_gate_up.rearrange("(c p) h -> p c h", p=P), "l3")
            load(q3d(ws_dn, SC3, D)[:, 0:SC3 - 1], Ws_down[0:(SC3 - 1) * P, :].rearrange("(j p) o -> p j o", p=P), "l3")
            load(q3d(ws_dn, SC3, D)[0:H_S3 - (SC3 - 1) * P, SC3 - 1], Ws_down[(SC3 - 1) * P:H_S3, :], "l3")
            for c in range(DC):
                load(q3d(we_gu, DC, E, 2 * H_R3)[:, c], We_gate_up.rearrange("e (c p) h -> c p e h", p=P)[c], "l3")
            load(q3d(we_dn, RC3, D), We_down.rearrange("e i o -> (e i) o").rearrange("(j p) o -> p j o", p=P), "l3")

            f = pl["l3x"]["A"]
            with sp.Fori(0, TURNS) as i:
                for s in range(2):
                    sp.wait_ge(f.drained(("shT", s)), f.read(i, ("shT", s)))
                    for r in range(2):
                        for par in range(2):
                            row, src = 64 * par + K3 + r, (2 * r + par) * (NH3 // 2)
                            sp.dma_start(qT3[s][row:row + 1, :], shT3[s][src:src + NH3 // 2, :])\
                              .then_inc(shift_in["l3x"].sem, 16)

            out_v = out.rearrange("b (t p) d -> b p t d", p=P)
            with sp.Fori(0, TURNS) as i:
                for s in range(2):
                    n = 2 * i + s
                    sp.wait_ge(x_done.sem, x_done.count(n))
                    sp.dma_start(out_v[n], q3d(xs[:, n, :], T, D)).then_inc(stored, 16)
            sp.wait_ge(stored, 16 * B)

        @block.gpsimd
        def _(pool):
            for signal in with_credit:
                pool.sem_inc(signal.sem, signal.credit)
            for k in range(8):
                pool.sem_inc(bank_drained[k], 1)
            pool.memset(onesb, 1.0)
            pool.wait_ge(ld["con"], 16)
            pool.tensor_copy(identb, ident)
            pool.tensor_copy(conb[:, P:3 * P], con[:, 2 * P:4 * P])
            pool.drain().then_inc(const_ready, 1)
            pool.wait_ge(wsum_ready, TURNS)
            pool.partition_all_reduce(wsums, wsum, P, bass.bass_isa.ReduceOp.add).then_inc(wsum_ready, 1)
            pool.wait_ge(wsum_ready, TURNS + 2)
            for w in range(3):
                pool.tensor_scalar(raw_f1[w], raw_f1[w], wscale[:, w:w + 1], ROUND, ALU.mult, ALU.add)
            pool.drain()
            for w in range(3):
                pool.tensor_scalar(raw_f1[w], raw_f1[w], -ROUND, 1.0, ALU.add, ALU.mult)
            pool.drain()
            for w in range(3):
                last = pool.tensor_scalar(tern[w], raw_f1[w], 1.0, -1.0, ALU.min, ALU.max)
            last.then_inc(tern_ready, 1)

            pool.drain()
            for s in range(2):
                pool.memset(vpad1[s], 0.0)
            pool.drain()
            for s in range(2):
                v = vpad1[s].rearrange("p (n x) -> p n x", x=G1 * M1)
                for k in range(G1):
                    at = k * (M1 + HD1 + 1) + HD1
                    pool.memset(v[:, :, at:at + 1], 1.0)
            pool.wait_ge(rexp_free.sem, rexp_free.count(B - 1))
            for s in range(2):
                pool.memset(ks1[s].rearrange("p (h k) -> p h k", k=K1 + 2)[:, :, K1:], 1.0)
            pool.drain().then_inc(vpad_ready, 1)

            with pool.Fori(0, TURNS) as i:
                for s in range(2):
                    for t in range(T):
                        rows = slice(t * H_FFN, (t + 1) * H_FFN)
                        pool.wait_ge(y_ready.sem, y_ready.count(2 * i + s, t + 1))
                        own_instruction(pool)
                        pool.tensor_scalar(ha[s][:, rows], ha[s][:, rows], c2[s][:, t:t + 1], ROUND, ALU.mult, ALU.add)
                        pool.drain()
                        pool.tensor_scalar(yqb[s][:, rows], ha[s][:, rows], -ROUND, 1.0, ALU.add, ALU.mult)\
                            .then_inc(yq_ready.sem, 1)

            def diagonal3(s, t):
                return vpad3[s][:, t * KV3 * M3:(t + 1) * KV3 * M3 + M3].rearrange("p (j x) -> p j x", x=M3 + HD3 + 1)

            pool.wait_ge(pl["l2f"]["A"].filled, pl["l2f"]["A"].full(TURNS - 1, ("dn", 1)))
            for s in range(2):
                pool.memset(vpad3[s], 0.0)
                pool.memset(qs3[s].rearrange("p (h k) -> p h k", k=64)[:, :, K3:], 0.0)
                kv = ks3[s].rearrange("p (h k) -> p h k", k=64)
                pool.memset(kv[:, :, K3:K3 + 2], 1.0)
                pool.memset(kv[:, :, K3 + 2:], 0.0)
            pool.drain()
            for s in range(2):
                for t in range(T):
                    pool.memset(diagonal3(s, t)[:, :, HD3:HD3 + 1], 1.0)
            pool.drain().then_inc(pads_ready, 1)
            with pool.Fori(0, TURNS) as i:
                for s in range(2):
                    n = 2 * i + s
                    pool.wait_ge(cx_ready["l3x"].sem, cx_ready["l3x"].count(n))
                    own_instruction(pool)
                    for t in range(T):
                        pool.tensor_copy(diagonal3(s, t)[:, :, 0:HD3],
                                         cx[s][:, t * C:(t + 1) * C].rearrange("p (j k) -> p j k", k=HD3))
                    pool.drain().then_inc(v_ready.sem, 1)

        @block.tensor
        def _(pe):
            def banks_free(loop):
                for k in range(8):
                    pe.wait_ge(bank_drained[k], loop_start[loop][k])

            def turn(f, i, key, blocks, idn, dt=F32):
                pe.wait_ge(f.drained(key), f.empty(i, key))
                v = f.slot(key)
                v = v if dt is F32 else v.bitcast(dt)
                if blocks[0][2].shape[1] < P:
                    own_instruction(pe)
                for parts, at, src in blocks:
                    k = src.shape[0]
                    last = pe.transpose(v[0:parts, at:at + k], src, idn[0:k, 0:k])
                last.then_inc(f.filled, 1)

            def turn_x(f, i, s, key, src, idn=ident, dt=F32):
                turn(f, i, key, [(P, c * S + t * P, src[:, t * D + c * P:t * D + (c + 1) * P])
                                 for c in range(DC) for t in range(T)], idn, dt)

            def turn_next(loop, i, group="A"):
                for s in range(2):
                    pe.wait_ge(xn_ready.sem, xn_ready.count(normed[loop] + 2 * i + 2 + s))
                    turn_x(pl[loop][group], i, s, ("xT", s), xn[s])

            def next_turned(f, i):
                for s in range(2):
                    pe.wait_ge(f.drained(("xT", s)), f.read(i, ("xT", s)))

            def turn_cx(f, i, s):
                turn(f, i, ("cT", s), [(C, t * P, cx[s][:, t * C:(t + 1) * C]) for t in range(T)], ident)

            pe.wait_ge(ld["con"], 16)
            pe.wait_ge(ld["cols"], 16 * 14)
            pe.wait_ge(const_ready, 1)
            turn(pl["prep0"]["A"], 0, ("w64",), [(C, k * C, raw64[:, k * C:(k + 1) * C]) for k in range(3)], ident)
            for s in range(2):
                pe.wait_ge(xn_ready.sem, xn_ready.count(s))
                turn_x(pl["prep0"]["A"], 0, s, ("xT", s), xn[s])
            next_turned(pl["prep0"]["A"], 0)

            def turn_adjacency(f, i, n, a):
                pe.wait_ge(aa_ready.sem, aa_ready.count(n))
                for t in range(T):
                    turn(f, i, ("AT", t), [(P, u * P, a[:, u * S + t * P:u * S + (t + 1) * P]) for u in range(T)], ident)

            banks_free("l0x")
            f = pl["l0x"]["A"]
            with pe.Fori(0, TURNS) as i:
                for s in range(2):
                    pe.wait_ge(cx_ready["l0x"].sem, cx_ready["l0x"].count(2 * i + s))
                    turn_cx(f, i, s)
                for s in range(2):
                    pe.wait_ge(f.drained(("cT", s)), f.read(i, ("cT", s)))
                    pe.wait_ge(f.drained(("kv", s)), f.empty(i, ("kv", s)))
                    v = f.slot(("kv", s))
                    for t in range(T):
                        pe.matmul(v[:, t * C:(t + 1) * C], ctxT[s][:, t * P:(t + 1) * P], wk0T, start=True, stop=True)
                    pe.matmul(v[0:C, S:2 * S], wk0T, ctxT[s], start=True, stop=True).then_inc(f.filled, 1)
                for s in range(2):
                    pe.wait_ge(f.drained(("kv", s)), f.read(i, ("kv", s)))
                    pe.wait_ge(f.drained(("oT", s)), f.empty(i, ("oT", s)))
                    v = f.slot(("oT", s))
                    for t in range(T):
                        mm = pe.matmul(v[0:C, 0:S], kv0[s][:, t * C:(t + 1) * C], xnT[s][:, t * S:(t + 1) * S],
                                       start=(t == 0), stop=(t == T - 1))
                    mm.then_inc(f.filled, 1)
                for s in range(2):
                    pe.wait_ge(f.drained(("oT", s)), f.read(i, ("oT", s)))
                    pe.wait_ge(f.drained(("sim", s)), f.empty(i, ("sim", s)))
                    v = f.slot(("sim", s))
                    for t in range(T):
                        mm = pe.matmul(v[:, t * S:(t + 1) * S], oT0[s][:, t * P:(t + 1) * P], kvT0[s], start=True, stop=True)
                    mm.then_inc(f.filled, 1)
                turn_next("l0x", i)
                next_turned(f, i)

            banks_free("l0f")
            fa, fb, fc = (pl["l0f"][g] for g in "ABC")
            pe.wait_ge(ld["ex"], 16 * DC)
            pe.wait_ge(ld["bias"], 16 * 3)
            with pe.Fori(0, TURNS) as i:
                for s in range(2):
                    pe.wait_ge(fa.drained(("gate", s)), fa.empty(i, ("gate", s)))
                    v = fa.slot(("gate", s))
                    for t in range(T):
                        for c in range(DC):
                            mm = pe.matmul(v[:, t * E:(t + 1) * E], xnT[s][:, c * S + t * P:c * S + (t + 1) * P],
                                           gate0[:, c * E:(c + 1) * E], start=(c == 0), stop=(c == DC - 1))
                    mm.then_inc(fa.filled, 1)
                for s in range(2):
                    pe.wait_ge(cx_ready["l0f"].sem, cx_ready["l0f"].count(2 * i + s))
                    turn_cx(fc, i, s)
                for s in range(2):
                    pe.wait_ge(fc.drained(("cT", s)), fc.read(i, ("cT", s)))
                    pe.wait_ge(fc.drained(("qk", s)), fc.empty(i, ("qk", s)))
                    v = fc.slot(("qk", s))
                    own_instruction(pe)
                    pe.matmul(v[0:C, 0:S], wq2T, ctxT[s], start=True, stop=True)
                    pe.matmul(v[0:C, S:2 * S], wk2T, ctxT[s], start=True, stop=True).then_inc(fc.filled, 1)
                for s in range(2):
                    pe.wait_ge(fc.drained(("qk", s)), fc.read(i, ("qk", s)))
                    pe.wait_ge(fc.drained(("sim", s)), fc.empty(i, ("sim", s)))
                    v = fc.slot(("sim", s))
                    for t in range(T):
                        mm = pe.matmul(v[:, t * S:(t + 1) * S], qkT[s][:, t * P:(t + 1) * P], qkT[s][:, S:2 * S],
                                       start=True, stop=True)
                    mm.then_inc(fc.filled, 1)
                for s in range(2):
                    for t in range(T):
                        for k in range(E // 2):
                            pe.wait_ge(fb.drained(("ex", s, t, k)), fb.empty(i, ("ex", s, t, k)))
                            v = fb.slot(("ex", s, t, k))
                            for c in range(DC):
                                at = c * E * D + k * 2 * D
                                pe.matmul(v, xnT[s][:, c * S + t * P:c * S + (t + 1) * P], ex_w[:, at:at + 2 * D],
                                          start=(c == 0), stop=False)
                            pe.matmul(v, onesb[0:3, :], bias3[:, k * 2 * D:(k + 1) * 2 * D],
                                      start=False, stop=True).then_inc(fb.filled, 1)
                    if s == 0:
                        turn_adjacency(fc, i, i, aa[0])
                turn_next("l0f", i)
                next_turned(fa, i)

            banks_free("prep1")
            f = pl["prep1"]["A"]
            pe.wait_ge(ld["l1a"], 16 * 3)
            for key, raw in ((("wq",), raw_wq1), (("wout",), raw_wout1)):
                if key == ("wout",):
                    turn(f, 0, ("wkv",), [(C, o * P, raw_wkv1[:, o * C:(o + 1) * C]) for o in range(4)], ident)
                turn_x(f, 0, 0, key, raw)
            def attention(layer, i, turn_columns, score_max, n_max, nshift, sh, score_exp, values, n_exp, token_blocks,
                          first_results=None):
                fm, fe = pl[layer]["A"], pl[layer]["B"]

                def shift(s):
                    pe.wait_ge(shift_ready[layer].sem, shift_ready[layer].count(2 * i + s))
                    turn(fm, i, ("shT", s), [(nshift, t * P, sh[s][:, t * nshift:(t + 1) * nshift]) for t in range(T)],
                         identb, BF16)

                def tokens(s):
                    fv = pl[layer]["V"]
                    pe.wait_ge(fv.drained(("pv", s)), fv.read(i, ("pv", s)))
                    for t in range(T):
                        turn(fm, i, ("tok", s, t), token_blocks(s, t), ident)

                def exponentials(s, between):
                    pe.wait_ge(shift_in[layer].sem, shift_in[layer].count(2 * i + s))
                    for m in range(n_exp + 1):
                        if m < n_exp:
                            score_exp(i, s, m)
                        for k in between[m]:
                            score_max(i, 1, k)
                        if s == 1 and m == 2:
                            tokens(0)
                        if s == 1 and first_results is not None:
                            first_results(i, m)
                        if m == 0:
                            pe.wait_ge(pl[layer]["V"].drained(("pv", s)), pl[layer]["V"].empty(i, ("pv", s)))
                        else:
                            pe.wait_ge(fe.drained(("sc", s, m - 1)), fe.read(i, ("sc", s, m - 1)))
                            values(s, m - 1).then_inc(pv_done[layer].sem, 1)

                turn_columns(i, 0)
                for k in range(n_max):
                    score_max(i, 0, k)
                shift(0)
                turn_columns(i, 1)
                head = min(4, n_max)
                for k in range(head):
                    score_max(i, 1, k)
                rest = list(range(head, n_max))
                cut = [len(rest) * m // (n_exp + 1) for m in range(n_exp + 2)]
                exponentials(0, [rest[cut[m]:cut[m + 1]] for m in range(n_exp + 1)])
                shift(1)
                exponentials(1, [[]] * (n_exp + 1))
                turn_adjacency(fm, i, TURNS + i, aa1)
                turn_next(layer, i)
                tokens(1)

            banks_free("l1x")
            fa, fb = pl["l1x"]["A"], pl["l1x"]["B"]

            def turn_columns1(i, s):
                for name, ready, stack, pitch in (("qsT", qparts_ready, qs1, K1), ("ksT", kparts_ready, ks1, K1 + 2)):
                    pe.wait_ge(ready["l1x"].sem, ready["l1x"].count(2 * i + s))
                    for k in range(4):
                        turn(fa, i, (name, s, k), [(pitch, j * S + t * P, stack[s][:, (t * NH1 + 4 * k + j) * pitch:
                                                                                   (t * NH1 + 4 * k + j + 1) * pitch])
                                                   for j in range(4) for t in range(T)], identb, BF16)
                pe.wait_ge(fa.drained(("ksT", s, 3)), fa.read(i, ("ksT", s, 3)))
                pe.wait_ge(fa.drained(("ksT", s, 2)), fa.read(i, ("ksT", s, 2)))

            def max1(i, s, k):
                pe.wait_ge(fa.drained(("max", s, k)), fa.empty(i, ("max", s, k)))
                v = fa.slot(("max", s, k))
                t, heads, nk = (0, range(4 * k, 4 * k + 4), P) if k < 4 else (1, range(2 * k - 8, 2 * k - 6), S)
                for j, h in enumerate(heads):
                    pe.matmul(v[:, j * nk:(j + 1) * nk], qT1[s][0:K1, h * S + t * P:h * S + (t + 1) * P],
                              kT1[s][0:K1, h * S:h * S + nk], start=True, stop=True)
                    mm = pe.matmul(v[:, (j + 1) * nk - P:(j + 1) * nk], identb, mask_q, start=False, stop=True,
                                   skip_group_check=True)
                mm.then_inc(fa.filled, 1)

            def exp1(i, s, m):
                pe.wait_ge(fb.drained(("sc", s, m)), fb.empty(i, ("sc", s, m)))
                v = fb.slot(("sc", s, m))
                for j in range(2):
                    h, o = 2 * m + j, j * BANK
                    for t, at, nq in ((0, o, S), (1, o + S, P)):
                        pe.matmul(v[:, at:at + nq], kT1[s][0:K1 + 2, h * S + t * P:h * S + (t + 1) * P],
                                  qT1[s][0:K1 + 2, h * S + t * P:(h + 1) * S], start=True, stop=True)
                        mm = pe.matmul(v[:, at:at + P], identb, mask_k, start=False, stop=True, skip_group_check=True)
                mm.then_inc(fb.filled, 1)

            def values1(s, m):
                pv, p = pl["l1x"]["V"].slot(("pv", s)), pexp1[m % 2]
                for j in range(2):
                    h, o = 2 * m + j, j * (S + P)
                    g, first, last = h // G1, h % G1 == 0, h % G1 == G1 - 1
                    pe.matmul(pv[0:M1, g * S:(g + 1) * S], vpad1[s][:, h * M1:(h + 1) * M1], p[:, o:o + S],
                              start=first, stop=last)
                    mm = pe.matmul(pv[0:M1, g * S + P:(g + 1) * S], vpad1[s][:, (NH1 + h) * M1:(NH1 + h + 1) * M1],
                                   p[:, o + S:o + S + P], start=False, stop=last, skip_group_check=True)
                return mm

            def token_blocks1(s, t):
                return [(P, g * M1, oT13[s][0:M1, g * S + t * P:g * S + (t + 1) * P]) for g in range(NH1 // G1)]

            def turn_heads(i, s):
                pe.wait_ge(fa.drained(("tok", s, 1)), fa.read(i, ("tok", s, 1)))
                turn_x(fa, i, s, ("oT", s), rest1[s])

            def project(i, s):
                pe.wait_ge(fa.drained(("oT", s)), fa.read(i, ("oT", s)))
                pe.wait_ge(fa.drained(("out", s)), fa.empty(i, ("out", s)))
                v = fa.slot(("out", s))
                for t in range(T):
                    for c in range(DC):
                        mm = pe.matmul(v[:, t * D:(t + 1) * D], xoT1[s][:, c * S + t * P:c * S + (t + 1) * P],
                                       wout1T[:, c * D:(c + 1) * D], start=(c == 0), stop=(c == DC - 1))
                mm.then_inc(fa.filled, 1)

            def first_results(i, m):
                if m == 4:
                    turn_heads(i, 0)
                elif m == 6:
                    project(i, 0)

            with pe.Fori(0, TURNS) as i:
                for s in range(2):
                    pe.wait_ge(fb.drained(("q", s)), fb.empty(i, ("q", s)))
                    v = fb.slot(("q", s))
                    for t in range(T):
                        for c in range(DC):
                            mm = pe.matmul(v[:, t * D:(t + 1) * D], xnT[s][:, c * S + t * P:c * S + (t + 1) * P],
                                           wq1T[:, c * D:(c + 1) * D], start=(c == 0), stop=(c == DC - 1))
                    mm.then_inc(fb.filled, 1)
                for s in range(2):
                    pe.wait_ge(cx_ready["l1x"].sem, cx_ready["l1x"].count(2 * i + s))
                    turn_cx(fa, i, s)
                for s in range(2):
                    pe.wait_ge(fa.drained(("cT", s)), fa.read(i, ("cT", s)))
                    pe.wait_ge(fb.drained(("kv", s)), fb.empty(i, ("kv", s)))
                    v = fb.slot(("kv", s))
                    for t in range(T):
                        mm = pe.matmul(v[:, t * BANK:(t + 1) * BANK], ctxT[s][:, t * P:(t + 1) * P], wkv1T,
                                       start=True, stop=True)
                    mm.then_inc(fb.filled, 1)
                attention("l1x", i, turn_columns1, max1, 12, 2 * NH1, sh1, exp1, values1, NH1 // 2, token_blocks1, first_results)
                turn_heads(i, 1)
                project(i, 1)
                next_turned(fa, i)

            banks_free("prep1b")
            f = pl["prep1b"]["A"]
            pe.wait_ge(tern_ready, 1)
            for w in range(2):
                for c in range(DC):
                    turn(f, 0, ("tern", w, c), [(P, o * P, tern[w][:, o * D + c * P:o * D + (c + 1) * P])
                                                for o in range(HC)], identb, BF16)
            for k in range(2):
                turn(f, 0, ("tern", 2, k), [(P, (c % 4) * D + o * P, tern[2][:, o * H_FFN + c * P:o * H_FFN + (c + 1) * P])
                                            for c in range(4 * k, 4 * k + 4) for o in range(T)], identb, BF16)
            f = pl["prep2a"]["A"]
            pe.wait_ge(ld["sw12"], 16 * 2)
            for w in range(2):
                for k in range(4):
                    c, half = k // 2, k % 2
                    turn(f, 0, ("sw", w, k), [(P, j * P, raw_sw[w][:, (4 * half + j) * D + c * P:(4 * half + j) * D + (c + 1) * P])
                                              for j in range(4)], ident)
            pe.wait_ge(ld["sw3"], 16)
            for k in range(4):
                turn(f, 0, ("sw", 2, k), [(P, j * D + o * P, raw_sw[2][:, o * H_FFN + (2 * k + j) * P:o * H_FFN + (2 * k + j + 1) * P])
                                          for j in range(2) for o in range(T)], ident)

            banks_free("l1f")
            fa, fb, fc = (pl["l1f"][g] for g in "ABC")
            with pe.Fori(0, TURNS) as i:
                for s in range(2):
                    pe.wait_ge(xq_ready.sem, xq_ready.count(2 * i + s))
                    turn_x(fa, i, s, ("qT", s), xq[s], identb, BF16)
                for s in range(2):
                    pe.wait_ge(fa.drained(("qT", s)), fa.read(i, ("qT", s)))
                    for t in range(T):
                        for h in range(2):
                            for w, wT in (("g", wgT), ("u", wuT)):
                                pe.wait_ge(fb.drained((w, s, t, h)), fb.empty(i, (w, s, t, h)))
                                v = fb.slot((w, s, t, h))
                                for c in range(DC):
                                    at = c * H_FFN + h * BANK
                                    mm = pe.matmul(v, xqT[s][:, c * S + t * P:c * S + (t + 1) * P], wT[:, at:at + BANK],
                                                   start=(c == 0), stop=(c == DC - 1))
                                mm.then_inc(fb.filled, 1)
                for s in range(2):
                    for t in range(T):
                        for h in range(2):
                            pe.wait_ge(fb.drained(("u", s, t, h)), fb.read(i, ("u", s, t, h)))
                            turn(fc, i, ("hT", s, t, h), [(P, j * P, ha[s][:, t * H_FFN + (4 * h + j) * P:t * H_FFN + (4 * h + j + 1) * P])
                                                          for j in range(4)], ident)
                for s in range(2):
                    for t in range(T):
                        for h in range(2):
                            pe.wait_ge(fc.drained(("hT", s, t, h)), fc.read(i, ("hT", s, t, h)))
                            pe.wait_ge(fc.drained(("had", s, t, h)), fc.empty(i, ("had", s, t, h)))
                            v = fc.slot(("had", s, t, h))
                            for j in range(4):
                                at = t * H_FFN + (4 * h + j) * P
                                mm = pe.matmul(v[:, j * P:(j + 1) * P], hb[s][:, at:at + P], hadamard, start=True, stop=True)
                            mm.then_inc(fc.filled, 1)
                turn_next("l1f", i)
                for s in range(2):
                    for t in range(T):
                        pe.wait_ge(yq_ready.sem, yq_ready.count(2 * i + s, t + 1))
                        turn(fa, i, ("yT", s, t), [(P, c * P, yqb[s][:, t * H_FFN + c * P:t * H_FFN + (c + 1) * P])
                                                   for c in range(HC)], identb, BF16)
                for s in range(2):
                    pe.wait_ge(fa.drained(("dn", s)), fa.empty(i, ("dn", s)))
                    v = fa.slot(("dn", s))
                    for t in range(T):
                        pe.wait_ge(fa.drained(("yT", s, t)), fa.read(i, ("yT", s, t)))
                        for c in range(HC):
                            at = t * H_FFN + c * P
                            mm = pe.matmul(v[:, t * D:(t + 1) * D], yqT[s][:, at:at + P], wdT[:, c * D:(c + 1) * D],
                                           start=(c == 0), stop=(c == HC - 1))
                    mm.then_inc(fa.filled, 1)
                next_turned(fa, i)

            banks_free("prep2b")
            f = pl["prep2b"]["A"]
            pe.wait_ge(ld["w12"], 16)
            for k in range(8):
                c, q = k // 4, k % 4
                turn(f, 0, ("w12", k), [(P, j * P, raw_w12[:, (4 * q + j) * D + c * P:(4 * q + j) * D + (c + 1) * P])
                                        for j in range(4)], ident)
            pe.wait_ge(ld["w3"], 16 * 4)
            for k in range(4):
                turn(f, 0, ("w3", k), [(P, j * P, raw_w3[:, (4 * k + j) * P:(4 * k + j + 1) * P]) for j in range(4)], ident)
            turn(f, 0, ("r",), [(P, c * E, raw_r2[:, c * P:(c + 1) * P]) for c in range(DC)]
                 + [(P, DC * E + c * (E + 1), raw_r3[:, c * P:(c + 1) * P]) for c in range(DC)], ident)

            def logits(f, i, s, wT, n):
                pe.wait_ge(f.drained(("gate", s)), f.empty(i, ("gate", s)))
                v = f.slot(("gate", s))
                for t in range(T):
                    for c in range(DC):
                        mm = pe.matmul(v[:, t * n:(t + 1) * n], xnT[s][:, c * S + t * P:c * S + (t + 1) * P],
                                       wT[:, c * n:(c + 1) * n], start=(c == 0), stop=(c == DC - 1))
                mm.then_inc(f.filled, 1)

            def shared_up(f, i, s, j, rows, gate_at, up_at, w_g, w_u, width):
                pe.wait_ge(f.drained(("sh", s, j)), f.empty(i, ("sh", s, j)))
                v = f.slot(("sh", s, j))
                for half, wT, at in ((0, w_g, gate_at), (1, w_u, up_at)):
                    for c in range(DC):
                        mm = pe.matmul(v[0:rows, half * S:(half + 1) * S], wT[:, c * width + at:c * width + at + rows],
                                       xnT[s][:, c * S:(c + 1) * S], start=(c == 0), stop=(c == DC - 1))
                mm.then_inc(f.filled, 1)

            banks_free("l2f")
            fa, fb = pl["l2f"]["A"], pl["l2f"]["B"]
            with pe.Fori(0, TURNS) as i:
                for s in range(2):
                    logits(fa, i, s, r2T, E)
                def turn_hidden(s):
                    for t in range(T):
                        pe.wait_ge(fb.drained(("ro", s, t, E // 2 - 1)), fb.read(i, ("ro", s, t, E // 2 - 1)))
                        for k in range(2):
                            turn(fa, i, ("hrT", s, t, k), [(P, j * P, hr2[t][:, (4 * k + j) * P:(4 * k + j + 1) * P])
                                                           for j in range(4)], ident)

                for s in range(2):
                    for j in range(HC):
                        shared_up(fb, i, s, j, P, j * P, j * P, sw1T, sw2T, H_FFN)
                    if s == 1:
                        turn_hidden(0)
                    for t in range(T):
                        for k in range(E // 2):
                            pe.wait_ge(fb.drained(("ro", s, t, k)), fb.empty(i, ("ro", s, t, k)))
                            v = fb.slot(("ro", s, t, k))
                            for c in range(DC):
                                at = c * E * 2 * H_R2 + k * BANK
                                mm = pe.matmul(v, xnT[s][:, c * S + t * P:c * S + (t + 1) * P], w12T[:, at:at + BANK],
                                               start=(c == 0), stop=(c == DC - 1))
                            mm.then_inc(fb.filled, 1)
                for s in range(2):
                    if s == 1:
                        turn_hidden(1)
                    pe.wait_ge(fa.drained(("dn", s)), fa.empty(i, ("dn", s)))
                    v = fa.slot(("dn", s))
                    pe.wait_ge(fb.drained(("sh", s, HC - 1)), fb.read(i, ("sh", s, HC - 1)))
                    pe.wait_ge(fa.drained(("hrT", s, 1, 0)), fa.read(i, ("hrT", s, 1, 0)))
                    pe.wait_ge(fa.drained(("hrT", s, 1, 1)), fa.read(i, ("hrT", s, 1, 1)))
                    for t in range(T):
                        o = v[:, t * D:(t + 1) * D]
                        for j in range(HC):
                            pe.matmul(o, hsT2[s][:, j * S + t * P:j * S + (t + 1) * P], sw3T[:, j * D:(j + 1) * D],
                                      start=(j == 0), stop=False)
                        for e in range(E):
                            mm = pe.matmul(o, hrT2[s][:, (t * E + e) * P:(t * E + e + 1) * P], w3T[:, e * D:(e + 1) * D],
                                           start=False, stop=(e == E - 1))
                    mm.then_inc(fa.filled, 1)
                    if s == 0:
                        turn_next("l2f", i)
                next_turned(fa, i)

            banks_free("l3x")
            fa, fb = pl["l3x"]["A"], pl["l3x"]["B"]

            def turn_queries3(i, s, fills):
                pe.wait_ge(qparts_ready["l3x"].sem, qparts_ready["l3x"].count(2 * i + s))
                for k in fills:
                    turn(fa, i, ("qsT", s, k), [(P, j * S + t * P, qs3[s][:, (t * 16 + 4 * k + j) * P:(t * 16 + 4 * k + j + 1) * P])
                                                for j in range(4) for t in range(T)], identb, BF16)

            def turn_keys3(i, s):
                pe.wait_ge(kparts_ready["l3x"].sem, kparts_ready["l3x"].count(2 * i + s))
                for k in range(2):
                    turn(fa, i, ("ksT", s, k), [(P, j * S + t * P, ks3[s][:, (t * KV3 + 4 * k + j) * P:(t * KV3 + 4 * k + j + 1) * P])
                                                for j in range(4) for t in range(T)], identb, BF16)

            def columns_turned3(i, s):
                for k in range(2):
                    pe.wait_ge(fa.drained(("ksT", s, k)), fa.read(i, ("ksT", s, k)))

            def shift3(i, s):
                pe.wait_ge(shift_ready["l3x"].sem, shift_ready["l3x"].count(2 * i + s))
                turn(fa, i, ("shT", s), [(2 * NH3, t * P, sh3[s][:, t * 2 * NH3:(t + 1) * 2 * NH3]) for t in range(T)],
                     identb, BF16)

            def max3(i, s, k):
                pe.wait_ge(fa.drained(("max", s, k)), fa.empty(i, ("max", s, k)))
                v = fa.slot(("max", s, k))
                t, j, r = k // 16, k % 16 // 2, 64 * (k % 2)
                for a in range(2):
                    hh = 2 * j + a
                    mm = pe.matmul(v[:, a * S:(a + 1) * S], qT3[s][r:r + K3, hh * S + t * P:hh * S + (t + 1) * P],
                                   kT3[s][r:r + K3, j * S:(j + 1) * S], start=True, stop=True)
                mm.then_inc(fa.filled, 1)

            def exp3(i, s, m):
                pe.wait_ge(fb.drained(("sc", s, m)), fb.empty(i, ("sc", s, m)))
                v = fb.slot(("sc", s, m))
                j, r = m // 2, 64 * (m % 2)
                for u in range(T):
                    mm = pe.matmul(v[:, u * BANK:(u + 1) * BANK], kT3[s][r:r + K3 + 2, j * S + u * P:j * S + (u + 1) * P],
                                   qT3[s][r:r + K3 + 2, 2 * j * S:(2 * j + 2) * S], start=True, stop=True)
                mm.then_inc(fb.filled, 1)

            def values3(s, m, u):
                pv, p = pl["l3x"]["V"].slot(("pv", s)), pexp3[m % 2]
                j, par = m // 2, m % 2
                return pe.matmul(pv[0:M3, par * BANK:(par + 1) * BANK],
                                 vpad3[s][:, (u * KV3 + j) * M3:(u * KV3 + j + 1) * M3], p[:, u * BANK:(u + 1) * BANK],
                                 start=(j == 0 and u == 0), stop=(j == KV3 - 1 and u == T - 1))

            def tokens3(i, s):
                fv = pl["l3x"]["V"]
                pe.wait_ge(fv.drained(("pv", s)), fv.read(i, ("pv", s)))
                turn(fb, i, ("tok", s), [(P, t * BANK + (2 * a + par) * M3,
                                          oT13[s][0:M3, par * BANK + a * S + t * P:par * BANK + a * S + (t + 1) * P])
                                         for t in range(T) for a in range(2) for par in range(2)], ident)

            def exponentials3(i, s, between):
                fv, n_exp = pl["l3x"]["V"], NH3 // 2
                pe.wait_ge(shift_in["l3x"].sem, shift_in["l3x"].count(2 * i + s))
                for m in range(n_exp + 1):
                    if m < n_exp:
                        exp3(i, s, m)
                    between(m, 0)
                    if m == 0:
                        pe.wait_ge(fv.drained(("pv", s)), fv.empty(i, ("pv", s)))
                        pe.wait_ge(v_ready.sem, v_ready.count(2 * i + s))
                    else:
                        pe.wait_ge(fb.drained(("sc", s, m - 1)), fb.read(i, ("sc", s, m - 1)))
                        values3(s, m - 1, 0)
                        between(m, 1)
                        values3(s, m - 1, 1).then_inc(pv_done["l3x"].sem, 1)
                        between(m, 2)

            def prefix3(i, s, m, at):
                if at == 0:
                    if m == 1 or m == 3:
                        turn_queries3(i, s, range(m - 1, m + 1))
                    elif m == 4:
                        turn_keys3(i, s)
                    elif m == 5:
                        columns_turned3(i, s)
                    elif m == 14:
                        shift3(i, s)
                if 5 <= m < 13:
                    for k in ((0, 1), (2,), (3,))[at]:
                        max3(i, s, 4 * (m - 5) + k)

            def batches3(i, last):
                def second(m, at):
                    prefix3(i, 1, m, at)

                def following(m, at):
                    if m == 1 and at == 0:
                        turn_next("l3x", i, "B")
                    if not last:
                        prefix3(i + 1, 0, m, at)

                exponentials3(i, 0, second)
                tokens3(i, 0)
                exponentials3(i, 1, following)
                tokens3(i, 1)
                next_turned(fb, i)

            pe.wait_ge(pads_ready, 1)
            turn_queries3(0, 0, range(4))
            turn_keys3(0, 0)
            columns_turned3(0, 0)
            for k in range(32):
                max3(0, 0, k)
            shift3(0, 0)
            with pe.Fori(0, TURNS - 1) as i:
                batches3(i, False)
            batches3(TURNS - 1, True)

            banks_free("l3f")
            fa, fb = pl["l3f"]["A"], pl["l3f"]["B"]
            pe.wait_ge(ld["l3"], 16 * 6)
            with pe.Fori(0, TURNS) as i:
                for s in range(2):
                    logits(fa, i, s, r3T, E + 1)
                def turn_hidden(s):
                    for t in range(T):
                        pe.wait_ge(fb.drained(("ro", s, t, E - 1)), fb.read(i, ("ro", s, t, E - 1)))
                        for k in range(3):
                            turn(fa, i, ("hrT", s, t, k), [(P, (j - 4 * k) * P, hr3[t][:, j * P:(j + 1) * P])
                                                           for j in range(4 * k, min(4 * k + 4, RC3))], ident)

                for s in range(2):
                    for j in range(SC3):
                        shared_up(fb, i, s, j, min(P, H_S3 - j * P), j * P, H_S3 + j * P, ws_gu, ws_gu, 2 * H_S3)
                    if s == 1:
                        turn_hidden(0)
                    for t in range(T):
                        for e in range(E):
                            pe.wait_ge(fb.drained(("ro", s, t, e)), fb.empty(i, ("ro", s, t, e)))
                            v = fb.slot(("ro", s, t, e))
                            for c in range(DC):
                                at = (c * E + e) * 2 * H_R3
                                mm = pe.matmul(v[:, 0:2 * H_R3], xnT[s][:, c * S + t * P:c * S + (t + 1) * P],
                                               we_gu[:, at:at + 2 * H_R3], start=(c == 0), stop=(c == DC - 1))
                            mm.then_inc(fb.filled, 1)
                for s in range(2):
                    if s == 1:
                        turn_hidden(1)
                    pe.wait_ge(fa.drained(("dnS", s)), fa.empty(i, ("dnS", s)))
                    v = fa.slot(("dnS", s))
                    pe.wait_ge(fb.drained(("sh", s, SC3 - 1)), fb.read(i, ("sh", s, SC3 - 1)))
                    for t in range(T):
                        for j in range(SC3):
                            r = min(P, H_S3 - j * P)
                            mm = pe.matmul(v[:, t * D:(t + 1) * D], hsT3[s][0:r, j * S + t * P:j * S + (t + 1) * P],
                                           ws_dn[0:r, j * D:(j + 1) * D], start=(j == 0), stop=(j == SC3 - 1))
                    mm.then_inc(fa.filled, 1)
                    pe.wait_ge(fa.drained(("dnR", s)), fa.empty(i, ("dnR", s)))
                    v = fa.slot(("dnR", s))
                    pe.wait_ge(fa.drained(("hrT", s, 1, 1)), fa.read(i, ("hrT", s, 1, 1)))
                    pe.wait_ge(fa.drained(("hrT", s, 1, 2)), fa.read(i, ("hrT", s, 1, 2)))
                    for t in range(T):
                        for j in range(RC3):
                            mm = pe.matmul(v[:, t * D:(t + 1) * D], hrT3[s][:, (t * RC3 + j) * P:(t * RC3 + j + 1) * P],
                                           we_dn[:, j * D:(j + 1) * D], start=(j == 0), stop=(j == RC3 - 1))
                    mm.then_inc(fa.filled, 1)
                    if s == 0:
                        turn_next("l3f", i)
                next_turned(fa, i)

        @block.scalar
        def _(act):
            def move(f, i, key, dst, view, scale=1.0):
                act.wait_ge(f.filled, f.full(i, key))
                v = f.slot(key)
                act.activation(dst, view(v), ACT.Copy, scale=scale).then_inc(f.drained(key), 1)

            def whole(v):
                return v

            act.wait_ge(ld["cols"], 16 * 14)
            act.activation(gt, graw, ACT.Tanh).then_inc(tanh_ready, 1)
            act.activation(gam_s, gam, ACT.Tanh, scale=0.5).then_inc(egam_ready, 1)
            move(pl["prep0"]["A"], 0, ("w64",), wT64, lambda v: v[0:C, 0:3 * C])
            act.wait_ge(const_ready, 1)

            def move_next(f, i):
                for s in range(2):
                    move(f, i, ("xT", s), xnT[s], lambda v: v[:, 0:W])

            move_next(pl["prep0"]["A"], 0)

            f = pl["l0x"]["A"]
            with act.Fori(0, TURNS) as i:
                for s in range(2):
                    move(f, i, ("cT", s), ctxT[s], lambda v: v[0:C, 0:S])
                for s in range(2):
                    move(f, i, ("oT", s), oT0[s], lambda v: v[0:C, 0:S])
                move_next(f, i)
                act.wait_ge(ld["l1f"], 16 * 3)
                for w in range(3):
                    last = act.activation(q3d(tern[w], TURNS, HC * D // TURNS)[:, i], q3d(raw_f1[w], TURNS, HC * D // TURNS)[:, i],
                                          ACT.Abs, accum_out=q3d(wsum, TURNS, 3)[:, i, w:w + 1])
                last.then_inc(wsum_ready, 1)
                for s in range(2):
                    act.wait_ge(l0_z_ready.sem, l0_z_ready.count(2 * i + s))
                    for t in range(T):
                        last = act.activation(e0[s][:, t * S:(t + 1) * S], z0[s][:, t * S:(t + 1) * S], ACT.Exp,
                                              bias=c1[s][:, t:t + 1], accum_out=c2[s][:, t:t + 1])
                    last.then_inc(l0_e_ready.sem, 1)

            fa, fb, fc = (pl["l0f"][g] for g in "ABC")
            with act.Fori(0, TURNS) as i:
                for s in range(2):
                    move(fc, i, ("cT", s), ctxT[s], lambda v: v[0:C, 0:S])
                for s in range(2):
                    move(fc, i, ("qk", s), qkT[s], lambda v: v[0:C, :])
                for s in range(2):
                    act.wait_ge(fc.filled, fc.full(i, ("sim", s)))
                    v = fc.slot(("sim", s))
                    if s == 0:
                        act.activation(sim[s], v, ACT.Copy, scale=1.0 / 16)
                        act.activation(th[s], v, ACT.Tanh, scale=1.0 / 32).then_inc(fc.drained(("sim", s)), 1)
                    else:
                        act.activation(adj[:, 2 * i + 1, :], v, ACT.Copy, scale=1.0 / 16).then_inc(fc.drained(("sim", s)), 1)
                for s in range(2):
                    n = 2 * i + s
                    act.wait_ge(l0_pick_ready.sem, l0_pick_ready.count(n))
                    for t in range(T):
                        act.wait_ge(rexp_free.sem, rexp_free.free(n, t))
                        for k in range(E // 2):
                            act.wait_ge(fb.filled, fb.full(i, ("ex", s, t, k)))
                            v = fb.slot(("ex", s, t, k))
                            for a in range(2):
                                e = 2 * k + a
                                last = act.activation(rexp[t][:, e * D:(e + 1) * D], v[:, a * D:(a + 1) * D], ACT.Relu,
                                                      scale=pick[s][:, t, e:e + 1])
                            last.then_inc(fb.drained(("ex", s, t, k)), 1)
                move_next(fa, i)

            f = pl["prep1"]["A"]
            move(f, 0, ("wq",), wq1T, whole)
            move(f, 0, ("wkv",), wkv1T, lambda v: v[0:C, :])
            move(f, 0, ("wout",), wout1T, whole)

            def first_parts(places, src, hd, at, n):
                step = 1 if n < 3 else 2
                heads = src.rearrange("p (h k) -> p h k", k=hd)
                dst = places[:, :, at * hd:(at + n * step) * hd].rearrange("p h (a k) -> p h a k", a=n)[:, :, :, 0:hd]
                return act.activation(dst, heads.unsqueeze(2).broadcast_to([P, heads.shape[1], n, hd]), ACT.Copy)

            def turned_queries(layer, i, s, rows, qT, fills=range(4)):
                f = pl[layer]["A"]
                for k in fills:
                    move(f, i, ("qsT", s, k), qT[s][0:rows, k * 1024:(k + 1) * 1024], lambda v: v[0:rows, :].bitcast(BF16))

            fa, fb = pl["l1x"]["A"], pl["l1x"]["B"]
            act.drain()
            act.wait_ge(rexp_free.sem, rexp_free.count(B - 1))
            with act.Fori(0, TURNS) as i:
                for s in range(2):
                    qv = qs1[s].rearrange("p (h k) -> p h k", k=K1)
                    act.wait_ge(fb.filled, fb.full(i, ("q", s)))
                    v = fb.slot(("q", s))[:, 0:W]
                    first_parts(qv, v, HD1, 0, 2)
                    first_parts(qv, v, HD1, 5, 1).then_inc(q1_ready["l1x"].sem, 1)
                for s in range(2):
                    move(fa, i, ("cT", s), ctxT[s], lambda v: v[0:C, 0:S])
                for s in range(2):
                    kv = ks1[s].rearrange("p (t h k) -> p t h k", t=T, k=K1 + 2)
                    act.wait_ge(fb.filled, fb.full(i, ("kv", s)))
                    v = fb.slot(("kv", s))
                    for t in range(T):
                        last = first_parts(kv[:, t], v[:, t * BANK:t * BANK + D], HD1, 0, 3)
                    last.then_inc(k1_ready["l1x"].sem, 1)
                for s in range(2):
                    turned_queries("l1x", i, s, K1, qT1)
                act.wait_ge(aa_ready.sem, aa_ready.count(TURNS - 1 + i))
                act.activation(sim1, adj[:, 2 * i + 1, :], ACT.Copy)
                act.activation(th1, adj[:, 2 * i + 1, :], ACT.Tanh, scale=0.5).then_inc(sim1_ready.sem, 1)
                for s in range(2):
                    for m in range(NH1 // 2):
                        if s == 1 and m == 5:
                            move(fa, i, ("oT", 0), xoT1[0], whole)
                        act.wait_ge(fb.filled, fb.full(i, ("sc", s, m)))
                        v = fb.slot(("sc", s, m))
                        act.wait_ge(pv_done["l1x"].sem, pv_done["l1x"].free(2 * i + s, m))
                        act.activation(q3d(pexp1[m % 2], 2, S + P), q3d(v, 2, BANK)[:, :, 0:S + P], ACT.Exp,
                                       scale=HD1 ** -0.5).then_inc(fb.drained(("sc", s, m)), 1)
                move_next(fa, i)
                move(fa, i, ("oT", 1), xoT1[1], whole)

            f = pl["prep1b"]["A"]
            for w, dst in ((0, wgT), (1, wuT), (2, wdT)):
                for k in range(2):
                    move(f, 0, ("tern", w, k), dst[:, k * H_FFN:(k + 1) * H_FFN], lambda v: v.bitcast(BF16))
            f = pl["prep2a"]["A"]
            for w, dst in ((0, sw1T), (1, sw2T), (2, sw3T)):
                for k in range(0, 4, 2):
                    move(f, 0, ("sw", w, k), dst[:, k * BANK:(k + 1) * BANK], whole)

            fa, fb, fc = (pl["l1f"][g] for g in "ABC")
            with act.Fori(0, TURNS) as i:
                for s in range(2):
                    move(fa, i, ("qT", s), xqT[s], lambda v: v.bitcast(BF16)[:, 0:W])
                for s in range(2):
                    for t in range(T):
                        for h in range(2):
                            act.wait_ge(fb.filled, fb.full(i, ("g", s, t, h)))
                            v = fb.slot(("g", s, t, h))
                            act.activation(sg1[2 * t + h], v, ACT.Silu, scale=c3[s][:, t:t + 1])\
                               .then_inc(fb.drained(("g", s, t, h)), 1)
                for s in range(2):
                    for t in range(T):
                        for h in range(2):
                            at = t * H_FFN + h * BANK
                            move(fc, i, ("hT", s, t, h), hb[s][:, at:at + BANK], whole)
                for s in range(2):
                    for t in range(T):
                        move(fc, i, ("had", s, t, 0), ha[s][:, t * H_FFN:t * H_FFN + BANK], whole)
                move_next(fa, i)

            f = pl["prep2b"]["A"]
            for k in range(8):
                move(f, 0, ("w12", k), w12T[:, k * BANK:(k + 1) * BANK], whole)
            for k in range(4):
                move(f, 0, ("w3", k), w3T[:, k * BANK:(k + 1) * BANK], whole)
            move(f, 0, ("r",), rT, lambda v: v[:, 0:DC * (2 * E + 1)])

            fa, fb = pl["l2f"]["A"], pl["l2f"]["B"]
            with act.Fori(0, TURNS) as i:
                for s in range(2):
                    act.wait_ge(fa.filled, fa.full(i, ("gate", s)))
                    v = fa.slot(("gate", s))
                    act.activation(lg[s], q3d(v[:, 0:T * E], T, E), ACT.Exp, scale=-1.0).then_inc(fa.drained(("gate", s)), 1)
                def move_hidden(s):
                    for t in range(T):
                        for k in range(2):
                            at = (t * E + 4 * k) * P
                            move(fa, i, ("hrT", s, t, k), hrT2[s][:, at:at + 4 * P], whole)

                for s in range(2):
                    for j in range(HC):
                        act.wait_ge(fb.filled, fb.full(i, ("sh", s, j)))
                        v = fb.slot(("sh", s, j))
                        act.activation(sg2[fb.index[("sh", s, j)] % 4], v[:, 0:S], ACT.Silu).then_inc(sg2_ready.sem, 1)
                    if s == 1:
                        move_hidden(0)
                    for t in range(T):
                        for k in range(E // 2):
                            act.wait_ge(fb.filled, fb.full(i, ("ro", s, t, k)))
                            v = fb.slot(("ro", s, t, k))
                            act.activation(q3d(sg2[fb.index[("ro", s, t, k)] % 4], 2, H_R2),
                                           q3d(v, 2, 2 * H_R2)[:, :, 0:H_R2], ACT.Silu).then_inc(sg2_ready.sem, 1)
                move_next(fa, i)
                move_hidden(1)

            fa, fb = pl["l3x"]["A"], pl["l3x"]["B"]
            def first_parts3(i, s):
                qv = qs3[s].rearrange("p (h k) -> p h k", k=64)
                kv = ks3[s].rearrange("p (h u k) -> p h u k", u=2, k=64)
                act.wait_ge(xn_ready.sem, xn_ready.count(normed["l3x"] + 2 * i + s))
                first_parts(qv, xn[s], HD3, 0, 2)
                first_parts(qv, xn[s], HD3, 5, 1).then_inc(q1_ready["l3x"].sem, 1)
                act.wait_ge(cx_ready["l3x"].sem, cx_ready["l3x"].count(2 * i + s))
                for u in range(2):
                    last = first_parts(kv[:, :, u], cx[s], HD3, 0, 3)
                last.then_inc(k1_ready["l3x"].sem, 1)

            def batches3(i, last):
                for s in range(2):
                    after = (i + s, 1 - s)
                    if s == 0 or not last:
                        first_parts3(*after)
                    for m in range(NH3 // 2):
                        if s == 1 and m == 2:
                            move_next(fb, i)
                        if (m == 2 or m == 4) and (s == 0 or not last):
                            turned_queries("l3x", *after, P, qT3, range(m - 2, m))
                        act.wait_ge(fb.filled, fb.full(i, ("sc", s, m)))
                        v = fb.slot(("sc", s, m))
                        act.wait_ge(pv_done["l3x"].sem, pv_done["l3x"].free(2 * i + s, m))
                        act.activation(pexp3[m % 2], v, ACT.Exp, scale=HD3 ** -0.5).then_inc(fb.drained(("sc", s, m)), 1)

            first_parts3(0, 0)
            turned_queries("l3x", 0, 0, P, qT3)
            with act.Fori(0, TURNS - 1) as i:
                batches3(i, False)
            batches3(TURNS - 1, True)

            fa, fb = pl["l3f"]["A"], pl["l3f"]["B"]
            with act.Fori(0, TURNS) as i:
                for s in range(2):
                    act.wait_ge(lg3_ready.sem, lg3_ready.count(2 * i + s))
                    for t in range(T):
                        act.activation(cw[s][:, t, :], lg[s][:, t, :], ACT.Exp, bias=c1[s][:, t:t + 1],
                                       accum_out=c2[s][:, t:t + 1])
                    act.activation(c4[s], c3[s], ACT.Exp, scale=-1.0).then_inc(sc3_ready.sem, 1)
                def move_hidden(s):
                    for t in range(T):
                        for k in range(3):
                            n, at = min(4, RC3 - 4 * k) * P, (t * RC3 + 4 * k) * P
                            move(fa, i, ("hrT", s, t, k), hrT3[s][:, at:at + n], lambda v: v[:, 0:n])

                for s in range(2):
                    for j in range(SC3):
                        act.wait_ge(fb.filled, fb.full(i, ("sh", s, j)))
                        v, r = fb.slot(("sh", s, j)), min(P, H_S3 - j * P)
                        act.activation(sg3[fb.index[("sh", s, j)] % 4][0:r, :], v[0:r, 0:S], ACT.Silu)\
                           .then_inc(sg3_ready.sem, 1)
                    if s == 1:
                        move_hidden(0)
                    for t in range(T):
                        for e in range(E):
                            act.wait_ge(fb.filled, fb.full(i, ("ro", s, t, e)))
                            v = fb.slot(("ro", s, t, e))
                            act.activation(sg3[fb.index[("ro", s, t, e)] % 4][:, 0:H_R3], v[:, 0:H_R3], ACT.Silu)\
                               .then_inc(sg3_ready.sem, 1)
                move_next(fa, i)
                move_hidden(1)

        @block.vector
        def _(dve):
            def statistics(rows):
                for k, v in enumerate(rows):
                    dve.bn_stats(st[:, k, :], v)
                dve.drain()
                for k in range(len(rows)):
                    dve.bn_aggr(mv[:, k, :], st[:, k, :])
                dve.drain()

            def one_over_root(eps, var_scale=1.0, times=1.0):
                dve.tensor_scalar(var, mv[:, :, 1], var_scale, eps, ALU.mult, ALU.add)
                dve.drain()
                dve.tensor_scalar(seed.bitcast(U32), var.bitcast(U32), 1, None, ALU.logical_shift_right)
                dve.drain()
                dve.tensor_copy(newton, seed.bitcast(U32))
                dve.drain()
                dve.tensor_scalar(rstd.bitcast(U32), newton, -1.0, RSQRT_BITS, ALU.mult, ALU.add)
                dve.drain()
                for step in range(3):
                    last = times if step == 2 else 1.0
                    dve.tensor_tensor(newton, rstd, rstd, ALU.mult)
                    dve.drain()
                    dve.scalar_tensor_tensor(newton, newton, -0.5 * last, var, ALU.mult, ALU.mult)
                    dve.drain()
                    dve.scalar_tensor_tensor(rstd, newton, 1.5 * last, rstd, ALU.add, ALU.mult)
                    dve.drain()

            def normalised(k, dst, src):
                return dve.tensor_scalar(dst, src, mv[:, k, 0:1], rstd[:, k:k + 1], ALU.subtract, ALU.mult)

            def x_rows(batches):
                return [xs[:, n, t * D:(t + 1) * D] for n in batches for t in range(T)]

            def norm_x(batches):
                rows = x_rows(batches)
                statistics(rows)
                one_over_root(EPS)
                for s in range(2):
                    for t in range(T):
                        last = normalised(s * T + t, xn[s][:, t * D:(t + 1) * D], rows[s * T + t])
                    last.then_inc(xn_ready.sem, 1)

            def norm_next(i):
                norm_x([2 + s - 2 * i for s in range(2)])

            def take_context(layer, n, s):
                dve.tensor_copy(cx[s], ctx_all[:, n, :]).then_inc(cx_ready[layer].sem, 1)

            def two_largest(s, scores):
                for t in range(T):
                    dve.max(m8[s][:, t, :], scores[:, t, :])
                dve.drain()
                for t in range(T):
                    dve.max_index(idx[s][:, t, :], m8[s][:, t, :], scores[:, t, :])
                dve.drain()
                dve.tensor_copy(idf[s], idx[s][:, :, 0:2])
                dve.drain()
                for t in range(T):
                    dve.tensor_scalar(oh[s][:, t, :], iota8, idf[s][:, t, 0:1], None, ALU.is_equal)
                dve.drain()
                for t in range(T):
                    last = dve.scalar_tensor_tensor(pick[s][:, t, :], iota8, idf[s][:, t, 1:2], oh[s][:, t, :],
                                                    ALU.is_equal, ALU.add)
                return last

            dve.wait_ge(ld["x"], 16)
            norm_x(range(2))
            dve.wait_ge(ld["ctx"], 16)
            dve.wait_ge(ld["cols"], 16 * 14)
            dve.wait_ge(ld["con"], 16)
            dve.tensor_copy(bias_p[0], bias_f)
            dve.drain()
            dve.tensor_tensor(bias_r, bias_f, bias_p[0], ALU.subtract)
            dve.drain()
            dve.tensor_copy(bias_p[1], bias_r)
            dve.drain()
            dve.tensor_tensor(bias_r, bias_r, bias_p[1], ALU.subtract)
            dve.drain()
            dve.tensor_copy(bias_p[2], bias_r).then_inc(bias_ready, 1)
            dve.wait_ge(tanh_ready, 1)
            dve.wait_ge(egam_ready, 1)
            dve.tensor_scalar(gt0_half, gt[:, 4:5], 0.5, None, ALU.mult)
            dve.tensor_scalar(gam_s, gam_s, 0.5, 0.5, ALU.mult, ALU.add)
            dve.drain()
            dve.tensor_scalar(keep_a, gam_s, gt[:, 2:3], 0.25, ALU.mult, ALU.mult)
            dve.tensor_scalar(keep_x, gam_s, -1.0, 1.0, ALU.mult, ALU.add)
            dve.drain()
            dve.tensor_scalar(keep_x, keep_x, gt[:, 2:3], None, ALU.mult)

            f = pl["l0x"]["A"]
            with dve.Fori(0, TURNS) as i:
                for s in range(2):
                    take_context("l0x", 2 * i + s, s)
                for s in range(2):
                    dve.wait_ge(f.filled, f.full(i, ("kv", s)))
                    v = f.slot(("kv", s))
                    dve.tensor_tensor(q3d(kv0[s], T, C), q3d(v[:, 0:T * C], T, C),
                                      bk_row.unsqueeze(1).broadcast_to([P, T, C]), ALU.add)
                    dve.tensor_scalar(kvT0[s], v[0:C, S:2 * S], bk_col, None, ALU.add).then_inc(f.drained(("kv", s)), 1)
                norm_next(i)
                for s in range(2):
                    dve.wait_ge(f.filled, f.full(i, ("sim", s)))
                sims = [f.slot(("sim", s))[:, t * S:(t + 1) * S] for s in range(2) for t in range(T)]
                statistics(sims)
                one_over_root(EPS0, 1.0 / S, S ** -0.5)
                for s in range(2):
                    for t in range(T):
                        last = normalised(s * T + t, z0[s][:, t * S:(t + 1) * S], sims[s * T + t])
                    last.then_inc(f.drained(("sim", s)), 1)
                    dve.drain()
                    z = q3d(z0[s], T, S)
                    dve.tensor_tensor(z, z, lng.unsqueeze(1).broadcast_to([P, T, S]), ALU.mult)
                    dve.drain()
                    dve.tensor_tensor(z, z, lnb.unsqueeze(1).broadcast_to([P, T, S]), ALU.add)
                    dve.drain()
                    dve.tensor_reduce(c1[s], z, X, ALU.max, negate=True).then_inc(l0_z_ready.sem, 1)
                for s in range(2):
                    n = 2 * i + s
                    dve.wait_ge(l0_e_ready.sem, l0_e_ready.count(n))
                    dve.reciprocal(c3[s], c2[s])
                    dve.drain()
                    dve.tensor_scalar(c3[s], c3[s], gt[:, 0:1], None, ALU.mult)
                    dve.drain()
                    for t in range(T):
                        xt = xs[:, n, t * D:(t + 1) * D]
                        dve.scalar_tensor_tensor(xt, e0[s][:, t * S:(t + 1) * S], c3[s][:, t:t + 1], xt, ALU.mult, ALU.add)
                dve.drain()

            dve.wait_ge(wsum_ready, TURNS + 1)
            dve.tensor_tensor(wmean, wsums[:, 0:3], wsums[:, 3:6], ALU.add)
            dve.drain()
            dve.tensor_scalar(wmean, wmean, 1.0 / (H_FFN * D), EPS, ALU.mult, ALU.max)
            dve.drain()
            dve.reciprocal(wscale, wmean).then_inc(wsum_ready, 1)

            def take_largest(sim, work, rounds):
                for r in rounds:
                    cur = sim if r == 0 else work
                    for t in range(T):
                        dve.max(m8[0][:, t, :], cur[:, t * S:(t + 1) * S])
                    dve.drain()
                    if r < ROUNDS - 1:
                        for t in range(T):
                            dve.match_replace(work[:, t * S:(t + 1) * S], m8[0][:, t, :], cur[:, t * S:(t + 1) * S], -3.0e38)
                        dve.drain()

            def choose(sim, th, aa):
                dve.tensor_scalar(th, th, 1.0, None, ALU.add)
                dve.drain()
                k = (TOPK_ROW - 1) % 8
                for t in range(T):
                    o = slice(t * S, (t + 1) * S)
                    last = dve.scalar_tensor_tensor(aa[:, o], sim[:, o], m8[0][:, t, k:k + 1], th[:, o], ALU.is_ge, ALU.mult)
                last.then_inc(aa_ready.sem, 1)

            def symmetric(f, i, n, aa):
                for t in range(T):
                    dve.wait_ge(f.filled, f.full(i, ("AT", t)))
                    o = slice(t * S, (t + 1) * S)
                    dve.tensor_tensor(adj[:, n, o], f.slot(("AT", t))[:, 0:S], aa[:, o], ALU.add)\
                       .then_inc(f.drained(("AT", t)), 1)

            fa, fb, fc = (pl["l0f"][g] for g in "ABC")
            with dve.Fori(0, TURNS) as i:
                for s in range(2):
                    take_context("l0f", 2 * i + s, s)
                for s in range(2):
                    dve.wait_ge(fa.filled, fa.full(i, ("gate", s)))
                    v = fa.slot(("gate", s))
                    dve.tensor_tensor(lg[s], q3d(v[:, 0:T * E], T, E), gate0_b.unsqueeze(1).broadcast_to([P, T, E]),
                                      ALU.add).then_inc(fa.drained(("gate", s)), 1)
                    dve.drain()
                    two_largest(s, lg[s]).then_inc(l0_pick_ready.sem, 1)
                for s in range(2):
                    n = 2 * i + s
                    if s == 0:
                        dve.wait_ge(fc.drained(("sim", s)), fc.read(i, ("sim", s)))
                        own_instruction(dve)
                        take_largest(sim[s], work[s], range(ROUNDS))
                        choose(sim[s], th[s], aa[s])
                    for t in range(T):
                        dve.wait_ge(fb.drained(("ex", s, t, E // 2 - 1)), fb.read(i, ("ex", s, t, E // 2 - 1)))
                        dve.tensor_reduce(acc0[s][:, t * D:(t + 1) * D], rexp[t].rearrange("p (e d) -> p d e", e=E), X,
                                          ALU.add).then_inc(rexp_free.sem, 1)
                    dve.drain()
                    dve.scalar_tensor_tensor(xs[:, n, :], acc0[s], gt0_half, xs[:, n, :], ALU.mult, ALU.add)
                    if s == 0:
                        symmetric(fc, i, n, aa[s])
                        norm_next(i)
                dve.drain()

            def rest_of_parts(hd, src, first, second, third, rest, read):
                last = dve.tensor_tensor(rest, src, first, ALU.subtract)
                if read is not None:
                    last.then_inc(read, 1)
                dve.drain()
                for dst in second:
                    dve.tensor_copy(dst, rest)
                dve.drain()
                return dve.tensor_tensor(third, rest, second[0], ALU.subtract)

            def turned_keys(layer, i, s, n, rows, kT):
                f = pl[layer]["A"]
                for k in range(n):
                    dve.wait_ge(f.filled, f.full(i, ("ksT", s, k)))
                    v = f.slot(("ksT", s, k))
                    dve.tensor_copy(kT[s][0:rows, k * 1024:(k + 1) * 1024], v[0:rows, :].bitcast(BF16))\
                       .then_inc(f.drained(("ksT", s, k)), 1)

            def maxima(layer, i, s, n_max, reduce, nmax, hi, lo, shT, between=None):
                f = pl[layer]["A"]
                for k in range(n_max):
                    dst, heads = reduce(k)
                    dve.wait_ge(f.filled, f.full(i, ("max", s, k)))
                    v = f.slot(("max", s, k))
                    dve.tensor_reduce(dst, heads(v), X, ALU.max, negate=True).then_inc(f.drained(("max", s, k)), 1)
                    if between is not None:
                        between(k)
                dve.drain()
                for t in range(T):
                    dve.tensor_copy(hi(t), nmax(t))
                dve.drain()
                for t in range(T):
                    last = dve.tensor_tensor(lo(t), nmax(t), hi(t), ALU.subtract)
                last.then_inc(shift_ready[layer].sem, 1)
                dve.wait_ge(f.filled, f.full(i, ("shT", s)))
                v = f.slot(("shT", s))
                dve.tensor_copy(shT, v[0:shT.shape[0], 0:S // 2].bitcast(BF16)).then_inc(f.drained(("shT", s)), 1)

            def sums_of_values(layer, i, s, rows):
                f = pl[layer]["V"]
                dve.wait_ge(pv_done[layer].sem, pv_done[layer].count(2 * i + s))
                dve.tensor_copy(oT13[s][0:rows, :], f.slot(("pv", s))[0:rows, :]).then_inc(f.drained(("pv", s)), 1)

            def weighted(f, i, s, kv, hd, rec, dst, one_slot):
                g = D // kv // hd
                for t in range(T):
                    key = ("tok", s) if one_slot else ("tok", s, t)
                    dve.wait_ge(f.filled, f.full(i, key))
                    at = t * BANK if one_slot else 0
                    v = f.slot(key)[:, at:at + g * kv * (hd + 1)]
                    r = rec[s][:, t * g * kv:(t + 1) * g * kv]
                    dve.reciprocal(r, v.rearrange("p (h k) -> p h k", k=hd + 1)[:, :, hd])
                    dve.drain()
                    last = dve.tensor_tensor(dst[s][:, t * D:(t + 1) * D].rearrange("p (j g k) -> p g j k", j=kv, g=g),
                                             v.rearrange("p (g j k) -> p g j k", g=g, k=hd + 1)[:, :, :, 0:hd],
                                             q3d(r, g, kv).unsqueeze(3).broadcast_to([P, g, kv, hd]), ALU.mult)
                    if t == T - 1 or not one_slot:
                        last.then_inc(f.drained(key), 1)

            fa, fb = pl["l1x"]["A"], pl["l1x"]["B"]
            dve.wait_ge(vpad_ready, 1)
            FIRST, EARLY = 4, 6
            with dve.Fori(0, TURNS) as i:
                for s in range(2):
                    take_context("l1x", 2 * i + s, s)

                def place(s, stack, pitch, a):
                    return stack[s].rearrange("p (t h k) -> p t h k", t=T, k=pitch)[:, :, :, a * HD1:(a + 1) * HD1]

                def rest(s):
                    return rest1[s].rearrange("p (t h k) -> p t h k", t=T, k=HD1)

                for s in range(2):
                    n = 2 * i + s
                    dve.wait_ge(q1_ready["l1x"].sem, q1_ready["l1x"].count(n))
                    vq = fb.slot(("q", s))[:, 0:W].rearrange("p (t h k) -> p t h k", t=T, k=HD1)
                    rest_of_parts(HD1, vq, place(s, qs1, K1, 0), [place(s, qs1, K1, a) for a in (2, 3)], place(s, qs1, K1, 4),
                                  rest(s), fb.drained(("q", s))).then_inc(qparts_ready["l1x"].sem, 1)
                for s in range(2):
                    n = 2 * i + s
                    dve.wait_ge(k1_ready["l1x"].sem, k1_ready["l1x"].count(n))
                    own_instruction(dve)
                    dve.drain()
                    vkv = q3d(fb.slot(("kv", s)), T, BANK)
                    rest_of_parts(HD1, vkv[:, :, 0:D].rearrange("p t (h k) -> p t h k", k=HD1), place(s, ks1, K1 + 2, 0),
                                  [place(s, ks1, K1 + 2, a) for a in (1, 3)], place(s, ks1, K1 + 2, 5), rest(s), None)\
                        .then_inc(kparts_ready["l1x"].sem, 1)
                    vd = vpad1[s].rearrange("p (t g x) -> p t g x", t=T, x=G1 * M1)
                    vv = vkv[:, :, D:2 * D].rearrange("p t (g l k) -> p t g l k", l=G1, k=HD1)
                    for l in range(G1):
                        at = l * (M1 + HD1 + 1)
                        last = dve.tensor_copy(vd[:, :, :, at:at + HD1], vv[:, :, :, l])
                    last.then_inc(fb.drained(("kv", s)), 1)
                for s in range(2):
                    turned_keys("l1x", i, s, 4, K1 + 2, kT1)

                    def reduce1(k):
                        nm = q3d(nmax1[s], T, NH1)
                        if k < 4:
                            return nm[:, 0, 4 * k:4 * k + 4], lambda v: q3d(v, 4, P)
                        return nm[:, 1, 2 * k - 8:2 * k - 6], lambda v: q3d(v, 2, S)

                    def adjacency(k):
                        if k == FIRST:
                            dve.wait_ge(sim1_ready.sem, sim1_ready.count(i))
                            own_instruction(dve)
                        if FIRST <= k < FIRST + EARLY:
                            take_largest(sim1, work1, range(k - FIRST, k - FIRST + 1))

                    sh = sh1[s].rearrange("p (t r h) -> p t r h", t=T, r=2)
                    maxima("l1x", i, s, 12, reduce1, lambda t: q3d(nmax1[s], T, NH1)[:, t], lambda t: sh[:, t, 0],
                           lambda t: sh[:, t, 1], shT1[s], adjacency if s == 1 else None)

                def add_projected(s):
                    dve.wait_ge(fa.filled, fa.full(i, ("out", s)))
                    n, v = 2 * i + s, fa.slot(("out", s))
                    dve.scalar_tensor_tensor(xs[:, n, :], v, gt[:, 1:2], xs[:, n, :], ALU.mult, ALU.add)\
                       .then_inc(fa.drained(("out", s)), 1)

                sums_of_values("l1x", i, 0, M1)
                norm_next(i)
                weighted(fa, i, 0, NH1, HD1, rec1, rest1, False)
                take_largest(sim1, work1, range(EARLY, ROUNDS))
                choose(sim1, th1, aa1)
                add_projected(0)
                symmetric(fa, i, 2 * i + 1, aa1)
                sums_of_values("l1x", i, 1, M1)
                weighted(fa, i, 1, NH1, HD1, rec1, rest1, False)
                add_projected(1)
                dve.drain()

            def quantise():
                for s in range(2):
                    dve.tensor_reduce(c1[s], q3d(xn[s], T, D), X, ALU.max, apply_absolute_value=True)
                    dve.drain()
                    dve.tensor_scalar(c1[s], c1[s], EPS, None, ALU.max)
                    dve.drain()
                    dve.reciprocal(c2[s], c1[s])
                    dve.tensor_scalar(c3[s], c1[s], wmean[:, 0:1], 1.0 / QB, ALU.mult, ALU.mult)
                    dve.tensor_scalar(c4[s], c1[s], wmean[:, 1:2], 1.0 / QB, ALU.mult, ALU.mult)
                    dve.drain()
                    dve.tensor_scalar(c2[s], c2[s], QB, None, ALU.mult)
                    dve.drain()
                    for t in range(T):
                        o = xn[s][:, t * D:(t + 1) * D]
                        dve.tensor_scalar(o, o, c2[s][:, t:t + 1], ROUND, ALU.mult, ALU.add)
                    dve.drain()
                    dve.tensor_scalar(xq[s], xn[s], ROUND, QB - 1, ALU.subtract, ALU.min).then_inc(xq_ready.sem, 1)
            quantise()

            f = pl["prep2a"]["A"]
            for w, dst in ((0, sw1T), (1, sw2T), (2, sw3T)):
                for k in range(1, 4, 2):
                    dve.wait_ge(f.filled, f.full(0, ("sw", w, k)))
                    v = f.slot(("sw", w, k))
                    dve.tensor_copy(dst[:, k * BANK:(k + 1) * BANK], v).then_inc(f.drained(("sw", w, k)), 1)

            fa, fb, fc = (pl["l1f"][g] for g in "ABC")

            def feed_forward1(i, last):
                for s in range(2):
                    for t in range(T):
                        for h in range(2):
                            dve.wait_ge(fb.filled, fb.full(i, ("u", s, t, h)))
                            at, v = t * H_FFN + h * BANK, fb.slot(("u", s, t, h))
                            dve.wait_ge(fb.drained(("g", s, t, h)), fb.read(i, ("g", s, t, h)))
                            dve.scalar_tensor_tensor(ha[s][:, at:at + BANK], v, c4[s][:, t:t + 1], sg1[2 * t + h],
                                                     ALU.mult, ALU.mult).then_inc(fb.drained(("u", s, t, h)), 1)
                norm_next(i)

                def transform(s, t):
                    dve.wait_ge(fc.drained(("had", s, t, 0)), fc.read(i, ("had", s, t, 0)))
                    dve.wait_ge(fc.filled, fc.full(i, ("had", s, t, 1)))
                    y, z, hi = ha[s][:, t * H_FFN:(t + 1) * H_FFN], bfly, fc.slot(("had", s, t, 1))
                    dve.tensor_tensor(y[:, 4 * P:], y[:, 0:4 * P], hi, ALU.subtract)
                    dve.tensor_tensor(y[:, 0:4 * P], y[:, 0:4 * P], hi, ALU.add)\
                       .then_inc(fc.drained(("had", s, t, 1)), 1)
                    dve.drain()
                    for src, dst, width in ((y, z, 2 * P), (z, y, P)):
                        a = src.rearrange("p (n two w) -> p n two w", two=2, w=width)
                        b = dst.rearrange("p (n two w) -> p n two w", two=2, w=width)
                        dve.tensor_tensor(b[:, :, 0], a[:, :, 0], a[:, :, 1], ALU.add)
                        dve.tensor_tensor(b[:, :, 1], a[:, :, 0], a[:, :, 1], ALU.subtract)
                        dve.drain()
                    k = slice(t, t + 1)
                    dve.tensor_reduce(c1[s][:, k], y, X, ALU.max, apply_absolute_value=True)
                    dve.drain()
                    dve.tensor_scalar(c1[s][:, k], c1[s][:, k], H_FFN ** -0.5, EPS, ALU.mult, ALU.max)
                    dve.drain()
                    dve.reciprocal(c2[s][:, k], c1[s][:, k])
                    dve.tensor_scalar(c3[s][:, k], c1[s][:, k], wmean[:, 2:3], 1.0 / QB, ALU.mult, ALU.mult)
                    dve.drain()
                    dve.tensor_scalar(c2[s][:, k], c2[s][:, k], QB * H_FFN ** -0.5, None, ALU.mult)\
                       .then_inc(y_ready.sem, 1)
                    dve.tensor_scalar(c3[s][:, k], c3[s][:, k], gt[:, 5:6], None, ALU.mult)

                def cut_rows(s, t):
                    dve.wait_ge(fa.filled, fa.full(i, ("yT", s, t)))
                    v = fa.slot(("yT", s, t))
                    dve.tensor_scalar(yqT[s][:, t * H_FFN:(t + 1) * H_FFN], v.bitcast(BF16), QB - 1, None, ALU.min)\
                       .then_inc(fa.drained(("yT", s, t)), 1)

                for n in range(2 * T + 2):
                    if n < 2 * T:
                        transform(n // T, n % T)
                    if n >= 2:
                        cut_rows((n - 2) // T, (n - 2) % T)
                dve.drain()
                for s in range(2):
                    dve.wait_ge(fa.filled, fa.full(i, ("dn", s)))
                    n, v = 2 * i + s, fa.slot(("dn", s))
                    for t in range(T):
                        xt = xs[:, n, t * D:(t + 1) * D]
                        added = dve.scalar_tensor_tensor(xt, v[:, t * D:(t + 1) * D], c3[s][:, t:t + 1], xt, ALU.mult, ALU.add)
                    added.then_inc(fa.drained(("dn", s)), 1)
                dve.drain()
                if not last:
                    quantise()
                rows = x_rows([2 * i + s for s in range(2)])
                statistics(rows)
                one_over_root(EPS)
                for k, row in enumerate(rows):
                    normalised(k, bfly[:, k * D:(k + 1) * D], row)
                dve.drain()
                for s in range(2):
                    n = 2 * i + s
                    dve.scalar_tensor_tensor(xs[:, n, :], bfly[:, s * W:(s + 1) * W], keep_x, xs[:, n, :], ALU.mult, ALU.add)
                dve.drain()
                for s in range(2):
                    n = 2 * i + s
                    dve.scalar_tensor_tensor(xs[:, n, :], adj[:, n, :], keep_a, xs[:, n, :], ALU.mult, ALU.add)
                dve.drain()

            with dve.Fori(0, TURNS - 1) as i:
                feed_forward1(i, False)
            feed_forward1(TURNS - 1, True)

            fa, fb = pl["l2f"]["A"], pl["l2f"]["B"]
            with dve.Fori(0, TURNS) as i:
                for s in range(2):
                    dve.wait_ge(fa.drained(("gate", s)), fa.read(i, ("gate", s)))
                    dve.tensor_scalar(cw[s], lg[s], 1.0, None, ALU.add)
                    dve.drain()
                    dve.reciprocal(cw[s], cw[s])
                    dve.drain()
                    dve.tensor_tensor(lg[s], cw[s], ebias.unsqueeze(1).broadcast_to([P, T, E]), ALU.add)
                    dve.drain()
                    two_largest(s, lg[s])
                    dve.drain()
                    dve.tensor_tensor(cw[s], cw[s], pick[s], ALU.mult)
                    dve.drain()
                    dve.tensor_reduce(c1[s], cw[s], X, ALU.add)
                    dve.drain()
                    dve.tensor_scalar(c1[s], c1[s], 1e-9, None, ALU.add)
                    dve.drain()
                    dve.reciprocal(c2[s], c1[s])
                    dve.drain()
                    for t in range(T):
                        dve.tensor_scalar(cw[s][:, t, :], cw[s][:, t, :], c2[s][:, t:t + 1], None, ALU.mult)
                    dve.drain()
                for s in range(2):
                    n = 2 * i + s
                    for j in range(HC):
                        dve.wait_ge(fb.filled, fb.full(i, ("sh", s, j)))
                        v = fb.slot(("sh", s, j))
                        dve.wait_ge(sg2_ready.sem, sg2_ready.count(n, j + 1))
                        dve.tensor_tensor(hsT2[s][:, j * S:(j + 1) * S], v[:, S:2 * S], sg2[fb.index[("sh", s, j)] % 4],
                                          ALU.mult).then_inc(fb.drained(("sh", s, j)), 1)
                    for t in range(T):
                        if s == 1:
                            dve.wait_ge(fa.filled, fa.full(i, ("hrT", 0, t, 1)))
                        for k in range(E // 2):
                            dve.wait_ge(fb.filled, fb.full(i, ("ro", s, t, k)))
                            v, sg = fb.slot(("ro", s, t, k)), sg2[fb.index[("ro", s, t, k)] % 4]
                            dve.wait_ge(sg2_ready.sem, sg2_ready.count(n, HC + t * E // 2 + k + 1))
                            for a in range(2):
                                e = 2 * k + a
                                last = dve.scalar_tensor_tensor(hr2[t][:, e * H_R2:(e + 1) * H_R2],
                                                                v[:, (2 * a + 1) * H_R2:(2 * a + 2) * H_R2], cw[s][:, t, e:e + 1],
                                                                sg[:, a * H_R2:(a + 1) * H_R2], ALU.mult, ALU.mult)
                            last.then_inc(fb.drained(("ro", s, t, k)), 1)
                norm_next(i)
                for s in range(2):
                    dve.wait_ge(fa.filled, fa.full(i, ("dn", s)))
                    n, v = 2 * i + s, fa.slot(("dn", s))
                    dve.scalar_tensor_tensor(xs[:, n, :], v, gt[:, 6:7], xs[:, n, :], ALU.mult, ALU.add)\
                       .then_inc(fa.drained(("dn", s)), 1)
                dve.drain()

            fb = pl["l3x"]["B"]

            def split3(i, s):
                n = 2 * i + s
                qv = qs3[s].rearrange("p (h k) -> p h k", k=64)
                kv = ks3[s].rearrange("p (h u k) -> p h u k", u=2, k=64)

                def place(v, a):
                    return v[:, :, a * HD3:(a + 1) * HD3]

                dve.wait_ge(q1_ready["l3x"].sem, q1_ready["l3x"].count(n))
                rest_of_parts(HD3, xn[s].rearrange("p (h k) -> p h k", k=HD3), place(qv, 0),
                              [place(qv, a) for a in (2, 3)], place(qv, 4), rest3[s].rearrange("p (h k) -> p h k", k=HD3),
                              None).then_inc(qparts_ready["l3x"].sem, 1)
                dve.wait_ge(k1_ready["l3x"].sem, k1_ready["l3x"].count(n))
                own_instruction(dve)
                dve.drain()
                rest = rest3[s][:, 0:T * C].rearrange("p (h k) -> p h k", k=HD3)
                rest_of_parts(HD3, cx[s].rearrange("p (h k) -> p h k", k=HD3), place(kv[:, :, 0], 0),
                              [place(kv[:, :, u], a) for u in range(2) for a in (1, 3)], place(kv[:, :, 0], 5), rest, None)
                dve.tensor_tensor(place(kv[:, :, 1], 5), rest, place(kv[:, :, 0], 1), ALU.subtract)\
                   .then_inc(kparts_ready["l3x"].sem, 1)

            def maxima3(i, s):
                turned_keys("l3x", i, s, 2, P, kT3)
                nm = q3d(nmax3[s], T, NH3)
                sh = sh3[s].rearrange("p (t r u h) -> p t r u h", t=T, r=2, u=2)

                def reduce3(k):
                    j, par = k % 16 // 2, k % 2
                    return nm[:, k // 16].rearrange("p (j a u) -> p j a u", a=2, u=2)[:, j, :, par], lambda v: q3d(v, 2, S)

                maxima("l3x", i, s, 32, reduce3, lambda t: nm[:, t].rearrange("p (h u) -> p u h", u=2), lambda t: sh[:, t, 0],
                       lambda t: sh[:, t, 1], shT3[s])

            def results3(i, s):
                n = 2 * i + s
                weighted(fb, i, s, KV3, HD3, rec3, rest3, True)
                dve.drain()
                dve.scalar_tensor_tensor(xs[:, n, :], rest3[s], gt[:, 3:4], xs[:, n, :], ALU.mult, ALU.add)
                dve.drain()

            def batches3(i, last):
                split3(i, 1)
                norm_next(i)
                maxima3(i, 1)
                sums_of_values("l3x", i, 0, M3)
                if not last:
                    take_context("l3x", 2 * i + 2, 0)
                results3(i, 0)
                if not last:
                    split3(i + 1, 0)
                    maxima3(i + 1, 0)
                sums_of_values("l3x", i, 1, M3)
                if not last:
                    take_context("l3x", 2 * i + 3, 1)
                results3(i, 1)

            for s in range(2):
                take_context("l3x", s, s)
            split3(0, 0)
            maxima3(0, 0)
            with dve.Fori(0, TURNS - 1) as i:
                batches3(i, False)
            batches3(TURNS - 1, True)

            fa, fb = pl["l3f"]["A"], pl["l3f"]["B"]
            with dve.Fori(0, TURNS) as i:
                for s in range(2):
                    dve.wait_ge(fa.filled, fa.full(i, ("gate", s)))
                    v = fa.slot(("gate", s))
                    v = q3d(v[:, 0:T * (E + 1)], T, E + 1)
                    dve.tensor_copy(c3[s], v[:, :, E])
                    dve.tensor_copy(lg[s], v[:, :, 0:E]).then_inc(fa.drained(("gate", s)), 1)
                    dve.drain()
                    dve.tensor_reduce(c1[s], lg[s], X, ALU.max, negate=True).then_inc(lg3_ready.sem, 1)
                for s in range(2):
                    dve.wait_ge(sc3_ready.sem, sc3_ready.count(2 * i + s))
                    dve.reciprocal(c1[s], c2[s])
                    dve.tensor_scalar(c4[s], c4[s], 1.0, None, ALU.add)
                    dve.drain()
                    dve.reciprocal(c3[s], c4[s])
                    for t in range(T):
                        dve.tensor_scalar(lg[s][:, t, :], cw[s][:, t, :], c1[s][:, t:t + 1], None, ALU.mult)
                    dve.drain()
                    dve.tensor_scalar(c3[s], c3[s], gt[:, 7:8], None, ALU.mult)
                    two_largest(s, lg[s])
                    dve.drain()
                    dve.tensor_tensor(cw[s], lg[s], pick[s], ALU.mult)
                    dve.drain()
                for s in range(2):
                    n = 2 * i + s
                    for j in range(SC3):
                        dve.wait_ge(fb.filled, fb.full(i, ("sh", s, j)))
                        r, v = min(P, H_S3 - j * P), fb.slot(("sh", s, j))
                        dve.wait_ge(sg3_ready.sem, sg3_ready.count(n, j + 1))
                        dve.tensor_tensor(hsT3[s][0:r, j * S:(j + 1) * S], v[0:r, S:2 * S],
                                          sg3[fb.index[("sh", s, j)] % 4][0:r, :], ALU.mult).then_inc(fb.drained(("sh", s, j)), 1)
                    for t in range(T):
                        if s == 1:
                            dve.wait_ge(fa.filled, fa.full(i, ("hrT", 0, t, 2)))
                        for e in range(E):
                            dve.wait_ge(fb.filled, fb.full(i, ("ro", s, t, e)))
                            v, sg = fb.slot(("ro", s, t, e)), sg3[fb.index[("ro", s, t, e)] % 4]
                            dve.wait_ge(sg3_ready.sem, sg3_ready.count(n, SC3 + t * E + e + 1))
                            dve.scalar_tensor_tensor(hr3[t][:, e * H_R3:(e + 1) * H_R3], v[:, H_R3:2 * H_R3],
                                                     cw[s][:, t, e:e + 1], sg[:, 0:H_R3], ALU.mult, ALU.mult)\
                               .then_inc(fb.drained(("ro", s, t, e)), 1)
                norm_next(i)
                for s in range(2):
                    dve.wait_ge(fa.filled, fa.full(i, ("dnS", s)))
                    n, v = 2 * i + s, fa.slot(("dnS", s))
                    for t in range(T):
                        xt = xs[:, n, t * D:(t + 1) * D]
                        last = dve.scalar_tensor_tensor(xt, v[:, t * D:(t + 1) * D], c3[s][:, t:t + 1], xt, ALU.mult, ALU.add)
                    last.then_inc(fa.drained(("dnS", s)), 1)
                    dve.drain()
                    dve.wait_ge(fa.filled, fa.full(i, ("dnR", s)))
                    v = fa.slot(("dnR", s))
                    dve.scalar_tensor_tensor(xs[:, n, :], v, gt[:, 7:8], xs[:, n, :], ALU.mult, ALU.add)\
                       .then_inc(fa.drained(("dnR", s)), 1)
                    dve.drain().then_inc(x_done.sem, 1)


_INS = ['x', 'ctx_512', 'g_xattn', 'g_ffn', 'L0_xattn_W_k', 'L0_xattn_b_k', 'L0_xattn_ln_gamma', 'L0_xattn_ln_beta',
        'L0_ffn_gate_w', 'L0_ffn_gate_b', 'L0_ffn_expert_w', 'L0_ffn_expert_b', 'L1_xattn_Wq', 'L1_xattn_Wkv_expand',
        'L1_xattn_Wout', 'L1_ffn_w_gate', 'L1_ffn_w_up', 'L1_ffn_w_down', 'L2_xattn_Wq', 'L2_xattn_Wk',
        'L2_xattn_gamma_raw', 'L2_ffn_w12', 'L2_ffn_w3', 'L2_ffn_router_w', 'L2_ffn_expert_bias', 'L2_ffn_sw1',
        'L2_ffn_sw2', 'L2_ffn_sw3', 'L3_ffn_W_router', 'L3_ffn_W_sgate', 'L3_ffn_Ws_gate_up', 'L3_ffn_Ws_down',
        'L3_ffn_We_gate_up', 'L3_ffn_We_down']


def kernel(**inputs):
    import numpy as _np
    import concourse.bacc as _bacc
    from concourse import mybir as _mybir
    from concourse.bass_utils import run_bass_kernel_spmd as _run

    nc = _bacc.Bacc("TRN2", target_bir_lowering=False, num_devices=1)
    arrays, args = {}, []

    def give(name, a):
        arrays[name] = a
        args.append(nc.dram_tensor(name, a.shape, _mybir.dt.from_np(a.dtype), kind="ExternalInput").ap())

    for name in _INS:
        a = _np.ascontiguousarray(inputs[name])
        give(f"in_{name}", a.reshape(1) if a.ndim == 0 else a)
    had = _np.ones((1, 1), _np.float32)
    while had.shape[0] < P:
        had = _np.block([[had, had], [had, -had]])
    row = _np.arange(P)
    later = _np.where(row[None, :] > row[:, None], NEG, 0.0)
    give("consts", _np.concatenate([_np.eye(P), had, later, later.T, _np.tile(_np.arange(E), (P, 1))], 1)
         .astype(_np.float32))
    args.append(nc.dram_tensor("out_0", (B, S, D), _mybir.dt.float32, kind="ExternalOutput").ap())
    flamingo_gated(nc, *args)
    r = _run(nc, [arrays], core_ids=[0])
    return r.results[0]["out_0"]
```
